# Optimizing a Trainium2 kernel written in Bass

```python
import numpy as np
import jax
import jax.numpy as jnp

def _softmax(x, axis=-1):
    return jax.nn.softmax(x, axis=axis)
def _gelu(x):
    return jax.nn.gelu(x, approximate=True)
def _silu(x):
    return jax.nn.silu(x)
def _sigmoid(x):
    return jax.nn.sigmoid(x)
def _layernorm(x, axis=-1, eps=1e-5):
    m = jnp.mean(x, axis=axis, keepdims=True)
    v = jnp.var(x, axis=axis, keepdims=True)
    return (x - m) / jnp.sqrt(v + eps)
def _scatter_add(tgt, idx, src, axis=0):
    return tgt.at[idx].add(src)
def _segment_sum(src, seg, n):
    return jax.ops.segment_sum(src, seg, n)

kernel_name = 'mk_conv_attn_hybrid_d2_conv_nhwc128_a3e8ec'

def setup_inputs(seed: int = 0):
    np.random.seed(seed)
    _w = jnp.asarray
    def _rec_inputs():
        import jax
        import jax.numpy as jnp
        _gk = jax.random.key(seed)
        x = -0.0005153 + 1.001 * jax.random.normal(jax.random.fold_in(_gk, 1), (8, 56, 56, 128), jnp.float32)
        return x
    x = _rec_inputs()
    def _L0_conv_setup():
        import jax, jax.numpy as jnp
        import numpy as np
        KH = KW = 3
        PAD = 1
        DIL = 1
        GROUP = 4
        OFFSET_SCALE = 1.0
        P = KH * KW

        def bilinear_sample(img, iy, ix, H, W):
            x0 = jnp.floor(ix)
            y0 = jnp.floor(iy)
            wx1 = ix - x0
            wy1 = iy - y0

            def corner(yf, xf, wgt):
                valid = (yf >= 0) & (yf < H) & (xf >= 0) & (xf < W)
                idx = jnp.clip(yf, 0, H - 1).astype(jnp.int32) * W + jnp.clip(xf, 0, W - 1).astype(jnp.int32)
                v = jax.vmap(lambda im, i: im[i])(img, idx)
                return v * (wgt * valid)[..., None]
            return corner(y0, x0, (1 - wy1) * (1 - wx1)) + corner(y0, x0 + 1, (1 - wy1) * wx1) + corner(y0 + 1, x0, wy1 * (1 - wx1)) + corner(y0 + 1, x0 + 1, wy1 * wx1)

        def dcn_core(x_proj, offset, mask_sm):
            N, H, W, C = x_proj.shape
            Hin, Win = (H + 2 * PAD, W + 2 * PAD)
            Cg = C // GROUP
            pad = jnp.pad(x_proj, ((0, 0), (PAD, PAD), (PAD, PAD), (0, 0)))
            img = pad.reshape(N, Hin, Win, GROUP, Cg).transpose(0, 3, 1, 2, 4).reshape(N * GROUP, Hin * Win, Cg)
            ref_x = (jnp.arange(W, dtype=jnp.float32) + DIL * (KW - 1) // 2 + 0.5) / Win
            ref_y = (jnp.arange(H, dtype=jnp.float32) + DIL * (KH - 1) // 2 + 0.5) / Hin
            gx = jnp.arange(KW, dtype=jnp.float32) * DIL - DIL * (KW - 1) // 2
            gy = jnp.arange(KH, dtype=jnp.float32) * DIL - DIL * (KH - 1) // 2
            gxx, gyy = jnp.meshgrid(gx, gy, indexing='ij')
            gpx = (gxx / Win).reshape(P)
            gpy = (gyy / Hin).reshape(P)
            loc_x = ref_x[None, None, :, None, None] + gpx[None, None, None, None, :] * OFFSET_SCALE + offset[..., 0] * (OFFSET_SCALE / Win)
            loc_y = ref_y[None, :, None, None, None] + gpy[None, None, None, None, :] * OFFSET_SCALE + offset[..., 1] * (OFFSET_SCALE / Hin)
            ix = (loc_x * Win - 0.5).transpose(0, 3, 1, 2, 4).reshape(N * GROUP, H * W * P)
            iy = (loc_y * Hin - 0.5).transpose(0, 3, 1, 2, 4).reshape(N * GROUP, H * W * P)
            samp = bilinear_sample(img, iy, ix, Hin, Win)
            samp = samp.reshape(N, GROUP, H, W, P, Cg)
            return jnp.einsum('nghwpc,nhwgp->nhwgc', samp, mask_sm).reshape(N, H, W, C)

        def layer_norm(z, g, b, eps=1e-05):
            m = z.mean(-1, keepdims=True)
            v = ((z - m) ** 2).mean(-1, keepdims=True)
            return (z - m) / jnp.sqrt(v + eps) * g + b
        key = jax.random.key(seed)
        ks = jax.random.split(key, 12)
        N, H, W, C, G, R = (8, 56, 56, 128, GROUP, 4)

        def w(k, shp, s=0.02):
            return jax.random.normal(k, shp, jnp.float32) * s
        return dict(x=jax.random.normal(ks[0], (N, H, W, C), jnp.float32), w_in=w(ks[1], (C, C)), b_in=jnp.zeros((C,), jnp.float32), dw_w=w(ks[2], (C, 1, KH, KW)), dw_b=jnp.zeros((C,), jnp.float32), bn_g=jnp.ones((C,), jnp.float32), bn_b=jnp.zeros((C,), jnp.float32), bn_m=w(ks[3], (C,), 0.1), bn_v=jax.random.uniform(ks[4], (C,), jnp.float32, 0.5, 1.5), w_off=w(ks[5], (C, G * P * 2)), b_off=jnp.zeros((G * P * 2,), jnp.float32), w_msk=w(ks[6], (C, G * P)), b_msk=jnp.zeros((G * P,), jnp.float32), w_out=w(ks[7], (C, C)), b_out=jnp.zeros((C,), jnp.float32), ln1_g=jnp.ones((C,), jnp.float32), ln1_b=jnp.zeros((C,), jnp.float32), w_fc1=w(ks[8], (C, R * C)), b_fc1=jnp.zeros((R * C,), jnp.float32), w_fc2=w(ks[9], (R * C, C)), b_fc2=jnp.zeros((C,), jnp.float32), ln2_g=jnp.ones((C,), jnp.float32), ln2_b=jnp.zeros((C,), jnp.float32), gamma1=jnp.ones((C,), jnp.float32), gamma2=jnp.ones((C,), jnp.float32))
    _L0_conv_all = _L0_conv_setup()
    _L0_conv_in = {k: v for k, v in _L0_conv_all.items() if k in ('w_in', 'b_in', 'dw_w', 'dw_b', 'bn_g', 'bn_b', 'bn_m', 'bn_v', 'w_off', 'b_off', 'w_msk', 'b_msk', 'w_out', 'b_out', 'ln1_g', 'ln1_b', 'w_fc1', 'b_fc1', 'w_fc2', 'b_fc2', 'ln2_g', 'ln2_b', 'gamma1', 'gamma2', )}
    del _L0_conv_all

    def _L1_attn_setup():
        import jax, jax.numpy as jnp
        import numpy as np
        B, T, C = (4, 4096, 128)
        key = jax.random.key(seed)
        k1, k2, k3, k4 = jax.random.split(key, 4)
        x = jax.random.normal(k1, (B, T, C), dtype=jnp.float32)
        Wq = jax.random.normal(k2, (C, C), dtype=jnp.float32) * C ** (-0.5)
        Wk = jax.random.normal(k3, (C, C), dtype=jnp.float32) * C ** (-0.5)
        Wv = jax.random.normal(k4, (C, C), dtype=jnp.float32) * C ** (-0.5)
        return {'x': x, 'Wq': Wq, 'Wk': Wk, 'Wv': Wv}
    _L1_attn_all = _L1_attn_setup()
    _L1_attn_in = {k: v for k, v in _L1_attn_all.items() if k in ('Wq', 'Wk', 'Wv', )}
    del _L1_attn_all

    def _L1_ffn_setup():
        import jax, jax.numpy as jnp
        import numpy as np
        B, N, D, C, E, K = (8, 8192, 128, 128, 8, 2)
        key = jax.random.key(seed)
        k0, k1, k2 = jax.random.split(key, 3)
        x = jax.random.normal(k0, (B, N, D), dtype=jnp.float32)
        router_w = jax.random.normal(k1, (D, E), dtype=jnp.float32) * 0.05
        router_b = jnp.zeros((E,), dtype=jnp.float32)
        expert_w = jax.random.normal(k2, (E, D, C), dtype=jnp.float32) * (1.0 / np.sqrt(D))
        expert_b = jnp.zeros((E, C), dtype=jnp.float32)
        return {'x': x, 'router_w': router_w, 'router_b': router_b, 'expert_w': expert_w, 'expert_b': expert_b}
    _L1_ffn_all = _L1_ffn_setup()
    _L1_ffn_in = {k: v for k, v in _L1_ffn_all.items() if k in ('router_w', 'router_b', 'expert_w', 'expert_b', )}
    del _L1_ffn_all

    return {
        "x": x,
        "L0_conv_w_in": _L0_conv_in["w_in"],
        "L0_conv_b_in": _L0_conv_in["b_in"],
        "L0_conv_dw_w": _L0_conv_in["dw_w"],
        "L0_conv_dw_b": _L0_conv_in["dw_b"],
        "L0_conv_bn_g": _L0_conv_in["bn_g"],
        "L0_conv_bn_b": _L0_conv_in["bn_b"],
        "L0_conv_bn_m": _L0_conv_in["bn_m"],
        "L0_conv_bn_v": _L0_conv_in["bn_v"],
        "L0_conv_w_off": _L0_conv_in["w_off"],
        "L0_conv_b_off": _L0_conv_in["b_off"],
        "L0_conv_w_msk": _L0_conv_in["w_msk"],
        "L0_conv_b_msk": _L0_conv_in["b_msk"],
        "L0_conv_w_out": _L0_conv_in["w_out"],
        "L0_conv_b_out": _L0_conv_in["b_out"],
        "L0_conv_ln1_g": _L0_conv_in["ln1_g"],
        "L0_conv_ln1_b": _L0_conv_in["ln1_b"],
        "L0_conv_w_fc1": _L0_conv_in["w_fc1"],
        "L0_conv_b_fc1": _L0_conv_in["b_fc1"],
        "L0_conv_w_fc2": _L0_conv_in["w_fc2"],
        "L0_conv_b_fc2": _L0_conv_in["b_fc2"],
        "L0_conv_ln2_g": _L0_conv_in["ln2_g"],
        "L0_conv_ln2_b": _L0_conv_in["ln2_b"],
        "L0_conv_gamma1": _L0_conv_in["gamma1"],
        "L0_conv_gamma2": _L0_conv_in["gamma2"],
        "L1_attn_Wq": _L1_attn_in["Wq"],
        "L1_attn_Wk": _L1_attn_in["Wk"],
        "L1_attn_Wv": _L1_attn_in["Wv"],
        "L1_ffn_router_w": _L1_ffn_in["router_w"],
        "L1_ffn_router_b": _L1_ffn_in["router_b"],
        "L1_ffn_expert_w": _L1_ffn_in["expert_w"],
        "L1_ffn_expert_b": _L1_ffn_in["expert_b"],
    }

def reference(x, L0_conv_w_in, L0_conv_b_in, L0_conv_dw_w, L0_conv_dw_b, L0_conv_bn_g, L0_conv_bn_b, L0_conv_bn_m, L0_conv_bn_v, L0_conv_w_off, L0_conv_b_off, L0_conv_w_msk, L0_conv_b_msk, L0_conv_w_out, L0_conv_b_out, L0_conv_ln1_g, L0_conv_ln1_b, L0_conv_w_fc1, L0_conv_b_fc1, L0_conv_w_fc2, L0_conv_b_fc2, L0_conv_ln2_g, L0_conv_ln2_b, L0_conv_gamma1, L0_conv_gamma2, L1_attn_Wq, L1_attn_Wk, L1_attn_Wv, L1_ffn_router_w, L1_ffn_router_b, L1_ffn_expert_w, L1_ffn_expert_b):
    import jax
    import jax.numpy as jnp
    def _L0_conv_ref(x, w_in, b_in, dw_w, dw_b, bn_g, bn_b, bn_m, bn_v, w_off, b_off, w_msk, b_msk, w_out, b_out, ln1_g, ln1_b, w_fc1, b_fc1, w_fc2, b_fc2, ln2_g, ln2_b, gamma1, gamma2):
        import jax, jax.numpy as jnp
        import numpy as np
        KH = KW = 3
        PAD = 1
        DIL = 1
        GROUP = 4
        OFFSET_SCALE = 1.0
        P = KH * KW

        def bilinear_sample(img, iy, ix, H, W):
            x0 = jnp.floor(ix)
            y0 = jnp.floor(iy)
            wx1 = ix - x0
            wy1 = iy - y0

            def corner(yf, xf, wgt):
                valid = (yf >= 0) & (yf < H) & (xf >= 0) & (xf < W)
                idx = jnp.clip(yf, 0, H - 1).astype(jnp.int32) * W + jnp.clip(xf, 0, W - 1).astype(jnp.int32)
                v = jax.vmap(lambda im, i: im[i])(img, idx)
                return v * (wgt * valid)[..., None]
            return corner(y0, x0, (1 - wy1) * (1 - wx1)) + corner(y0, x0 + 1, (1 - wy1) * wx1) + corner(y0 + 1, x0, wy1 * (1 - wx1)) + corner(y0 + 1, x0 + 1, wy1 * wx1)

        def dcn_core(x_proj, offset, mask_sm):
            N, H, W, C = x_proj.shape
            Hin, Win = (H + 2 * PAD, W + 2 * PAD)
            Cg = C // GROUP
            pad = jnp.pad(x_proj, ((0, 0), (PAD, PAD), (PAD, PAD), (0, 0)))
            img = pad.reshape(N, Hin, Win, GROUP, Cg).transpose(0, 3, 1, 2, 4).reshape(N * GROUP, Hin * Win, Cg)
            ref_x = (jnp.arange(W, dtype=jnp.float32) + DIL * (KW - 1) // 2 + 0.5) / Win
            ref_y = (jnp.arange(H, dtype=jnp.float32) + DIL * (KH - 1) // 2 + 0.5) / Hin
            gx = jnp.arange(KW, dtype=jnp.float32) * DIL - DIL * (KW - 1) // 2
            gy = jnp.arange(KH, dtype=jnp.float32) * DIL - DIL * (KH - 1) // 2
            gxx, gyy = jnp.meshgrid(gx, gy, indexing='ij')
            gpx = (gxx / Win).reshape(P)
            gpy = (gyy / Hin).reshape(P)
            loc_x = ref_x[None, None, :, None, None] + gpx[None, None, None, None, :] * OFFSET_SCALE + offset[..., 0] * (OFFSET_SCALE / Win)
            loc_y = ref_y[None, :, None, None, None] + gpy[None, None, None, None, :] * OFFSET_SCALE + offset[..., 1] * (OFFSET_SCALE / Hin)
            ix = (loc_x * Win - 0.5).transpose(0, 3, 1, 2, 4).reshape(N * GROUP, H * W * P)
            iy = (loc_y * Hin - 0.5).transpose(0, 3, 1, 2, 4).reshape(N * GROUP, H * W * P)
            samp = bilinear_sample(img, iy, ix, Hin, Win)
            samp = samp.reshape(N, GROUP, H, W, P, Cg)
            return jnp.einsum('nghwpc,nhwgp->nhwgc', samp, mask_sm).reshape(N, H, W, C)

        def layer_norm(z, g, b, eps=1e-05):
            m = z.mean(-1, keepdims=True)
            v = ((z - m) ** 2).mean(-1, keepdims=True)
            return (z - m) / jnp.sqrt(v + eps) * g + b
        N, H, W, C = x.shape
        xp = x @ w_in + b_in
        h = x.transpose(0, 3, 1, 2)
        h = jax.lax.conv_general_dilated(h, dw_w, (1, 1), ((PAD, PAD), (PAD, PAD)), feature_group_count=C, dimension_numbers=('NCHW', 'OIHW', 'NCHW')) + dw_b[None, :, None, None]
        h = (h - bn_m[None, :, None, None]) * (bn_g / jnp.sqrt(bn_v + 1e-05))[None, :, None, None] + bn_b[None, :, None, None]
        h = jax.nn.gelu(h.transpose(0, 2, 3, 1), approximate=False)
        offset = (h @ w_off + b_off).reshape(N, H, W, GROUP, P, 2)
        mask = jax.nn.softmax((h @ w_msk + b_msk).reshape(N, H, W, GROUP, P), axis=-1)
        y = dcn_core(xp, offset, mask) @ w_out + b_out
        x = x + gamma1 * layer_norm(y, ln1_g, ln1_b)
        m = jax.nn.gelu(x @ w_fc1 + b_fc1, approximate=False) @ w_fc2 + b_fc2
        x = x + gamma2 * layer_norm(m, ln2_g, ln2_b)
        return x

    def _L1_attn_ref(x, Wq, Wk, Wv):
        import jax, jax.numpy as jnp
        import numpy as np
        B, T, C = (4, 4096, 128)
        Bsz, Tlen, Ch = x.shape
        q = jnp.einsum('btc,cd->btd', x, Wq)
        k = jnp.einsum('btc,cd->btd', x, Wk)
        v = jnp.einsum('btc,cd->btd', x, Wv)
        scale = Ch ** (-0.5)
        scores = jnp.einsum('btd,bsd->bts', q, k) * scale
        causal = jnp.tril(jnp.ones((Tlen, Tlen), dtype=bool))
        scores = jnp.where(causal, scores, -jnp.inf)
        attn = jax.nn.softmax(scores, axis=-1)
        out = jnp.einsum('bts,bsd->btd', attn, v)
        return out

    def _L1_ffn_ref(x, router_w, router_b, expert_w, expert_b):
        import jax, jax.numpy as jnp
        import numpy as np
        B, N, D, C, E, K = (8, 8192, 128, 128, 8, 2)
        router_probs = jax.nn.softmax(x @ router_w + router_b, axis=-1)
        top_p, top_i = jax.lax.top_k(router_probs, K)
        top_p = top_p / jnp.sum(top_p, axis=-1, keepdims=True)
        expert_out = jnp.einsum('bnd,edc->bnec', x, expert_w) + expert_b
        gathered = jnp.take_along_axis(expert_out, top_i[..., None], axis=2)
        return jnp.einsum('bnk,bnkc->bnc', top_p, gathered)

    def _gn(v, G=32, eps=1e-5):
        B_, H_, W_, C_ = v.shape
        g = v.reshape(B_, H_, W_, G, C_ // G)
        m = jnp.mean(g, axis=(1, 2, 4), keepdims=True)
        s = jnp.var(g, axis=(1, 2, 4), keepdims=True)
        return ((g - m) / jnp.sqrt(s + eps)).reshape(v.shape)

    def _ln_c(v, eps=1e-6):
        m = jnp.mean(v, axis=-1, keepdims=True)
        s = jnp.var(v, axis=-1, keepdims=True)
        return (v - m) / jnp.sqrt(s + eps)

    def _ln_t(v, eps=1e-5):
        m = jnp.mean(v, axis=-1, keepdims=True)
        s = jnp.var(v, axis=-1, keepdims=True)
        return (v - m) / jnp.sqrt(s + eps)

    def _to_tokens(v):
        B_, H_, W_, C_ = v.shape
        return v.reshape(B_, H_ * W_, C_)
    def _from_tokens(t, like):
        return t.reshape(like.shape)

    x = _L0_conv_ref(x, L0_conv_w_in, L0_conv_b_in, L0_conv_dw_w, L0_conv_dw_b, L0_conv_bn_g, L0_conv_bn_b, L0_conv_bn_m, L0_conv_bn_v, L0_conv_w_off, L0_conv_b_off, L0_conv_w_msk, L0_conv_b_msk, L0_conv_w_out, L0_conv_b_out, L0_conv_ln1_g, L0_conv_ln1_b, L0_conv_w_fc1, L0_conv_b_fc1, L0_conv_w_fc2, L0_conv_b_fc2, L0_conv_ln2_g, L0_conv_ln2_b, L0_conv_gamma1, L0_conv_gamma2)
    t = _to_tokens(x)
    t = t + _L1_attn_ref(_ln_t(t), L1_attn_Wq, L1_attn_Wk, L1_attn_Wv)
    t = t + _L1_ffn_ref(_ln_t(t), L1_ffn_router_w, L1_ffn_router_b, L1_ffn_expert_w, L1_ffn_expert_b)
    x = _from_tokens(t, x)
    return x


_drawn_inputs = setup_inputs


def setup_inputs(seed=0):
    import zlib

    import numpy as np

    out = dict(_drawn_inputs(seed))
    spreads = {'L0_conv_b_in': (0.0, 0.1),
     'L0_conv_dw_b': (0.0, 0.526),
     'L0_conv_bn_g': (1.0, 0.6),
     'L0_conv_bn_b': (0.0, 0.739),
     'L0_conv_b_off': (0.0, 0.1),
     'L0_conv_b_msk': (0.0, 0.312),
     'L0_conv_b_out': (0.0, 0.1),
     'L0_conv_ln1_g': (1.0, 0.2),
     'L0_conv_ln1_b': (0.0, 0.1),
     'L0_conv_b_fc1': (0.0, 0.1),
     'L0_conv_b_fc2': (0.0, 0.1),
     'L0_conv_ln2_g': (1.0, 0.2),
     'L0_conv_ln2_b': (0.0, 0.1),
     'L0_conv_gamma1': (1.0, 0.2),
     'L0_conv_gamma2': (1.0, 0.2),
     'L1_ffn_router_b': (0.0, 0.1),
     'L1_ffn_expert_b': (0.0, 0.1)}
    factors = {'L0_conv_dw_w': 5.424,
     'L0_conv_bn_m': 4.448,
     'L0_conv_bn_v': 8.0,
     'L0_conv_w_off': 3.58,
     'L0_conv_w_msk': 4.664}
    for name, (base, spread) in spreads.items():
        noise = np.random.default_rng([zlib.crc32(name.encode()), seed]).standard_normal(out[name].shape)
        drawn = base * np.exp(spread * noise) if base else spread * noise
        out[name] = jnp.asarray(drawn.astype(out[name].dtype))
    for name, factor in factors.items():
        out[name] = (out[name] * factor).astype(out[name].dtype)
    return out
```

```python
from contextlib import ExitStack

import concourse.bass as bass
from concourse import mybir

F32 = mybir.dt.float32
I32 = mybir.dt.int32
U32 = mybir.dt.uint32
ALU = mybir.AluOpType
ACT = mybir.ActivationFunctionType
AX = mybir.AxisListType

C = 128
IMG = 56
PAD = IMG + 2
TOK = IMG * IMG
ROWS = 8
CH = ROWS * IMG
NJ = IMG // ROWS
TT = 112
NT = CH // TT
G = 4
CG = C // G
P9 = 9
GP = G * P9
CORNERS = 4
POS = IMG + 1
BLK = 7
RING = 2
HID = 4 * C
NH = HID // C
NE = 8
NEG = -1.0e30
MAGIC = 1597463007.0


class Steps:

    def __init__(self, eng, sem):
        self.eng, self.sem, self.n = eng, sem, 0

    def did(self, ins):
        ins.then_inc(self.sem, 1)
        self.n += 1
        return ins

    def wait(self):
        self.eng.wait_ge(self.sem, self.n)

    def restart(self):
        self.wait()
        self.eng.sem_clear(self.sem)
        self.n = 0


def per_parity(j):
    return (NJ + 1) // 2 if j % 2 == 0 else NJ // 2


def build(nc, x, w, consts, out):
    N = x.shape[0]
    NTOK = N * TOK
    TILES = NTOK // 128
    SLOTS = TILES // BLK
    assert TILES % RING == 0 and TILES % BLK == 0

    table = nc.dram_tensor("corner_table", (N * POS * POS * G, CORNERS * CG), F32).ap()
    idx_d = nc.dram_tensor("corner_index", (NTOK, GP), U32).ap()
    wts_d = nc.dram_tensor("corner_weight", (NTOK, GP * CORNERS), F32).ap()
    tok_d = nc.dram_tensor("tokens", (NTOK, C), F32).ap()

    ctx = ExitStack()

    def sb(name, shape, dt=F32):
        return ctx.enter_context(nc.sbuf_tensor(name, shape, dt))

    def sem(name):
        return ctx.enter_context(nc.semaphore(name))

    with ctx:
        bank = [ctx.enter_context(nc.psum_tensor(f"bank{i}", [128, 512], F32)) for i in range(8)]

        ident = sb("ident", [128, 128])
        diag = sb("diag", [C, P9, C])
        w_in = sb("w_in", [C, C])
        w_om = sb("w_om", [C, 3 * GP])
        w_out = sb("w_out", [C, C])
        w_fc1 = sb("w_fc1", [C, HID])
        w_fc2 = sb("w_fc2", [C, NH, C])
        b_fc1 = sb("b_fc1", [C, NH])
        wq = sb("wq", [C, C])
        wk = sb("wk", [C, C])
        wv = sb("wv", [C, C])
        w_rt = sb("w_rt", [C, NE])
        w_ex = sb("w_ex", [C, NE, C])
        b_ex = sb("b_ex", [NE, C])
        cols = sb("cols", [C, 16])
        dw = sb("dw", [C, P9])
        b_in = sb("b_in", [TT, C])
        b_out = sb("b_out", [128, C])
        b_fc2 = sb("b_fc2", [128, C])
        ln_a = sb("ln_a", [128, 2, C])
        ln_c = sb("ln_c", [128, 2, C])
        gamma = sb("gamma", [128, 2, C])
        b_rt = sb("b_rt", [TT, NE])
        b_om = sb("b_om", [TT, 3 * GP])
        grid = sb("grid", [TT, 2, NT, GP])
        gidx = sb("gidx", [TT, NT * GP])
        ioff = sb("ioff", [TT, N])
        causal = sb("causal", [TT, 3 * TT + CH])
        lower = sb("lower", [TT, NE * NE])
        zeros = sb("zeros", [POS, G * CORNERS * CG])

        xin = sb("xin", [TT, 2, NT, C])
        xpad = sb("xpad", [C, PAD, PAD])
        xflat = sb("xflat", [C, 2, CH])
        proj = sb("proj", [TT, 2, NT, C])
        hT = sb("hT", [C, 2, CH])
        pos = sb("pos", [TT, 2, NT * GP])
        rnd = sb("rnd", [TT, 2, NT * GP], I32)
        above = sb("above", [TT, 2, NT * GP])
        low = sb("low", [TT, 2, NT * GP])
        frac = sb("frac", [TT, 2, NT * GP])
        spot = sb("spot", [TT, NT * GP])
        msk = sb("msk", [TT, NT * GP])
        mred = sb("mred", [TT, 3, NT * G])
        my = sb("my", [TT, 2, NT * GP])
        idx_s = sb("idx_s", [TT, 2, NT * GP], U32)
        wts_s = sb("wts_s", [TT, 2, NT * GP * CORNERS])

        ring = sb("ring", [128, RING, GP * CORNERS, CG])
        idx_r = sb("idx_r", [128, RING, GP], U32)
        wts_r = sb("wts_r", [128, RING, GP * CORNERS])
        y = sb("y", [128, 2, C])
        yT = sb("yT", [128, 2, 128])
        z = sb("z", [128, BLK, C])
        xb = sb("xb", [128, BLK, C])
        x1 = sb("x1", [128, BLK, C])
        x1T = sb("x1T", [C, BLK * 128])
        hid = sb("hid", [C, NH, 512])
        m = sb("m", [128, BLK, C])

        st = sb("st", [128, BLK, 6])
        mv = sb("mv", [128, BLK, 2])
        nwt = sb("nwt", [128, 6, BLK])
        seed = sb("seed", [128, BLK], I32)

        tin = sb("tin", [TT, 2, NT, C])
        xn = sb("xn", [TT, NT, C])
        xnT = sb("xnT", [C, CH])
        qT = sb("qT", [C, CH])
        q_t = sb("q_t", [C, TT])
        kT = sb("kT", [C, NJ, CH])
        v = sb("v", [TT, NJ * NT, C])
        S = sb("S", [TT, NJ, CH])
        cmax = sb("cmax", [TT, NJ])
        nmax = sb("nmax", [TT, 1])
        rsum = sb("rsum", [TT, 1])
        rinv = sb("rinv", [TT, 1])
        pT = sb("pT", [TT, 2, NT, TT])
        t1 = sb("t1", [TT, NT, C])
        lg = sb("lg", [TT, NT, NE])
        cmp1 = sb("cmp1", [TT, NT, NE, NE])
        cmp2 = sb("cmp2", [TT, NT, NE, NE])
        rank = sb("rank", [TT, NT * NE])
        gate = sb("gate", [TT, NT, NE])
        sred = sb("sred", [TT, 3, NT])
        gT = sb("gT", [NE, CH])
        o = sb("o", [TT, 2, NT, C])

        cst_in = sem("cst_in")
        border_out = sem("border_out")
        x_in = [sem(f"x_in{i}") for i in range(2)]
        table_out = [sem(f"table_out{i}") for i in range(2)]
        iw_out = [sem(f"iw_out{i}") for i in range(2)]
        iw_in = [sem(f"iw_in{i}") for i in range(RING)]
        gathered = [sem(f"gathered{i}") for i in range(RING)]
        xb_in = sem("xb_in")
        tok_out = sem("tok_out")
        tok_in = [sem(f"tok_in{i}") for i in range(2)]
        o_out = [sem(f"o_out{i}") for i in range(2)]
        zeroed = sem("zeroed")
        pad_zeroed = sem("pad_zeroed")
        consts_made = sem("consts_made")
        f_turned = sem("f_turned")
        f_padded = sem("f_padded")
        f_flat = sem("f_flat")
        f_projected = sem("f_projected")
        f_proj_kept = sem("f_proj_kept")
        f_convolved = sem("f_convolved")
        f_hidden = sem("f_hidden")
        f_logits = sem("f_logits")
        f_logits_read = sem("f_logits_read")
        f_mask_shifted = sem("f_mask_shifted")
        f_mask_exp = sem("f_mask_exp")
        f_iw_made = sem("f_iw_made")
        ring_free = sem("ring_free")
        tile_ready = sem("tile_ready")
        tile_begun = sem("tile_begun")
        y_made = sem("y_made")
        y_turned = sem("y_turned")
        yT_kept = sem("yT_kept")
        z_made = sem("z_made")
        z_kept = sem("z_kept")
        x1_made = sem("x1_made")
        x1_turned = sem("x1_turned")
        x1T_kept = sem("x1T_kept")
        fc1_made = sem("fc1_made")
        hid_kept = sem("hid_kept")
        fc2_made = sem("fc2_made")
        m_kept = sem("m_kept")
        x2_made = sem("x2_made")
        xn_made = sem("xn_made")
        xn_turned = sem("xn_turned")
        xnT_kept = sem("xnT_kept")
        qkv_made = sem("qkv_made")
        qkv_kept = sem("qkv_kept")
        q_staged = sem("q_staged")
        s_made = sem("s_made")
        s_copied = sem("s_copied")
        s_masked = sem("s_masked")
        max_made = sem("max_made")
        p_made = sem("p_made")
        p_turned = sem("p_turned")
        pT_kept = sem("pT_kept")
        pv_made = sem("pv_made")
        t1_made = sem("t1_made")
        xm_made = sem("xm_made")
        xm_turned = sem("xm_turned")
        xmT_kept = sem("xmT_kept")
        route_made = sem("route_made")
        route_shifted = sem("route_shifted")
        route_exp = sem("route_exp")
        gate_made = sem("gate_made")
        gate_turned = sem("gate_turned")
        gT_kept = sem("gT_kept")
        experts_made = sem("experts_made")
        experts_read = sem("experts_read")
        o_made = sem("o_made")
        dve_steps = sem("dve_steps")

        SC, SH, TMP = 0, 1, 2
        BG, BB, BM, BV, DB = 4, 5, 6, 7, 8

        table_v = table.rearrange("(n y x g) d -> n y x g d", n=N, y=POS, x=POS, g=G)
        x_ch = x.rearrange("n (j t r) w c -> n j (r w) t c", j=NJ, t=NT, r=2)
        x_tok = x.rearrange("n h w c -> (n h w) c")
        idx_ch = idx_d.rearrange("(n j t p) e -> n j p t e", n=N, j=NJ, t=NT)
        wts_ch = wts_d.rearrange("(n j t p) e -> n j p t e", n=N, j=NJ, t=NT)
        idx_t = idx_d.rearrange("(q r p) e -> q r p e", r=RING, p=128)
        wts_t = wts_d.rearrange("(q r p) e -> q r p e", r=RING, p=128)
        x_slot = x_tok.rearrange("(s k p) c -> s p k c", k=BLK, p=128)
        tok_slot = tok_d.rearrange("(s k p) c -> s p k c", k=BLK, p=128)
        tok_ch = tok_d.rearrange("(n j t p) c -> n j p t c", n=N, j=NJ, t=NT)
        out_ch = out.rearrange("n h w c -> (n h w) c").rearrange("(n j t p) c -> n j p t c", n=N, j=NJ, t=NT)

        def column(v_):
            return v_.rearrange("(p a) -> p a", a=1)

        NCONST = [0]

        def units(i, j, q):
            return i * (2 * NJ * (NJ + 1)) + 2 * j * (j + 1) + q * (j + 1)

        def units_below(i, j, q):
            return i * (2 * NJ * (NJ - 1)) + 2 * j * (j - 1) + q * j

        block = ctx.enter_context(nc.Block())

        @block.sync
        def _(sp):
            def const(dst, src):
                sp.dma_start(dst, src).then_inc(cst_in, 16)
                NCONST[0] += 1

            with nc.allow_non_contiguous_dma("constants"):
                const(ident[:, :], consts["ident"])
                const(dw[:, :], w["dw_w"].rearrange("c a h w -> c (a h w)"))
                for col, name in ((BG, "bn_g"), (BB, "bn_b"), (BM, "bn_m"), (BV, "bn_v"), (DB, "dw_b")):
                    const(cols[:, col:col + 1], column(w[name]))
                const(w_in[:, :], w["w_in"])
                off_v = w["w_off"].rearrange("c (e a) -> c a e", a=2)
                boff_v = w["b_off"].partition_broadcast(TT).rearrange("p (e a) -> p a e", a=2)
                for a in range(2):
                    const(w_om[:, a * GP:(a + 1) * GP], off_v[:, a, :])
                    const(b_om[:, a * GP:(a + 1) * GP], boff_v[:, a, :])
                const(w_om[:, 2 * GP:], w["w_msk"])
                const(b_om[:, 2 * GP:], w["b_msk"].partition_broadcast(TT))
                const(w_out[:, :], w["w_out"])
                const(w_fc1[:, :], w["w_fc1"])
                const(w_fc2[:, :, :], w["w_fc2"].rearrange("(m p) c -> p m c", p=C))
                const(b_fc1[:, :], w["b_fc1"].rearrange("(m p) -> p m", p=C))
                const(wq[:, :], w["Wq"])
                const(wk[:, :], w["Wk"])
                const(wv[:, :], w["Wv"])
                const(w_rt[:, :], w["router_w"])
                const(w_ex[:, :, :], w["expert_w"].rearrange("e d c -> d e c"))
                const(b_ex[:, :], w["expert_b"])
                const(b_rt[:, :], w["router_b"].partition_broadcast(TT))
                const(b_in[:, :], w["b_in"].partition_broadcast(TT))
                const(b_out[:, :], w["b_out"].partition_broadcast(128))
                const(b_fc2[:, :], w["b_fc2"].partition_broadcast(128))
                for k, (g_, a_, c_) in enumerate((("gamma1", "ln1_g", "ln1_b"), ("gamma2", "ln2_g", "ln2_b"))):
                    const(gamma[:, k, :], w[g_].partition_broadcast(128))
                    const(ln_a[:, k, :], w[a_].partition_broadcast(128))
                    const(ln_c[:, k, :], w[c_].partition_broadcast(128))
                const(grid[:, :, :, :], consts["grid"].rearrange("p (a t e) -> p a t e", a=2, t=NT))
                const(gidx[:, :], consts["gidx"])
                const(ioff[:, :], consts["ioff"])
                const(causal[:, :], consts["causal"])
                const(lower[:, :], consts["lower"])

            sp.wait_ge(zeroed, 1)
            for n in range(N):
                for y0 in (0, POS - 1):
                    sp.dma_start(table_v[n, y0].rearrange("x g d -> x (g d)"), zeros[:, :]).then_inc(border_out, 16)
                for x0 in (0, POS - 1):
                    sp.dma_start(table_v[n, 1:POS - 1, x0].rearrange("y g d -> y (g d)"), zeros[0:POS - 2, :])\
                        .then_inc(border_out, 16)
            sp.wait_ge(border_out, 16 * 4 * N)

            with sp.Fori(0, N) as i:
                def load(j):
                    sp.wait_ge(f_turned, i * NJ + max(j - 1, 0))
                    sp.dma_start(xin[0:IMG, j % 2], x_ch[i, j, 0:IMG]).then_inc(x_in[j % 2], 16)
                    sp.dma_start(xin[IMG:TT, j % 2], x_ch[i, j, IMG:TT]).then_inc(x_in[j % 2], 16)

                load(0)
                load(1)
                for j in range(NJ):
                    sp.wait_ge(f_proj_kept, i * NJ + j + 1)
                    for r in range(2):
                        for slot in range(CORNERS):
                            dy, dx = slot // 2, slot % 2
                            for t in range(NT):
                                y0 = ROWS * j + 2 * t + r + 1 - dy
                                dst = table_v[i, y0, 1 - dx:1 - dx + IMG, :, slot * CG:(slot + 1) * CG]
                                src = proj[IMG * r:IMG * (r + 1), j % 2, t].rearrange("p (g c) -> p g c", g=G)
                                sp.dma_start(dst, src).then_inc(table_out[j % 2], 16)
                    if j + 2 < NJ:
                        load(j + 2)
                for j in range(NJ):
                    sp.wait_ge(f_iw_made, i * NJ + j + 1)
                    sp.dma_start(idx_ch[i, j], idx_s[:, j % 2].rearrange("p (t e) -> p t e", t=NT))\
                        .then_inc(iw_out[j % 2], 16)
                    sp.dma_start(wts_ch[i, j], wts_s[:, j % 2].rearrange("p (t e) -> p t e", t=NT))\
                        .then_inc(iw_out[j % 2], 16)

            for par in range(2):
                sp.wait_ge(table_out[par], 16 * 2 * CORNERS * NT * N * per_parity(par))
                sp.wait_ge(iw_out[par], 32 * N * per_parity(par))
            with sp.Fori(0, TILES // RING) as q:
                for r in range(RING):
                    sp.wait_ge(ring_free, q * RING + r + 1)
                    sp.dma_start(idx_r[:, r], idx_t[q, r]).then_inc(iw_in[r], 16)
                    sp.dma_start(wts_r[:, r], wts_t[q, r]).then_inc(iw_in[r], 16)

            sp.wait_ge(tok_out, 16 * SLOTS)
            with sp.Fori(0, N) as i:
                def load_tokens(j):
                    sp.wait_ge(t1_made, (i * NJ + max(j - 1, 0)) * NT)
                    sp.dma_start(tin[:, j % 2], tok_ch[i, j]).then_inc(tok_in[j % 2], 16)

                load_tokens(0)
                load_tokens(1)
                for j in range(NJ):
                    sp.wait_ge(o_made, i * NJ + j + 1)
                    sp.dma_start(out_ch[i, j], o[:, j % 2]).then_inc(o_out[j % 2], 16)
                    if j + 2 < NJ:
                        load_tokens(j + 2)
            for par in range(2):
                sp.wait_ge(o_out[par], 16 * N * per_parity(par))

        @block.gpsimd
        def _(pool):
            pool.memset(zeros[:, :], 0.0).then_inc(zeroed, 1)
            with pool.Fori(0, TILES // RING) as q:
                for r in range(RING):
                    pool.wait_ge(iw_in[r], q * 32 + 32)
                    pool.wait_ge(ring_free, q * RING + r + 1)
                    pool.sem_inc(tile_begun, 1)
                    for e in range(GP):
                        pool.indirect_dma_start(
                            ring[:, r, e * CORNERS:(e + 1) * CORNERS, :].rearrange("p s c -> p (s c)"), None,
                            table, bass.IndirectOffsetOnAxis(ap=idx_r[:, r, e:e + 1], axis=0),
                        ).then_inc(gathered[r], 16)
                        if e == 5:
                            before = (r - 1) % RING
                            pool.wait_ge(gathered[before], q * (16 * GP) + (16 * GP if r else 0))
                            pool.sem_inc(tile_ready, 1)
            pool.wait_ge(gathered[RING - 1], 16 * GP * (TILES // RING))
            pool.sem_inc(tile_ready, 1)

        @block.scalar
        def _(act):
            act.wait_ge(consts_made, 1)
            act.wait_ge(pad_zeroed, 1)
            with act.Fori(0, N) as i:
                for j in range(NJ):
                    act.wait_ge(f_turned, i * NJ + j + 1)
                    if j == 0:
                        act.wait_ge(f_convolved, i * NJ)
                        act.wait_ge(f_flat, i * NJ)
                    act.activation(xpad[:, 1 + ROWS * j:1 + ROWS * (j + 1), 1:1 + IMG],
                                   bank[0][:, 0:CH].rearrange("c (h w) -> c h w", w=IMG), ACT.Copy)\
                        .then_inc(f_padded, 1)

                def gelu(j):
                    act.wait_ge(f_convolved, i * NJ + j + 1)
                    act.wait_ge(f_logits, i * NJ + max(j - 1, 0))
                    act.activation(hT[:, j % 2], bank[2 + j % 2][:, 0:CH], ACT.Gelu,
                                   bias=cols[:, SH:SH + 1], scale=cols[:, SC:SC + 1]).then_inc(f_hidden, 1)

                gelu(0)
                for j in range(NJ):
                    if j + 1 < NJ:
                        gelu(j + 1)
                    act.wait_ge(f_mask_shifted, i * NJ + j + 1)
                    act.activation(msk[:, :], msk[:, :], ACT.Exp).then_inc(f_mask_exp, 1)

            with act.Fori(0, SLOTS) as s:
                act.wait_ge(x1_made, s)
                act.dma_start(xb[:, :, :], x_slot[s]).then_inc(xb_in, 16)
                for k in range(BLK):
                    act.wait_ge(y_turned, s * BLK + k + 1)
                    act.wait_ge(z_made, s * BLK + max(k - 1, 0))
                    act.activation(yT[:, k % 2], bank[7][:, 0:128], ACT.Copy).then_inc(yT_kept, 1)
                for half, (k0, k1) in enumerate(((0, 4), (4, BLK))):
                    n = (k1 - k0) * 128
                    act.wait_ge(x1_turned, s * 2 + half + 1)
                    act.wait_ge(fc1_made, s * 2 * NH)
                    act.activation(x1T[:, k0 * 128:k1 * 128], bank[half][:, 0:n], ACT.Copy).then_inc(x1T_kept, 1)
                for half, (k0, k1) in enumerate(((0, 4), (4, BLK))):
                    n = (k1 - k0) * 128
                    act.wait_ge(fc2_made, s * 2 + half)
                    for c in range(NH):
                        act.wait_ge(fc1_made, s * 2 * NH + half * NH + c + 1)
                        act.activation(hid[:, c, 0:n], bank[3 + c % 2][:, 0:n], ACT.Gelu,
                                       bias=b_fc1[:, c:c + 1]).then_inc(hid_kept, 1)
                act.wait_ge(x2_made, s + 1)
                act.dma_start(tok_slot[s], m[:, :, :]).then_inc(tok_out, 16)

            with act.Fori(0, N) as i:
                for j in range(NJ):
                    g = i * NJ + j
                    act.wait_ge(xn_turned, g + 1)
                    act.activation(xnT[:, :], bank[0][:, 0:CH], ACT.Copy).then_inc(xnT_kept, 1)
                    act.wait_ge(qkv_made, g * 3 + 1)
                    act.activation(qT[:, :], bank[1][:, 0:CH], ACT.Copy, scale=float(C) ** -0.5).then_inc(qkv_kept, 1)
                    act.wait_ge(qkv_made, g * 3 + 2)
                    if j == 0:
                        act.wait_ge(pv_made, units(i, 0, 0))
                    act.activation(kT[:, j], bank[2][:, 0:CH], ACT.Copy).then_inc(qkv_kept, 1)
                    act.wait_ge(qkv_made, g * 3 + 3)
                    act.activation(v[:, NT * j:NT * (j + 1), :],
                                   bank[3][0:TT, :].rearrange("p (t c) -> p t c", t=NT), ACT.Copy)\
                        .then_inc(qkv_kept, 1)
                    act.wait_ge(qkv_kept, g * 3 + 3)
                    with act.Fori(0, NT) as q:
                        u0, a0, qg = units(i, j, q), units_below(i, j, q), g * NT + q
                        act.wait_ge(s_made, u0)
                        act.activation(q_t[:, :], qT[:, bass.ds(q * TT, TT)], ACT.Copy).then_inc(q_staged, 1)
                        act.wait_ge(p_turned, u0)
                        for c in range(j):
                            act.wait_ge(s_made, u0 + c + 1)
                            act.activation(S[:, c], bank[4 + c % 2][0:TT, 0:CH], ACT.Copy).then_inc(s_copied, 1)
                        act.wait_ge(max_made, qg + 1)
                        act.wait_ge(s_copied, a0 + j)
                        act.activation(S[:, 0:j + 1], S[:, 0:j + 1], ACT.Exp, bias=nmax[:, 0:1],
                                       accum_out=rsum[:, 0:1]).then_inc(p_made, 1)
                    act.wait_ge(xm_turned, g + 1)
                    act.activation(xnT[:, :], bank[0][:, 0:CH], ACT.Copy).then_inc(xmT_kept, 1)
                    act.wait_ge(route_shifted, g + 1)
                    act.activation(lg[:, :, :], lg[:, :, :], ACT.Exp).then_inc(route_exp, 1)
                    act.wait_ge(gate_turned, g + 1)
                    act.activation(gT[:, :], bank[0][0:NE, 0:CH], ACT.Copy).then_inc(gT_kept, 1)

        @block.vector
        def _(dve):
            step = Steps(dve, dve_steps)

            def rsqrt(val, n, p, eps, scratch):
                ve, half, y_, a_, b_ = (scratch[0:p, k, 0:n] for k in range(5))
                step.did(dve.tensor_scalar(ve, val, eps, None, ALU.add))
                step.wait()
                step.did(dve.tensor_scalar(half, ve, -0.5, None, ALU.mult))
                step.did(dve.tensor_scalar(seed[0:p, 0:n], ve.bitcast(I32), -0.5, MAGIC, ALU.mult, ALU.add))
                step.wait()
                cur = seed[0:p, 0:n].bitcast(F32)
                for _ in range(3):
                    step.did(dve.tensor_tensor(a_, cur, cur, ALU.mult))
                    step.wait()
                    step.did(dve.tensor_tensor(b_, a_, half, ALU.mult))
                    step.wait()
                    step.did(dve.scalar_tensor_tensor(y_, b_, 1.5, cur, ALU.add, ALU.mult))
                    step.wait()
                    cur = y_
                return y_

            def layer_norm(src, dst, n, p, eps):
                for k in range(n):
                    step.did(dve.bn_stats(st[0:p, k, :], src[:, k, :]))
                step.wait()
                for k in range(n):
                    step.did(dve.bn_aggr(mv[0:p, k, :], st[0:p, k, :]))
                step.wait()
                r = rsqrt(mv[0:p, 0:n, 1], n, p, eps, nwt)
                for k in range(n - 1):
                    step.did(dve.tensor_scalar(dst[:, k, :], src[:, k, :], mv[0:p, k, 0:1], r[:, k:k + 1],
                                               ALU.subtract, ALU.mult))
                return dve.tensor_scalar(dst[:, n - 1, :], src[:, n - 1, :], mv[0:p, n - 1, 0:1], r[:, n - 1:n],
                                         ALU.subtract, ALU.mult)

            dve.memset(xpad[:, :, :], 0.0).then_inc(pad_zeroed, 1)
            dve.wait_ge(cst_in, 16 * NCONST[0])
            r = rsqrt(cols[:, BV:BV + 1], 1, C, 1e-5, nwt)
            step.did(dve.tensor_tensor(cols[:, SC:SC + 1], cols[:, BG:BG + 1], r, ALU.mult))
            step.did(dve.tensor_tensor(cols[:, TMP:TMP + 1], cols[:, DB:DB + 1], cols[:, BM:BM + 1], ALU.subtract))
            step.wait()
            step.did(dve.scalar_tensor_tensor(cols[:, SH:SH + 1], cols[:, TMP:TMP + 1], cols[:, SC:SC + 1],
                                              cols[:, BB:BB + 1], ALU.mult, ALU.add))
            for k in range(P9):
                step.did(dve.tensor_scalar(diag[:, k, :], ident[:, :], dw[:, k:k + 1], None, ALU.mult))
            step.did(dve.tensor_tensor(ln_a[:, :, :], ln_a[:, :, :], gamma[:, :, :], ALU.mult))
            step.did(dve.tensor_tensor(ln_c[:, :, :], ln_c[:, :, :], gamma[:, :, :], ALU.mult))
            for a in range(2):
                step.did(dve.tensor_tensor(grid[:, a], grid[:, a],
                                           b_om[:, a * GP:(a + 1) * GP].unsqueeze(1).broadcast_to([TT, NT, GP]),
                                           ALU.add))
            step.restart()
            dve.sem_inc(ring_free, RING)
            dve.sem_inc(consts_made, 1)

            with dve.Fori(0, N) as i:
                def flatten(j):
                    dve.wait_ge(f_padded, i * NJ + j + 1)
                    dve.wait_ge(f_projected, i * NJ + max(j - 1, 0))
                    dve.tensor_copy(xflat[:, j % 2].rearrange("c (h w) -> c h w", w=IMG),
                                    xpad[:, 1 + ROWS * j:1 + ROWS * (j + 1), 1:1 + IMG]).then_inc(f_flat, 1)

                flatten(0)
                for j in range(NJ):
                    if j + 1 < NJ:
                        flatten(j + 1)
                    dve.wait_ge(f_projected, i * NJ + j + 1)
                    dve.wait_ge(table_out[j % 2], (i * per_parity(j) + j // 2) * (16 * 2 * CORNERS * NT))
                    dve.tensor_tensor(proj[:, j % 2], bank[1][0:TT, :].rearrange("p (t c) -> p t c", t=NT),
                                      b_in[:, :].unsqueeze(1).broadcast_to([TT, NT, C]), ALU.add)\
                        .then_inc(f_proj_kept, 1)
                for j in range(NJ):
                    lt = bank[4][0:TT, :].rearrange("p (t e) -> p t e", t=NT)
                    dve.wait_ge(f_logits, i * NJ + j + 1)
                    for a in range(2):
                        step.did(dve.tensor_tensor(pos[:, a].rearrange("p (t e) -> p t e", t=NT),
                                                   lt[:, :, a * GP:(a + 1) * GP], grid[:, a], ALU.add))
                    dve.tensor_tensor(msk[:, :].rearrange("p (t e) -> p t e", t=NT), lt[:, :, 2 * GP:3 * GP],
                                      b_om[:, 2 * GP:].unsqueeze(1).broadcast_to([TT, NT, GP]), ALU.add)\
                        .then_inc(f_logits_read, 1)
                    step.wait()
                    dve.wait_ge(f_logits_read, i * NJ + j + 1)
                    step.did(dve.tensor_reduce(mred[:, 0], msk[:, :].rearrange("p (g e) -> p g e", e=P9),
                                               AX.X, ALU.max))
                    step.did(dve.tensor_scalar(pos[:, 1], pos[:, 1], float(ROWS * j), None, ALU.add))
                    step.wait()
                    dve.tensor_tensor(msk[:, :].rearrange("p (g e) -> p g e", e=P9),
                                      msk[:, :].rearrange("p (g e) -> p g e", e=P9),
                                      mred[:, 0].unsqueeze(2).broadcast_to([TT, NT * G, P9]), ALU.subtract)\
                        .then_inc(f_mask_shifted, 1)
                    step.did(dve.tensor_scalar(pos[:, :, :], pos[:, :, :], 0.0, float(IMG + 1), ALU.max, ALU.min))
                    step.wait()
                    step.did(dve.tensor_copy(rnd[:, :, :], pos[:, :, :]))
                    step.wait()
                    step.did(dve.tensor_tensor(above[:, :, :], rnd[:, :, :], pos[:, :, :], ALU.is_gt))
                    step.wait()
                    step.did(dve.tensor_tensor(low[:, :, :], rnd[:, :, :], above[:, :, :], ALU.subtract))
                    step.wait()
                    step.did(dve.tensor_scalar(low[:, :, :], low[:, :, :], float(IMG), None, ALU.min))
                    step.wait()
                    step.did(dve.tensor_tensor(frac[:, :, :], pos[:, :, :], low[:, :, :], ALU.subtract))
                    step.did(dve.scalar_tensor_tensor(spot[:, :], low[:, 1], float(POS), low[:, 0],
                                                      ALU.mult, ALU.add))
                    step.wait()
                    step.did(dve.scalar_tensor_tensor(spot[:, :], spot[:, :], float(G), gidx[:, :],
                                                      ALU.mult, ALU.add))
                    step.wait()
                    dve.wait_ge(iw_out[j % 2], (i * per_parity(j) + j // 2) * 32)
                    step.did(dve.tensor_scalar(idx_s[:, j % 2], spot[:, :], ioff[:, bass.ds(i, 1)], None, ALU.add))
                    dve.wait_ge(f_mask_exp, i * NJ + j + 1)
                    step.did(dve.tensor_reduce(mred[:, 1], msk[:, :].rearrange("p (g e) -> p g e", e=P9),
                                               AX.X, ALU.add))
                    step.wait()
                    step.did(dve.reciprocal(mred[:, 2], mred[:, 1]))
                    step.wait()
                    step.did(dve.tensor_tensor(msk[:, :].rearrange("p (g e) -> p g e", e=P9),
                                               msk[:, :].rearrange("p (g e) -> p g e", e=P9),
                                               mred[:, 2].unsqueeze(2).broadcast_to([TT, NT * G, P9]), ALU.mult))
                    step.wait()
                    step.did(dve.tensor_tensor(my[:, 1], msk[:, :], frac[:, 1], ALU.mult))
                    step.wait()
                    step.did(dve.tensor_tensor(my[:, 0], msk[:, :], my[:, 1], ALU.subtract))
                    step.wait()
                    wv_ = wts_s[:, j % 2].rearrange("p (e y x) -> p y x e", y=2, x=2)
                    for dy in range(2):
                        step.did(dve.tensor_tensor(wv_[:, dy, 1], my[:, dy], frac[:, 0], ALU.mult))
                    step.wait()
                    step.did(dve.tensor_tensor(wv_[:, 0, 0], my[:, 0], wv_[:, 0, 1], ALU.subtract))
                    step.did(dve.tensor_tensor(wv_[:, 1, 0], my[:, 1], wv_[:, 1, 1], ALU.subtract))
                    step.wait()
                    dve.sem_inc(f_iw_made, 1)
                step.restart()

            with dve.Fori(0, SLOTS) as s:
                def keep_z(k):
                    dve.wait_ge(z_made, s * BLK + k + 1)
                    dve.tensor_tensor(z[:, k, :], bank[2][:, 0:C], b_out[:, :], ALU.add).then_inc(z_kept, 1)

                for k in range(BLK):
                    r = (s * BLK + k) % RING
                    dve.wait_ge(tile_ready, s * BLK + k + 2)
                    dve.wait_ge(y_turned, s * BLK + max(k - 1, 0))
                    corners = ring[:, bass.ds(r, 1)].rearrange("p o e c -> p (o e) c")
                    step.did(dve.tensor_tensor(
                        corners, corners,
                        wts_r[:, bass.ds(r, 1)].rearrange("p o e -> p (o e)").unsqueeze(2)
                        .broadcast_to([128, GP * CORNERS, CG]), ALU.mult))
                    step.wait()
                    dve.tensor_reduce(
                        y[:, k % 2].rearrange("p (g c) -> p g c", g=G),
                        ring[:, bass.ds(r, 1)].rearrange("p o (g e) c -> p (o g) c e", g=G), AX.X, ALU.add)\
                        .then_inc(y_made, 1)
                    dve.wait_ge(y_made, s * BLK + k + 1)
                    dve.sem_inc(ring_free, 1)
                    if k:
                        keep_z(k - 1)
                keep_z(BLK - 1)
                dve.wait_ge(z_kept, s * BLK + BLK)
                step.did(layer_norm(z, z, BLK, 128, 1e-5))
                step.wait()

                def affine(t_, k_):
                    step.did(dve.tensor_tensor(t_[:, :, :], t_[:, :, :],
                                               ln_a[:, k_].unsqueeze(1).broadcast_to([128, BLK, C]), ALU.mult))
                    step.wait()
                    step.did(dve.tensor_tensor(t_[:, :, :], t_[:, :, :],
                                               ln_c[:, k_].unsqueeze(1).broadcast_to([128, BLK, C]), ALU.add))
                    step.wait()

                affine(z, 0)
                dve.wait_ge(xb_in, s * 16 + 16)
                dve.wait_ge(x1_turned, s * 2)
                dve.tensor_tensor(x1[:, :, :], z[:, :, :], xb[:, :, :], ALU.add).then_inc(x1_made, 1)
                dve.wait_ge(tok_out, s * 16)
                for half, (k0, k1) in enumerate(((0, 4), (4, BLK))):
                    dve.wait_ge(fc2_made, s * 2 + half + 1)
                    dve.tensor_tensor(m[:, k0:k1, :],
                                      bank[5 + half][:, 0:(k1 - k0) * C].rearrange("p (k c) -> p k c", c=C),
                                      b_fc2[:, :].unsqueeze(1).broadcast_to([128, k1 - k0, C]), ALU.add)\
                        .then_inc(m_kept, 1)
                dve.wait_ge(m_kept, s * 2 + 2)
                step.did(layer_norm(m, m, BLK, 128, 1e-5))
                step.wait()
                affine(m, 1)
                dve.wait_ge(x1_made, s + 1)
                dve.tensor_tensor(m[:, :, :], m[:, :, :], x1[:, :, :], ALU.add).then_inc(x2_made, 1)
                step.restart()

            with dve.Fori(0, N) as i:
                for j in range(NJ):
                    g = i * NJ + j
                    dve.wait_ge(tok_in[j % 2], (i * per_parity(j) + j // 2) * 16 + 16)
                    dve.wait_ge(xm_turned, g)
                    layer_norm(tin[:, j % 2], xn, NT, TT, 1e-5).then_inc(xn_made, 1)
                    step.restart()
                    with dve.Fori(0, NT) as q:
                        u0, a0, qg = units(i, j, q), units_below(i, j, q), g * NT + q
                        for c in range(j):
                            dve.wait_ge(s_copied, a0 + c + 1)
                            step.did(dve.tensor_reduce(cmax[:, c:c + 1], S[:, c], AX.X, ALU.max))
                        dve.wait_ge(s_made, u0 + j + 1)
                        dve.wait_ge(p_turned, u0)
                        dve.tensor_tensor(S[:, j], bank[4 + j % 2][0:TT, 0:CH],
                                          causal[:, bass.ds(q * (-TT) + 3 * TT, CH)], ALU.add)\
                            .then_inc(s_masked, 1)
                        dve.wait_ge(s_masked, qg + 1)
                        step.did(dve.tensor_reduce(cmax[:, j:j + 1], S[:, j], AX.X, ALU.max))
                        step.wait()
                        dve.wait_ge(p_made, qg)
                        dve.tensor_reduce(nmax[:, 0:1], cmax[:, 0:j + 1], AX.X, ALU.max, negate=True)\
                            .then_inc(max_made, 1)
                        for c in range(j + 1):
                            dve.wait_ge(p_turned, u0 + c + 1)
                            dve.wait_ge(pv_made, u0 + max(c - 1, 0))
                            dve.tensor_copy(pT[:, c % 2], bank[6 + c % 2][0:TT, 0:CH].rearrange(
                                "p (t k) -> p t k", t=NT)).then_inc(pT_kept, 1)
                        dve.wait_ge(p_made, qg + 1)
                        step.did(dve.reciprocal(rinv[:, 0:1], rsum[:, 0:1]))
                        step.wait()
                        dve.wait_ge(pv_made, u0 + j + 1)
                        dve.scalar_tensor_tensor(
                            t1[:, bass.ds(q, 1)].rearrange("p o c -> p (o c)"), bank[1][0:TT, 0:C], rinv[:, 0:1],
                            tin[:, j % 2, bass.ds(q, 1)].rearrange("p o c -> p (o c)"), ALU.mult, ALU.add)\
                            .then_inc(t1_made, 1)
                        step.restart()
                    dve.wait_ge(t1_made, g * NT + NT)
                    dve.wait_ge(xn_turned, g + 1)
                    layer_norm(t1, xn, NT, TT, 1e-5).then_inc(xm_made, 1)
                    dve.wait_ge(route_made, g + 1)
                    step.did(dve.tensor_tensor(
                        lg[:, :, :], bank[2][0:TT, 0:NT * NE].rearrange("p (t e) -> p t e", e=NE),
                        b_rt[:, :].unsqueeze(1).broadcast_to([TT, NT, NE]), ALU.add))
                    step.wait()
                    step.did(dve.tensor_reduce(sred[:, 0], lg[:, :, :], AX.X, ALU.max))
                    step.wait()
                    dve.tensor_tensor(lg[:, :, :], lg[:, :, :],
                                      sred[:, 0].unsqueeze(2).broadcast_to([TT, NT, NE]), ALU.subtract)\
                        .then_inc(route_shifted, 1)
                    dve.wait_ge(route_exp, g + 1)
                    other = lg[:, :, :].unsqueeze(2).broadcast_to([TT, NT, NE, NE])
                    own = lg[:, :, :].unsqueeze(3).broadcast_to([TT, NT, NE, NE])
                    step.did(dve.tensor_tensor(cmp1[:, :, :, :], other, own, ALU.is_gt))
                    step.did(dve.tensor_tensor(cmp2[:, :, :, :], other, own, ALU.is_equal))
                    step.wait()
                    step.did(dve.tensor_tensor(
                        cmp2[:, :, :, :].rearrange("p t a b -> p t (a b)"),
                        cmp2[:, :, :, :].rearrange("p t a b -> p t (a b)"),
                        lower[:, :].unsqueeze(1).broadcast_to([TT, NT, NE * NE]), ALU.mult))
                    step.wait()
                    step.did(dve.tensor_tensor(cmp1[:, :, :, :], cmp1[:, :, :, :], cmp2[:, :, :, :], ALU.add))
                    step.wait()
                    step.did(dve.tensor_reduce(rank[:, :].rearrange("p (t e) -> p t e", e=NE), cmp1[:, :, :, :],
                                               AX.X, ALU.add))
                    step.wait()
                    step.did(dve.scalar_tensor_tensor(
                        gate[:, :, :].rearrange("p t e -> p (t e)"), rank[:, :], 2.0,
                        lg[:, :, :].rearrange("p t e -> p (t e)"), ALU.is_lt, ALU.mult))
                    step.wait()
                    step.did(dve.tensor_reduce(sred[:, 1], gate[:, :, :], AX.X, ALU.add))
                    step.wait()
                    step.did(dve.reciprocal(sred[:, 2], sred[:, 1]))
                    step.wait()
                    dve.tensor_tensor(gate[:, :, :], gate[:, :, :],
                                      sred[:, 2].unsqueeze(2).broadcast_to([TT, NT, NE]), ALU.mult)\
                        .then_inc(gate_made, 1)
                    dve.wait_ge(o_out[j % 2], (i * per_parity(j) + j // 2) * 16)
                    dve.wait_ge(gate_made, g + 1)
                    for t in range(NT):
                        dve.wait_ge(experts_made, g * NT + t + 1)
                        ot = o[:, j % 2, t, :]
                        step.did(dve.tensor_tensor(ot, bank[3][0:TT, t * C:(t + 1) * C], t1[:, t, :], ALU.add))
                        for e in range(NE):
                            step.wait()
                            step.did(dve.scalar_tensor_tensor(
                                ot, bank[4 + 2 * (t % 2) + e // 4][0:TT, (e % 4) * C:(e % 4 + 1) * C],
                                gate[:, t, e:e + 1], ot, ALU.mult, ALU.add))
                        step.wait()
                        dve.sem_inc(experts_read, 1)
                    dve.sem_inc(o_made, 1)
                    step.restart()

        @block.tensor
        def _(pe):
            pe.wait_ge(consts_made, 1)
            with pe.Fori(0, N) as i:
                def turn(j):
                    pe.wait_ge(x_in[j % 2], (i * per_parity(j) + j // 2) * 32 + 32)
                    pe.wait_ge(f_padded, i * NJ + j)
                    for t in range(NT):
                        ins = pe.transpose(bank[0][:, t * TT:(t + 1) * TT], xin[:, j % 2, t, :], ident[0:TT, 0:TT])
                    ins.then_inc(f_turned, 1)

                turn(0)
                for j in range(NJ):
                    if j + 1 < NJ:
                        turn(j + 1)
                    pe.wait_ge(f_flat, i * NJ + j + 1)
                    pe.wait_ge(f_proj_kept, i * NJ + j)
                    for t in range(NT):
                        ins = pe.matmul(bank[1][0:TT, t * C:(t + 1) * C], xflat[:, j % 2, t * TT:(t + 1) * TT], w_in[:, :],
                                        start=True, stop=True)
                    ins.then_inc(f_projected, 1)

                def conv(j):
                    pe.wait_ge(f_hidden, i * NJ + max(j - 1, 0))
                    for k in range(P9):
                        dy, dx = k // 3, k % 3
                        ins = pe.matmul(bank[2 + j % 2][:, 0:CH], diag[:, k, :],
                                        xpad[:, ROWS * j + dy:ROWS * j + dy + ROWS, dx:dx + IMG],
                                        start=(k == 0), stop=(k == P9 - 1))
                    ins.then_inc(f_convolved, 1)

                pe.wait_ge(f_padded, i * NJ + NJ)
                conv(0)
                for j in range(NJ):
                    if j + 1 < NJ:
                        conv(j + 1)
                    pe.wait_ge(f_hidden, i * NJ + j + 1)
                    pe.wait_ge(f_logits_read, i * NJ + j)
                    for t in range(NT):
                        ins = pe.matmul(bank[4][0:TT, t * C:t * C + 3 * GP], hT[:, j % 2, t * TT:(t + 1) * TT],
                                        w_om[:, :], start=True, stop=True)
                    ins.then_inc(f_logits, 1)

            with pe.Fori(0, SLOTS) as s:
                def project(k):
                    pe.wait_ge(yT_kept, s * BLK + k + 1)
                    pe.wait_ge(z_kept, s * BLK + k)
                    pe.matmul(bank[2][:, 0:C], yT[:, k % 2], w_out[:, :], start=True, stop=True).then_inc(z_made, 1)

                for k in range(BLK):
                    pe.wait_ge(y_made, s * BLK + k + 1)
                    pe.wait_ge(yT_kept, s * BLK + k)
                    pe.transpose(bank[7][:, 0:128], y[:, k % 2], ident[:, :]).then_inc(y_turned, 1)
                    project(k)
                pe.wait_ge(x1_made, s + 1)
                for half, (k0, k1) in enumerate(((0, 4), (4, BLK))):
                    pe.wait_ge(x1T_kept, s * 2)
                    for k in range(k0, k1):
                        ins = pe.transpose(bank[half][:, (k - k0) * 128:(k - k0 + 1) * 128], x1[:, k, :], ident[:, :])
                    ins.then_inc(x1_turned, 1)
                for half, (k0, k1) in enumerate(((0, 4), (4, BLK))):
                    n = (k1 - k0) * 128
                    pe.wait_ge(x1T_kept, s * 2 + half + 1)
                    for c in range(NH):
                        f = half * NH + c
                        pe.wait_ge(hid_kept, s * 2 * NH + max(f - 1, 0))
                        pe.matmul(bank[3 + c % 2][:, 0:n], w_fc1[:, c * C:(c + 1) * C], x1T[:, k0 * 128:k1 * 128],
                                  start=True, stop=True).then_inc(fc1_made, 1)
                    pe.wait_ge(hid_kept, s * 2 * NH + (half + 1) * NH)
                    pe.wait_ge(m_kept, s * 2)
                    for k in range(k0, k1):
                        for c in range(NH):
                            ins = pe.matmul(bank[5 + half][:, (k - k0) * C:(k - k0 + 1) * C],
                                            hid[:, c, (k - k0) * 128:(k - k0 + 1) * 128], w_fc2[:, c, :],
                                            start=(c == 0), stop=(c == NH - 1))
                    ins.then_inc(fc2_made, 1)

            with pe.Fori(0, N) as i:
                for j in range(NJ):
                    g = i * NJ + j
                    pe.wait_ge(o_made, g)
                    pe.wait_ge(xn_made, g + 1)
                    for t in range(NT):
                        ins = pe.transpose(bank[0][:, t * TT:(t + 1) * TT], xn[:, t, :], ident[0:TT, 0:TT])
                    ins.then_inc(xn_turned, 1)
                    pe.wait_ge(xnT_kept, g + 1)
                    pe.matmul(bank[1][:, 0:CH], wq[:, :], xnT[:, :], start=True, stop=True).then_inc(qkv_made, 1)
                    pe.matmul(bank[2][:, 0:CH], wk[:, :], xnT[:, :], start=True, stop=True).then_inc(qkv_made, 1)
                    for t in range(NT):
                        ins = pe.matmul(bank[3][0:TT, t * C:(t + 1) * C], xnT[:, t * TT:(t + 1) * TT], wv[:, :],
                                        start=True, stop=True)
                    ins.then_inc(qkv_made, 1)
                    with pe.Fori(0, NT) as q:
                        u0, a0, qg = units(i, j, q), units_below(i, j, q), g * NT + q
                        pe.wait_ge(qkv_kept, g * 3 + 3)
                        pe.wait_ge(q_staged, qg + 1)
                        for c in range(j + 1):
                            if c < 2:
                                pe.wait_ge(s_masked, qg)
                            if j:
                                pe.wait_ge(s_copied, a0 + max(c - 1, 0))
                            pe.matmul(bank[4 + c % 2][0:TT, 0:CH], q_t[:, :], kT[:, c], start=True, stop=True)\
                                .then_inc(s_made, 1)

                        def turn_p(c):
                            pe.wait_ge(pT_kept, u0 + max(c - 1, 0))
                            for t in range(NT):
                                ins = pe.transpose(bank[6 + c % 2][0:TT, t * TT:(t + 1) * TT],
                                                   S[:, c, t * TT:(t + 1) * TT], ident[0:TT, 0:TT])
                            ins.then_inc(p_turned, 1)

                        pe.wait_ge(p_made, qg + 1)
                        pe.wait_ge(t1_made, qg)
                        turn_p(0)
                        for c in range(j + 1):
                            if c < j:
                                turn_p(c + 1)
                            pe.wait_ge(pT_kept, u0 + c + 1)
                            for t in range(NT):
                                ins = pe.matmul(bank[1][0:TT, 0:C], pT[:, c % 2, t], v[:, NT * c + t],
                                                start=(c == 0 and t == 0), stop=(c == j and t == NT - 1))
                            ins.then_inc(pv_made, 1)
                    pe.wait_ge(xm_made, g + 1)
                    for t in range(NT):
                        ins = pe.transpose(bank[0][:, t * TT:(t + 1) * TT], xn[:, t, :], ident[0:TT, 0:TT])
                    ins.then_inc(xm_turned, 1)
                    pe.wait_ge(xmT_kept, g + 1)
                    for t in range(NT):
                        ins = pe.matmul(bank[2][0:TT, t * NE:(t + 1) * NE], xnT[:, t * TT:(t + 1) * TT], w_rt[:, :],
                                        start=True, stop=True)
                    ins.then_inc(route_made, 1)
                    pe.wait_ge(gate_made, g + 1)
                    for t in range(NT):
                        ins = pe.transpose(bank[0][0:NE, t * TT:(t + 1) * TT], gate[:, t, :], ident[0:TT, 0:TT])
                    ins.then_inc(gate_turned, 1)
                    pe.wait_ge(gT_kept, g + 1)
                    for t in range(NT):
                        ins = pe.matmul(bank[3][0:TT, t * C:(t + 1) * C], gT[:, t * TT:(t + 1) * TT], b_ex[:, :],
                                        start=True, stop=True)
                    for t in range(NT):
                        pe.wait_ge(experts_read, g * NT + max(t - 1, 0))
                        for hf in range(2):
                            ins = pe.matmul(bank[4 + 2 * (t % 2) + hf][0:TT, :], xnT[:, t * TT:(t + 1) * TT],
                                            w_ex[:, 4 * hf:4 * hf + 4, :], start=True, stop=True)
                        ins.then_inc(experts_made, 1)


_CONV = ["w_in", "b_in", "dw_w", "dw_b", "bn_g", "bn_b", "bn_m", "bn_v", "w_off", "b_off", "w_msk", "b_msk",
         "w_out", "b_out", "ln1_g", "ln1_b", "w_fc1", "b_fc1", "w_fc2", "b_fc2", "ln2_g", "ln2_b", "gamma1", "gamma2"]
_NAMES = {"L0_conv_" + n: n for n in _CONV}
_NAMES.update({"L1_attn_" + n: n for n in ("Wq", "Wk", "Wv")})
_NAMES.update({"L1_ffn_" + n: n for n in ("router_w", "router_b", "expert_w", "expert_b")})


def shape_constants(n_images):
    import numpy as np
    p = np.arange(TT)
    e = np.arange(GP)
    grid = np.zeros((TT, 2, NT, GP), np.float32)
    grid[:, 0] = (p % IMG)[:, None, None] + (e % P9 // 3)[None, None, :]
    grid[:, 1] = (p // IMG)[:, None, None] + 2 * np.arange(NT)[None, :, None] + (e % P9 % 3)[None, None, :]
    gidx = np.tile((e // P9).astype(np.float32), (TT, NT))
    ioff = np.tile((np.arange(n_images) * POS * POS * G).astype(np.float32), (TT, 1))
    causal = np.where(np.arange(3 * TT + CH)[None, :] <= p[:, None] + 3 * TT, 0.0, NEG).astype(np.float32)
    lower = np.tile(np.tril(np.ones((NE, NE), np.float32), -1).reshape(1, -1), (TT, 1))
    return {"ident": np.eye(128, dtype=np.float32), "grid": grid.reshape(TT, -1), "gidx": gidx, "ioff": ioff,
            "causal": causal, "lower": lower}


def kernel(**inputs):
    import numpy as np
    import concourse.bacc as bacc
    from concourse.bass_utils import run_bass_kernel_spmd

    nc = bacc.Bacc("TRN2", target_bir_lowering=False, num_devices=1)
    arrays = {"x": np.ascontiguousarray(inputs["x"])}
    for long, short in _NAMES.items():
        arrays[short] = np.ascontiguousarray(inputs[long])
    consts = shape_constants(arrays["x"].shape[0])
    given = {**arrays, **{"const_" + k: a for k, a in consts.items()}}
    aps = {k: nc.dram_tensor("in_" + k, a.shape, mybir.dt.from_np(a.dtype), kind="ExternalInput").ap()
           for k, a in given.items()}
    out = nc.dram_tensor("out_0", arrays["x"].shape, F32, kind="ExternalOutput").ap()
    build(nc, aps["x"], aps, {k: aps["const_" + k] for k in consts}, out)
    r = run_bass_kernel_spmd(nc, [{"in_" + k: a for k, a in given.items()}], core_ids=[0])
    return r.results[0]["out_0"]
```

```python
from contextlib import ExitStack

import concourse.bass as bass
from concourse import mybir

F32 = mybir.dt.float32
I32 = mybir.dt.int32
U32 = mybir.dt.uint32
ALU = mybir.AluOpType
ACT = mybir.ActivationFunctionType
AX = mybir.AxisListType

C = 128
IMG = 56
PAD = IMG + 2
TOK = IMG * IMG
ROWS = 8
CH = ROWS * IMG
NJ = IMG // ROWS
TT = 112
NT = CH // TT
G = 4
CG = C // G
P9 = 9
GP = G * P9
CORNERS = 4
POS = IMG + 1
BLK = 7
SLOTS2 = 7
TABLES = 3
LEAD = 8
FIRST = 1
PRIMED = 16
RING = 4
HID = 4 * C
NH = HID // C
NE = 8
NEG = -1.0e30
PT_BANKS = (6, 3)
EXPERT_BANKS = ((4, 5), (6, 1))
MAGIC = 1597463007.0


class Steps:

    def __init__(self, eng, sem):
        self.eng, self.sem, self.n = eng, sem, 0

    def did(self, ins):
        ins.then_inc(self.sem, 1)
        self.n += 1
        return ins

    def wait(self):
        self.eng.wait_ge(self.sem, self.n)

    def restart(self):
        self.wait()
        self.eng.sem_clear(self.sem)
        self.n = 0


def per_parity(j):
    return (NJ + 1) // 2 if j % 2 == 0 else NJ // 2


def build(nc, x, w, consts, out):
    N = x.shape[0]
    NTOK = N * TOK
    TILES = NTOK // 128
    SLOTS = TILES // BLK
    PAIR_TILES = 2 * TOK // 128
    PAIRS = N // 2
    assert N % 2 == 0 and PAIRS >= 3 and TILES % RING == 0 and TILES == PAIRS * SLOTS2 * BLK

    proj_d = nc.dram_tensor("projected", (2, CH, C), F32).ap()
    table = nc.dram_tensor("corner_table", (TABLES * POS * POS * G, CORNERS * CG), F32).ap()
    idx_d = nc.dram_tensor("corner_index", (NTOK, GP), U32).ap()
    wts_d = nc.dram_tensor("corner_weight", (NTOK, GP * CORNERS), F32).ap()
    tok_d = nc.dram_tensor("tokens", (NTOK, C), F32).ap()

    ctx = ExitStack()

    def sb(name, shape, dt=F32):
        return ctx.enter_context(nc.sbuf_tensor(name, shape, dt))

    def sem(name):
        return ctx.enter_context(nc.semaphore(name))

    with ctx:
        bank = [ctx.enter_context(nc.psum_tensor(f"bank{i}", [128, 512], F32)) for i in range(8)]

        ident = sb("ident", [128, 128])
        diag = sb("diag", [C, P9, C])
        w_in = sb("w_in", [C, C])
        w_om = sb("w_om", [C, 3 * GP])
        w_out = sb("w_out", [C, C])
        w_fc1 = sb("w_fc1", [C, HID])
        w_fc2 = sb("w_fc2", [C, NH, C])
        b_fc1 = sb("b_fc1", [C, NH])
        wq = sb("wq", [C, C])
        wk = sb("wk", [C, C])
        wv = sb("wv", [C, C])
        w_rt = sb("w_rt", [C, NE])
        w_ex = sb("w_ex", [C, NE, C])
        b_ex = sb("b_ex", [NE, C])
        cols = sb("cols", [C, 16])
        dw = sb("dw", [C, P9])
        b_in = sb("b_in", [TT, C])
        b_out = sb("b_out", [128, C])
        b_fc2 = sb("b_fc2", [128, C])
        ln_a = sb("ln_a", [128, 2, C])
        ln_c = sb("ln_c", [128, 2, C])
        gamma = sb("gamma", [128, 2, C])
        b_rt = sb("b_rt", [TT, NE])
        b_om = sb("b_om", [TT, 3 * GP])
        grid = sb("grid", [TT, 2, NT, GP])
        gidx = sb("gidx", [TT, NT * GP])
        ioff = sb("ioff", [TT, N])
        causal = sb("causal", [TT, 3 * TT + CH])
        lower = sb("lower", [TT, NE * NE])

        xin = sb("xin", [TT, 2, NT, C])
        xpad = sb("xpad", [C, PAD, PAD])
        xflat = sb("xflat", [C, 2, CH])
        proj = sb("proj", [TT, 2, NT, C])
        hT = sb("hT", [C, 2, CH])
        idx_s = sb("idx_s", [TT, 2, NT * GP], U32)
        wts_s = sb("wts_s", [TT, 2, NT * GP * CORNERS])

        ring = sb("ring", [128, RING, GP * CORNERS, CG])
        idx_r = sb("idx_r", [128, RING, GP], U32)
        wts_r = sb("wts_r", [128, RING, GP * CORNERS])
        y = sb("y", [128, 2, C])
        yT = sb("yT", [128, 128])
        z = sb("z", [128, BLK, C])
        x1 = sb("x1", [128, BLK, C])

        st = sb("st", [128, BLK, 6])
        mv = sb("mv", [128, BLK, 2])
        nwt = sb("nwt", [128, 6, BLK])
        seed = sb("seed", [128, BLK], I32)

        tin = sb("tin", [TT, 2, NT, C])
        xn = sb("xn", [TT, NT, C])
        xnT = sb("xnT", [C, CH])
        qT = sb("qT", [C, CH])
        kT = sb("kT", [C, NJ, CH])
        v = sb("v", [TT, NJ * NT, C])
        cmax = sb("cmax", [TT, NJ])
        nmax = sb("nmax", [TT, 1])
        rsum = sb("rsum", [TT, 2, NJ])
        rinv = sb("rinv", [TT, 2])
        pT = sb("pT", [TT, 2, NT, TT])
        t1 = sb("t1", [TT, NT, C])
        lg = sb("lg", [TT, NT, NE])
        cmp1 = sb("cmp1", [TT, NT, NE, NE])
        cmp2 = sb("cmp2", [TT, NT, NE, NE])
        rank = sb("rank", [TT, NT * NE])
        gate = sb("gate", [TT, NT, NE])
        sred = sb("sred", [TT, 3, NT])
        gT = sb("gT", [NE, CH])
        o = sb("o", [TT, NT, C])

        arena = sb("arena", [128, NJ * CH])
        S = arena[0:TT, :].rearrange("p (c n) -> p c n", c=NJ)
        ng = NT * GP
        pos, above, low, frac, my = (
            arena[0:TT, 2 * ng * k:2 * ng * (k + 1)].rearrange("p (a e) -> p a e", a=2) for k in range(5))
        rnd = arena[0:TT, 10 * ng:12 * ng].bitcast(I32).rearrange("p (a e) -> p a e", a=2)
        spot = arena[0:TT, 12 * ng:13 * ng]
        msk = arena[0:TT, 13 * ng:14 * ng]
        mred = arena[0:TT, 14 * ng:14 * ng + 3 * NT * G].rearrange("p (a e) -> p a e", a=3)
        hid = arena[:, 0:NH * 512].rearrange("p (m n) -> p m n", m=NH)
        x1T = arena[:, NH * 512:NH * 512 + BLK * 128]
        picked = arena[0:TT, 0:2 * (NE + 1) * C].rearrange("p (b e c) -> p b e c", b=2, c=C)
        zeros = ring[0:POS, RING - 1].rearrange("p e c -> p (e c)")[:, 0:G * CORNERS * CG]

        cst_in = sem("cst_in")
        border_out = sem("border_out")
        x_in = [sem(f"x_in{i}") for i in range(2)]
        table_out = [sem(f"table_out{i}") for i in range(2)]
        iw_out = [sem(f"iw_out{i}") for i in range(2)]
        iw_in = sem("iw_in")
        passed = sem("passed")
        table_zeroed = sem("table_zeroed")
        proj_out = [sem(f"proj_out{i}") for i in range(2)]
        gathered = [sem(f"gathered{i}") for i in range(RING)]
        xb_in = sem("xb_in")
        tok_out = sem("tok_out")
        tok_in = [sem(f"tok_in{i}") for i in range(2)]
        o_out = sem("o_out")
        zeroed = sem("zeroed")
        pad_zeroed = sem("pad_zeroed")
        consts_made = sem("consts_made")
        f_turned = sem("f_turned")
        f_padded = sem("f_padded")
        f_flat = sem("f_flat")
        f_projected = sem("f_projected")
        f_proj_kept = sem("f_proj_kept")
        f_convolved = sem("f_convolved")
        f_hidden = sem("f_hidden")
        f_logits = sem("f_logits")
        f_logits_read = sem("f_logits_read")
        f_mask_shifted = sem("f_mask_shifted")
        f_mask_exp = sem("f_mask_exp")
        f_iw_made = sem("f_iw_made")
        ring_free = sem("ring_free")
        tile_ready = sem("tile_ready")
        tile_begun = sem("tile_begun")
        y_made = sem("y_made")
        y_turned = sem("y_turned")
        yT_kept = sem("yT_kept")
        z_made = sem("z_made")
        z_kept = sem("z_kept")
        x1_made = sem("x1_made")
        x1_turned = sem("x1_turned")
        x1T_kept = sem("x1T_kept")
        fc1_made = sem("fc1_made")
        hid_kept = sem("hid_kept")
        fc2_made = sem("fc2_made")
        m_kept = sem("m_kept")
        x2_made = sem("x2_made")
        xn_made = sem("xn_made")
        xn_turned = sem("xn_turned")
        xnT_kept = sem("xnT_kept")
        qkv_made = sem("qkv_made")
        qkv_kept = sem("qkv_kept")
        s_made = sem("s_made")
        s_copied = sem("s_copied")
        s_masked = sem("s_masked")
        max_made = sem("max_made")
        p_made = sem("p_made")
        p_turned = sem("p_turned")
        pT_kept = [sem(f"pT_kept{i}") for i in range(2)]
        pv_made = sem("pv_made")
        t1_made = sem("t1_made")
        xm_made = sem("xm_made")
        xm_turned = sem("xm_turned")
        xmT_kept = sem("xmT_kept")
        route_made = sem("route_made")
        route_shifted = sem("route_shifted")
        route_exp = sem("route_exp")
        gate_made = sem("gate_made")
        gate_turned = sem("gate_turned")
        bias_made = sem("bias_made")
        picked_made = sem("picked_made")
        gT_kept = sem("gT_kept")
        experts_made = sem("experts_made")
        experts_read = sem("experts_read")
        o_made = sem("o_made")
        dve_steps = sem("dve_steps")

        SC, SH, TMP = 0, 1, 2
        BG, BB, BM, BV, DB = 4, 5, 6, 7, 8

        table_v = table.rearrange("(n y x g) d -> n y x g d", n=TABLES, y=POS, x=POS, g=G)
        x_ch = x.rearrange("n (j t r) w c -> n j (r w) t c", j=NJ, t=NT, r=2)
        x_tok = x.rearrange("n h w c -> (n h w) c")
        idx_ch = idx_d.rearrange("(n j t p) e -> n j p t e", n=N, j=NJ, t=NT)
        wts_ch = wts_d.rearrange("(n j t p) e -> n j p t e", n=N, j=NJ, t=NT)
        idx_t = idx_d.rearrange("(t p) e -> t p e", p=128)
        wts_t = wts_d.rearrange("(t p) e -> t p e", p=128)
        x_slot = x_tok.rearrange("(s k p) c -> s p k c", k=BLK, p=128)
        tok_slot = tok_d.rearrange("(s k p) c -> s p k c", k=BLK, p=128)
        tok_pair = tok_d.rearrange("(s h t p) c -> s h p t c", h=2, t=NT, p=TT)
        out_ch = out.rearrange("n h w c -> (n h w) c").rearrange("(n j t p) c -> n j p t c", n=N, j=NJ, t=NT)

        def column(v_):
            return v_.rearrange("(p a) -> p a", a=1)

        NCONST = [0]
        STORES = 16 * CORNERS

        def primed(eng, sems):
            for x_ in sems:
                eng.sem_inc(x_, FIRST)

        def units(i, j, q):
            return i * (2 * NJ * (NJ + 1)) + 2 * j * (j + 1) + q * (j + 1)

        def units_below(i, j, q):
            return i * (2 * NJ * (NJ - 1)) + 2 * j * (j - 1) + q * j

        def units_of(par, i, j, q):
            n = [(jj + 2 - par) // 2 for jj in range(NJ)]
            return i * (NT * sum(n)) + NT * sum(n[:j]) + q * n[j]

        def turned_in(j):
            return [0, 1] if j == 0 else [j + 1] if j + 1 < NJ else []

        def turned(p, f):
            i, j = 2 * p + f // NJ, f % NJ
            return i * NJ + (min(j + 1, NJ) if j else 0)

        def timeline(eng, tile, attention, experts, front, mlp):
            attention = attention or (lambda i, j, h, s, fronts, first, second: None)

            def attended(p, a):
                return 2 * p + a // NJ, a % NJ

            def slots(p):
                fixed = isinstance(p, int)
                for n in range(SLOTS2):
                    s = p * SLOTS2 + n
                    att = not (fixed and p == 0 and n == 0)
                    fronts = [2 * n + LEAD + h for h in range(2)]
                    live = [not (fixed and f + 2 * NJ * p >= N * NJ) for f in fronts]
                    for h in range(2):
                        i, j = attended(p, 2 * (n - 1) + h)
                        first, second, third = ((p, n, 3 * h + k) for k in (1, 2, 3))
                        if att:
                            attention(i, j, h, s, (p, fronts[h]), first, second)
                            experts(i, j, h, s)
                        else:
                            tile(*first)
                            tile(*second)
                        if live[h]:
                            front(p, fronts[h], s, i * NJ + j + 1 if att else 0, third)
                        else:
                            tile(*third)
                    last = fixed and p == PAIRS - 1 and n == SLOTS2 - 1
                    mlp(s, n, last, (p, fronts[1] + 1), i * NJ + j + 1 if att else 0,
                        None if last else (p, n, BLK))

            for f in range(LEAD):
                front(0, f, 0, 0)
            tile(0, 0, 0)
            slots(0)
            with eng.Fori(1, PAIRS - 1) as p:
                slots(p)
            slots(PAIRS - 1)
            for h in range(2):
                i, j = attended(PAIRS, h - 2)
                attention(i, j, h, SLOTS, (PAIRS, 0), None, None)
                experts(i, j, h, SLOTS)

        block = ctx.enter_context(nc.Block())

        @block.sync
        def _(sp):
            def const(dst, src, count=None):
                sp.dma_start(dst, src).then_inc(cst_in if count is None else count, 16)
                if count is None:
                    NCONST[0] += 1

            with nc.allow_non_contiguous_dma("constants"):
                const(ident[:, :], consts["ident"])
                sp.dma_start(xin[:, 0], x_ch[0, 0]).then_inc(x_in[0], 16)
                sp.dma_start(xin[:, 1], x_ch[0, 1]).then_inc(x_in[1], 16)
                const(dw[:, :], w["dw_w"].rearrange("c a h w -> c (a h w)"))
                for col, name in ((BG, "bn_g"), (BB, "bn_b"), (BM, "bn_m"), (BV, "bn_v"), (DB, "dw_b")):
                    const(cols[:, col:col + 1], column(w[name]))
                const(w_in[:, :], w["w_in"])
                off_v = w["w_off"].rearrange("c (e a) -> c a e", a=2)
                boff_v = w["b_off"].partition_broadcast(TT).rearrange("p (e a) -> p a e", a=2)
                for a in range(2):
                    const(w_om[:, a * GP:(a + 1) * GP], off_v[:, a, :])
                    const(b_om[:, a * GP:(a + 1) * GP], boff_v[:, a, :])
                const(w_om[:, 2 * GP:], w["w_msk"])
                const(b_om[:, 2 * GP:], w["b_msk"].partition_broadcast(TT))
                const(b_in[:, :], w["b_in"].partition_broadcast(TT))
                const(grid[:, :, :, :], consts["grid"].rearrange("p (a t e) -> p a t e", a=2, t=NT))
                const(ioff[:, :], consts["ioff"])
                const(w_out[:, :], w["w_out"])
                const(w_fc1[:, :], w["w_fc1"])
                const(w_fc2[:, :, :], w["w_fc2"].rearrange("(m p) c -> p m c", p=C))
                const(b_fc1[:, :], w["b_fc1"].rearrange("(m p) -> p m", p=C))
                const(wq[:, :], w["Wq"])
                const(wk[:, :], w["Wk"])
                const(wv[:, :], w["Wv"])
                const(w_rt[:, :], w["router_w"])
                const(w_ex[:, :, :], w["expert_w"].rearrange("e d c -> d e c"))
                const(b_ex[:, :], w["expert_b"])
                for k, (g_, a_, c_) in enumerate((("gamma1", "ln1_g", "ln1_b"), ("gamma2", "ln2_g", "ln2_b"))):
                    const(gamma[:, k, :], w[g_].partition_broadcast(128))
                    const(ln_a[:, k, :], w[a_].partition_broadcast(128))
                    const(ln_c[:, k, :], w[c_].partition_broadcast(128))
                const(causal[:, :], consts["causal"])
                const(lower[:, :], consts["lower"], iw_out[0])
                const(b_rt[:, :], w["router_b"].partition_broadcast(TT), iw_out[1])
                const(b_out[:, :], w["b_out"].partition_broadcast(128), tok_out)
                const(b_fc2[:, :], w["b_fc2"].partition_broadcast(128), o_out)

            sp.wait_ge(zeroed, 1)
            for y0 in (0, POS - 1):
                sp.dma_start(table_v[0, y0].rearrange("x g d -> x (g d)"), zeros).then_inc(border_out, 16)
            for x0 in (0, POS - 1):
                sp.dma_start(table_v[0, 1:POS - 1, x0].rearrange("y g d -> y (g d)"), zeros[0:POS - 2, :])\
                    .then_inc(border_out, 16)
            for n in range(1, TABLES):
                sp.dma_start(table_v[n].rearrange("y x g d -> x y (g d)"),
                             zeros.unsqueeze(1).broadcast_to([POS, POS, G * CORNERS * CG]))\
                    .then_inc(table_zeroed, 16)
            sp.wait_ge(border_out, 16 * 4)

            def front(p, f, s, n_att, between=None):
                i, j = 2 * p + f // NJ, f % NJ
                i1, j1 = 2 * p + (f + 1) // NJ, (f + 1) % NJ
                if not (isinstance(i1, int) and i1 >= N):
                    for c in turned_in(j1):
                        sp.wait_ge(f_turned, FIRST + i1 * NJ + max(c - 1, 0))
                        sp.sem_inc(passed, 1)
                        sp.dma_start(xin[:, c % 2], x_ch[i1, c]).then_inc(x_in[c % 2], 16)
                if isinstance(i, int) and i == 1 and j == 0:
                    sp.wait_ge(table_zeroed, 16 * (TABLES - 1))
                for c in turned_in(j):
                    sp.wait_ge(f_proj_kept, FIRST + i * NJ + c + 1)
                    sp.sem_inc(passed, 1)
                    sp.dma_start(proj_d[c % 2].rearrange("(t p) c -> p t c", p=TT), proj[:, c % 2])\
                        .then_inc(proj_out[c % 2], 16)
                for c in turned_in(j):
                    sp.wait_ge(proj_out[c % 2], (i * per_parity(c) + c // 2) * 16 + 16)
                    sp.sem_inc(passed, 1)
                    for slot in range(CORNERS):
                        y0, x0 = ROWS * c + 1 - slot // 2, 1 - slot % 2
                        sp.dma_start(table_v[i % TABLES, y0:y0 + ROWS, x0:x0 + IMG, :, slot * CG:(slot + 1) * CG]
                                     .rearrange("y x g d -> y (x g) d"),
                                     proj_d[c % 2].rearrange("(y x) (g d) -> y (x g) d", y=ROWS, g=G))\
                            .then_inc(table_out[c % 2], 16)
                sp.wait_ge(f_iw_made, FIRST + i * NJ + j + 1)
                sp.sem_inc(passed, 1)
                sp.dma_start(idx_ch[i, j], idx_s[:, j % 2].rearrange("p (t e) -> p t e", t=NT))\
                    .then_inc(iw_out[j % 2], 16)
                sp.dma_start(wts_ch[i, j], wts_s[:, j % 2].rearrange("p (t e) -> p t e", t=NT))\
                    .then_inc(iw_out[j % 2], 16)
                if isinstance(i, int) and i == 0 and j == NJ - 1:
                    image_ready(0)
                    for r in range(RING):
                        ring_load(0, r)
                    sp.dma_start(x1[:, :, :], x_slot[0]).then_inc(xb_in, 16)
                if between:
                    tile(*between)

            def image_ready(i):
                for par in range(2):
                    sp.wait_ge(table_out[par], (i + 1) * (STORES * per_parity(par)))
                    sp.sem_inc(passed, 1)
                    sp.wait_ge(iw_out[par], PRIMED + (i + 1) * (32 * per_parity(par)))
                    sp.sem_inc(passed, 1)

            def ring_load(p, t):
                r = (p * PAIR_TILES + t) % RING
                sp.wait_ge(ring_free, p * PAIR_TILES + t + 1)
                sp.sem_inc(passed, 1)
                if not (isinstance(p, int) and p * PAIR_TILES + t == 0):
                    sp.wait_ge(iw_in, (p * PAIR_TILES + t) * 32)
                    sp.sem_inc(passed, 1)
                sp.dma_start(idx_r[:, bass.ds(r, 1)].rearrange("p o e -> p (o e)"), idx_t[p * PAIR_TILES + t])\
                    .then_inc(iw_in, 16)
                sp.dma_start(wts_r[:, bass.ds(r, 1)].rearrange("p o e -> p (o e)"), wts_t[p * PAIR_TILES + t])\
                    .then_inc(iw_in, 16)

            def tile(p, n, k):
                t = n * BLK + k + RING
                if isinstance(p, int) and p * PAIR_TILES + t >= TILES:
                    return
                if t == PAIR_TILES // 2:
                    image_ready(2 * p + 1)
                if t == PAIR_TILES:
                    image_ready(2 * p + 2)
                ring_load(p, t)

            def attention(i, j, h, s, fronts, first, second):
                if first:
                    tile(*first)
                    tile(*second)

            def mlp(s, n, last, fronts, n_att, between):
                if between:
                    tile(*between)
                sp.wait_ge(x2_made, FIRST + s + 1)
                sp.sem_inc(passed, 1)
                sp.dma_start(tok_slot[s], z[:, :, :]).then_inc(tok_out, 16)
                if not last:
                    sp.dma_start(x1[:, :, :], x_slot[s + 1]).then_inc(xb_in, 16)
                sp.wait_ge(tok_out, PRIMED + s * 16 + 16)
                sp.sem_inc(passed, 1)
                for h in range(2):
                    if not (isinstance(s, int) and s == 0):
                        sp.wait_ge(t1_made, FIRST + s * (2 * NT) + NT * (h - 1))
                        sp.sem_inc(passed, 1)
                    sp.dma_start(tin[:, h], tok_pair[s, h]).then_inc(tok_in[h], 16)

            def experts(i, j, h, s):
                g = i * NJ + j
                sp.wait_ge(o_made, FIRST + g + 1)
                sp.sem_inc(passed, 1)
                sp.dma_start(out_ch[i, j], o[:, :, :]).then_inc(o_out, 16)

            timeline(sp, tile, attention, experts, front, mlp)
            sp.wait_ge(o_out, PRIMED + 16 * N * NJ)

        @block.gpsimd
        def _(pool):
            pool.memset(zeros, 0.0).then_inc(zeroed, 1)
            pool.dma_start(gidx[:, :], consts["gidx"]).then_inc(gathered[RING - 1], 16)
            with pool.Fori(0, TILES // RING) as q:
                for r in range(RING):
                    pool.wait_ge(iw_in, q * (RING * 32) + (r + 1) * 32)
                    pool.sem_inc(tile_begun, 1)
                    for e in range(GP):
                        pool.indirect_dma_start(
                            ring[:, r, e * CORNERS:(e + 1) * CORNERS, :].rearrange("p s c -> p (s c)"), None,
                            table, bass.IndirectOffsetOnAxis(ap=idx_r[:, r, e:e + 1], axis=0),
                        ).then_inc(gathered[r], 16)
                        if e == 5:
                            if r:
                                pool.wait_ge(gathered[r - 1], q * (16 * GP) + 16 * GP)
                            else:
                                pool.wait_ge(gathered[RING - 1], q * (16 * GP) + PRIMED)
                            pool.sem_inc(tile_ready, 1)
            pool.wait_ge(gathered[RING - 1], 16 * GP * (TILES // RING) + PRIMED)
            pool.sem_inc(tile_ready, 1)

        @block.scalar
        def _(act):
            primed(act, (f_padded, f_hidden, f_mask_exp, yT_kept, x1T_kept, hid_kept, xnT_kept, qkv_kept, s_copied,
                         p_made, pT_kept[0], xmT_kept, route_exp, gT_kept, picked_made))
            act.wait_ge(pad_zeroed, 1)

            def front(p, f, s, n_att, between=None):
                i, j = 2 * p + f // NJ, f % NJ
                for c in turned_in(j):
                    act.wait_ge(f_turned, FIRST + i * NJ + c + 1)
                    if c == 0:
                        act.wait_ge(f_convolved, FIRST + i * NJ)
                        act.wait_ge(f_flat, FIRST + i * NJ)
                    act.activation(xpad[:, 1 + ROWS * c:1 + ROWS * (c + 1), 1:1 + IMG],
                                   bank[0][:, 0:CH].rearrange("c (h w) -> c h w", w=IMG), ACT.Copy)\
                        .then_inc(f_padded, 1)
                act.wait_ge(f_convolved, FIRST + i * NJ + j + 1)
                act.wait_ge(f_logits, FIRST + i * NJ + max(j - 1, 0))
                act.activation(hT[:, j % 2], bank[2 + j % 2][:, 0:CH], ACT.Gelu,
                               bias=cols[:, SH:SH + 1], scale=cols[:, SC:SC + 1]).then_inc(f_hidden, 1)
                if between:
                    tile(*between)
                act.wait_ge(f_mask_shifted, FIRST + i * NJ + j + 1)
                act.activation(msk, msk, ACT.Exp).then_inc(f_mask_exp, 1)

            def tile(p, n, k):
                if k % BLK:
                    turned_tile(p * PAIR_TILES + n * BLK + k - 1)

            def turned_tile(t):
                act.wait_ge(y_turned, FIRST + t + 1)
                act.activation(yT[:, :], bank[7][:, 0:128], ACT.Copy).then_inc(yT_kept, 1)

            def mlp(s, n, last, fronts, n_att, between):
                turned_tile(s * BLK + BLK - 1)
                for half, (k0, k1) in enumerate(((0, 4), (4, BLK))):
                    act.wait_ge(x1_turned, FIRST + s * 2 + half + 1)
                    act.activation(x1T[:, k0 * 128:k1 * 128], bank[half][:, 0:(k1 - k0) * 128], ACT.Copy)\
                        .then_inc(x1T_kept, 1)
                for half, (k0, k1) in enumerate(((0, 4), (4, BLK))):
                    cols_ = (k1 - k0) * 128
                    act.wait_ge(fc2_made, FIRST + s * 2 + half)
                    for c in range(NH):
                        act.wait_ge(fc1_made, FIRST + s * (2 * NH) + half * NH + c + 1)
                        act.activation(hid[:, c, 0:cols_], bank[2 + c % 2][:, 0:cols_], ACT.Gelu,
                                       bias=b_fc1[:, c:c + 1]).then_inc(hid_kept, 1)

            def attention(i, j, h, s, fronts, first, second):
                g = i * NJ + j
                act.wait_ge(xn_turned, FIRST + g + 1)
                act.activation(xnT[:, :], bank[0][:, 0:CH], ACT.Copy).then_inc(xnT_kept, 1)
                act.wait_ge(qkv_made, FIRST + g * 3 + 1)
                act.activation(qT[:, :], bank[1][:, 0:CH], ACT.Copy, scale=float(C) ** -0.5).then_inc(qkv_kept, 1)
                act.wait_ge(qkv_made, FIRST + g * 3 + 2)
                if j == 0:
                    act.wait_ge(pv_made, FIRST + units(i, 0, 0))
                act.activation(kT[:, j], bank[2][:, 0:CH], ACT.Copy).then_inc(qkv_kept, 1)
                act.wait_ge(qkv_made, FIRST + g * 3 + 3)
                act.activation(v[:, NT * j:NT * (j + 1), :],
                               bank[3][0:TT, :].rearrange("p (t c) -> p t c", t=NT), ACT.Copy)\
                    .then_inc(qkv_kept, 1)

                def keep_scores(q, c):
                    u0 = units(i, j, q)
                    act.wait_ge(s_made, FIRST + u0 + c + 1)
                    act.wait_ge(p_turned, FIRST + (units(i, j, q - 1) + c + 1 if q else u0))
                    act.activation(S[:, c], bank[4 + c % 2][0:TT, 0:CH], ACT.Copy).then_inc(s_copied, 1)

                for c in range(j):
                    keep_scores(0, c)
                if first:
                    tile(*first)
                for q in range(NT):
                    u0, e0, qg = units(i, j, q), units_of(0, i, j, q), g * NT + q
                    act.wait_ge(max_made, FIRST + qg + 1)
                    act.wait_ge(s_copied, FIRST + units_below(i, j, q) + j)
                    if q >= 2:
                        act.wait_ge(t1_made, FIRST + qg - 1)
                    for c in range(j + 1):
                        act.activation(S[:, c], S[:, c], ACT.Exp, bias=nmax[:, 0:1],
                                       accum_out=rsum[:, q % 2, c:c + 1]).then_inc(p_made, 1)
                    for c in range(j + 1):
                        if c % 2 == 0:
                            act.wait_ge(p_turned, FIRST + u0 + c + 1)
                            act.wait_ge(pv_made, FIRST + u0 + max(c - 1, 0))
                            act.activation(pT[:, 0], bank[6][0:TT, 0:CH].rearrange("p (t k) -> p t k", t=NT),
                                           ACT.Copy).then_inc(pT_kept[0], 1)
                        if q + 1 < NT and c < j:
                            keep_scores(q + 1, c)
                    if q == 1 and second:
                        tile(*second)

            def experts(i, j, h, s):
                g = i * NJ + j
                act.wait_ge(xm_turned, FIRST + g + 1)
                act.activation(xnT[:, :], bank[0][:, 0:CH], ACT.Copy).then_inc(xmT_kept, 1)
                act.wait_ge(route_shifted, FIRST + g + 1)
                act.activation(lg[:, :, :], lg[:, :, :], ACT.Exp).then_inc(route_exp, 1)
                act.wait_ge(gate_turned, FIRST + g + 1)
                act.activation(gT[:, :], bank[0][0:NE, 0:CH], ACT.Copy).then_inc(gT_kept, 1)
                for t in range(NT):
                    act.wait_ge(experts_made, FIRST + g * NT + t + 1)
                    act.wait_ge(experts_read, FIRST + g * NT + max(t - 1, 0))
                    for e in range(NE):
                        ins = act.activation(
                            picked[:, t % 2, e], bank[EXPERT_BANKS[t % 2][e // 4]][0:TT, (e % 4) * C:(e % 4 + 1) * C],
                            ACT.Copy, scale=gate[:, t, e:e + 1])
                    ins.then_inc(picked_made, 1)

            timeline(act, tile, attention, experts, front, mlp)

        @block.vector
        def _(dve):
            step = Steps(dve, dve_steps)
            primed(dve, (f_flat, f_proj_kept, f_logits_read, f_mask_shifted, f_iw_made, y_made, z_kept, x1_made,
                         m_kept, x2_made, xn_made, s_masked, max_made, pT_kept[1], t1_made, xm_made, route_shifted,
                         gate_made, experts_read, o_made))

            def rsqrt(val, n, p, eps, scratch):
                ve, half, y_, a_, b_ = (scratch[0:p, k, 0:n] for k in range(5))
                step.did(dve.tensor_scalar(ve, val, eps, None, ALU.add))
                step.wait()
                step.did(dve.tensor_scalar(half, ve, -0.5, None, ALU.mult))
                step.did(dve.tensor_scalar(seed[0:p, 0:n], ve.bitcast(I32), -0.5, MAGIC, ALU.mult, ALU.add))
                step.wait()
                cur = seed[0:p, 0:n].bitcast(F32)
                for _ in range(3):
                    step.did(dve.tensor_tensor(a_, cur, cur, ALU.mult))
                    step.wait()
                    step.did(dve.tensor_tensor(b_, a_, half, ALU.mult))
                    step.wait()
                    step.did(dve.scalar_tensor_tensor(y_, b_, 1.5, cur, ALU.add, ALU.mult))
                    step.wait()
                    cur = y_
                return y_

            def layer_norm(src, dst, n, p, eps):
                for k in range(n):
                    step.did(dve.bn_stats(st[0:p, k, :], src[:, k, :]))
                step.wait()
                for k in range(n):
                    step.did(dve.bn_aggr(mv[0:p, k, :], st[0:p, k, :]))
                step.wait()
                r = rsqrt(mv[0:p, 0:n, 1], n, p, eps, nwt)
                for k in range(n - 1):
                    step.did(dve.tensor_scalar(dst[:, k, :], src[:, k, :], mv[0:p, k, 0:1], r[:, k:k + 1],
                                               ALU.subtract, ALU.mult))
                return dve.tensor_scalar(dst[:, n - 1, :], src[:, n - 1, :], mv[0:p, n - 1, 0:1], r[:, n - 1:n],
                                         ALU.subtract, ALU.mult)

            dve.memset(xpad[:, :, :], 0.0).then_inc(pad_zeroed, 1)
            dve.wait_ge(cst_in, 16 * NCONST[0])
            for x_ in (iw_out[0], iw_out[1], tok_out, o_out, gathered[RING - 1]):
                dve.wait_ge(x_, PRIMED)
            r = rsqrt(cols[:, BV:BV + 1], 1, C, 1e-5, nwt)
            step.did(dve.tensor_tensor(cols[:, SC:SC + 1], cols[:, BG:BG + 1], r, ALU.mult))
            step.did(dve.tensor_tensor(cols[:, TMP:TMP + 1], cols[:, DB:DB + 1], cols[:, BM:BM + 1], ALU.subtract))
            step.wait()
            step.did(dve.scalar_tensor_tensor(cols[:, SH:SH + 1], cols[:, TMP:TMP + 1], cols[:, SC:SC + 1],
                                              cols[:, BB:BB + 1], ALU.mult, ALU.add))
            for k in range(P9):
                step.did(dve.tensor_scalar(diag[:, k, :], ident[:, :], dw[:, k:k + 1], None, ALU.mult))
            step.did(dve.tensor_tensor(ln_a[:, :, :], ln_a[:, :, :], gamma[:, :, :], ALU.mult))
            step.did(dve.tensor_tensor(ln_c[:, :, :], ln_c[:, :, :], gamma[:, :, :], ALU.mult))
            for a in range(2):
                step.did(dve.tensor_tensor(grid[:, a], grid[:, a],
                                           b_om[:, a * GP:(a + 1) * GP].unsqueeze(1).broadcast_to([TT, NT, GP]),
                                           ALU.add))
            step.restart()
            dve.sem_inc(ring_free, RING)
            dve.sem_inc(consts_made, 1)

            def front(p, f, s, n_att, between=None):
                i, j = 2 * p + f // NJ, f % NJ
                for c in turned_in(j):
                    dve.wait_ge(f_padded, FIRST + i * NJ + c + 1)
                    dve.wait_ge(f_projected, FIRST + i * NJ + max(c - 1, 0))
                    dve.tensor_copy(xflat[:, c % 2].rearrange("c (h w) -> c h w", w=IMG),
                                    xpad[:, 1 + ROWS * c:1 + ROWS * (c + 1), 1:1 + IMG]).then_inc(f_flat, 1)
                for c in turned_in(j):
                    dve.wait_ge(f_projected, FIRST + i * NJ + c + 1)
                    if not (isinstance(i, int) and i == 0 and c < 2):
                        dve.wait_ge(table_out[c % 2], (i * per_parity(c) + c // 2) * STORES)
                    dve.tensor_tensor(proj[:, c % 2], bank[1][0:TT, :].rearrange("p (t c) -> p t c", t=NT),
                                      b_in[:, :].unsqueeze(1).broadcast_to([TT, NT, C]), ALU.add)\
                        .then_inc(f_proj_kept, 1)
                if between:
                    tile(*between)
                lt = bank[4][0:TT, :].rearrange("p (t e) -> p t e", t=NT)
                by_group = msk.rearrange("p (g e) -> p g e", e=P9)
                dve.wait_ge(f_logits, FIRST + i * NJ + j + 1)
                for a in range(2):
                    step.did(dve.tensor_tensor(pos[:, a].rearrange("p (t e) -> p t e", t=NT),
                                               lt[:, :, a * GP:(a + 1) * GP], grid[:, a], ALU.add))
                dve.tensor_tensor(msk.rearrange("p (t e) -> p t e", t=NT), lt[:, :, 2 * GP:3 * GP],
                                  b_om[:, 2 * GP:].unsqueeze(1).broadcast_to([TT, NT, GP]), ALU.add)\
                    .then_inc(f_logits_read, 1)
                step.wait()
                dve.wait_ge(f_logits_read, FIRST + i * NJ + j + 1)
                step.did(dve.tensor_reduce(mred[:, 0], by_group, AX.X, ALU.max))
                step.did(dve.tensor_scalar(pos[:, 1], pos[:, 1], float(ROWS * j), None, ALU.add))
                step.wait()
                dve.tensor_tensor(by_group, by_group, mred[:, 0].unsqueeze(2).broadcast_to([TT, NT * G, P9]),
                                  ALU.subtract).then_inc(f_mask_shifted, 1)
                step.did(dve.tensor_scalar(pos, pos, 0.0, float(IMG + 1), ALU.max, ALU.min))
                step.wait()
                step.did(dve.tensor_copy(rnd, pos))
                step.wait()
                step.did(dve.tensor_tensor(above, rnd, pos, ALU.is_gt))
                step.wait()
                step.did(dve.tensor_tensor(low, rnd, above, ALU.subtract))
                step.wait()
                step.did(dve.tensor_scalar(low, low, float(IMG), None, ALU.min))
                step.wait()
                step.did(dve.tensor_tensor(frac, pos, low, ALU.subtract))
                step.did(dve.scalar_tensor_tensor(spot, low[:, 1], float(POS), low[:, 0], ALU.mult, ALU.add))
                step.wait()
                step.did(dve.scalar_tensor_tensor(spot, spot, float(G), gidx[:, :], ALU.mult, ALU.add))
                step.wait()
                dve.wait_ge(iw_out[j % 2], PRIMED + (i * per_parity(j) + j // 2) * 32)
                step.did(dve.tensor_scalar(idx_s[:, j % 2], spot, ioff[:, bass.ds(i, 1)], None, ALU.add))
                dve.wait_ge(f_mask_exp, FIRST + i * NJ + j + 1)
                step.did(dve.tensor_reduce(mred[:, 1], by_group, AX.X, ALU.add))
                step.wait()
                step.did(dve.reciprocal(mred[:, 2], mred[:, 1]))
                step.wait()
                step.did(dve.tensor_tensor(by_group, by_group,
                                           mred[:, 2].unsqueeze(2).broadcast_to([TT, NT * G, P9]), ALU.mult))
                step.wait()
                step.did(dve.tensor_tensor(my[:, 1], msk, frac[:, 1], ALU.mult))
                step.wait()
                step.did(dve.tensor_tensor(my[:, 0], msk, my[:, 1], ALU.subtract))
                step.wait()
                corner = wts_s[:, j % 2].rearrange("p (e y x) -> p y x e", y=2, x=2)
                for dy in range(2):
                    step.did(dve.tensor_tensor(corner[:, dy, 1], my[:, dy], frac[:, 0], ALU.mult))
                step.wait()
                for dy in range(2):
                    step.did(dve.tensor_tensor(corner[:, dy, 0], my[:, dy], corner[:, dy, 1], ALU.subtract))
                step.restart()
                dve.sem_inc(f_iw_made, 1)

            def keep_z(t, k):
                dve.wait_ge(z_made, FIRST + t + 1)
                dve.tensor_tensor(z[:, k, :], bank[7][:, 128:128 + C], b_out[:, :], ALU.add).then_inc(z_kept, 1)

            def multiply(p, n, k):
                t = p * PAIR_TILES + n * BLK + k
                r = t % RING
                dve.wait_ge(tile_ready, t + 2)
                dve.wait_ge(y_turned, FIRST + t - (1 if k % BLK else 0))
                corners = ring[:, bass.ds(r, 1)].rearrange("p o e c -> p (o e) c")
                step.did(dve.tensor_tensor(
                    corners, corners,
                    wts_r[:, bass.ds(r, 1)].rearrange("p o e -> p (o e)").unsqueeze(2)
                    .broadcast_to([128, GP * CORNERS, CG]), ALU.mult))

            def sum_up(p, n, k):
                t = p * PAIR_TILES + n * BLK + k
                step.restart()
                dve.tensor_reduce(
                    y[:, k % BLK % 2].rearrange("p (g c) -> p g c", g=G),
                    ring[:, bass.ds(t % RING, 1)].rearrange("p o (g e) c -> p (o g) c e", g=G), AX.X, ALU.add)\
                    .then_inc(y_made, 1)
                if k % BLK:
                    keep_z(t - 1, k - 1)
                dve.wait_ge(y_made, FIRST + t + 1)
                dve.sem_inc(ring_free, 1)

            def tile(p, n, k):
                multiply(p, n, k)
                sum_up(p, n, k)

            def mlp(s, n, last, fronts, n_att, between):
                def affine(k_):
                    step.did(dve.tensor_tensor(z[:, :, :], z[:, :, :],
                                               ln_a[:, k_].unsqueeze(1).broadcast_to([128, BLK, C]), ALU.mult))
                    step.wait()
                    step.did(dve.tensor_tensor(z[:, :, :], z[:, :, :],
                                               ln_c[:, k_].unsqueeze(1).broadcast_to([128, BLK, C]), ALU.add))
                    step.wait()

                keep_z(s * BLK + BLK - 1, BLK - 1)
                dve.wait_ge(z_kept, FIRST + s * BLK + BLK)
                step.did(layer_norm(z, z, BLK, 128, 1e-5))
                step.wait()
                affine(0)
                dve.wait_ge(xb_in, s * 16 + 16)
                dve.tensor_tensor(x1[:, :, :], z[:, :, :], x1[:, :, :], ALU.add).then_inc(x1_made, 1)
                dve.wait_ge(x1_made, FIRST + s + 1)
                if between:
                    tile(*between)
                for half, (k0, k1) in enumerate(((0, 4), (4, BLK))):
                    dve.wait_ge(fc2_made, FIRST + s * 2 + half + 1)
                    dve.tensor_tensor(z[:, k0:k1, :],
                                      bank[4 + half][:, 0:(k1 - k0) * C].rearrange("p (k c) -> p k c", c=C),
                                      b_fc2[:, :].unsqueeze(1).broadcast_to([128, k1 - k0, C]), ALU.add)\
                        .then_inc(m_kept, 1)
                dve.wait_ge(m_kept, FIRST + s * 2 + 2)
                step.did(layer_norm(z, z, BLK, 128, 1e-5))
                step.wait()
                affine(1)
                dve.tensor_tensor(z[:, :, :], z[:, :, :], x1[:, :, :], ALU.add).then_inc(x2_made, 1)
                step.restart()
                dve.wait_ge(tok_out, PRIMED + s * 16 + 16)

            def attention(i, j, h, s, fronts, first, second):
                g = i * NJ + j
                dve.wait_ge(tok_in[h], s * 16)
                dve.wait_ge(xm_turned, FIRST + g)
                layer_norm(tin[:, h], xn, NT, TT, 1e-5).then_inc(xn_made, 1)
                if first:
                    tile(*first)

                def chunk_max(q, c):
                    u0 = units(i, j, q)
                    if c < j:
                        dve.wait_ge(s_copied, FIRST + units_below(i, j, q) + c + 1)
                    else:
                        dve.wait_ge(s_made, FIRST + u0 + j + 1)
                        dve.wait_ge(p_turned, FIRST + u0)
                        dve.tensor_tensor(S[:, j], bank[4 + j % 2][0:TT, 0:CH],
                                          causal[:, (NT - 1 - q) * TT:(NT - 1 - q) * TT + CH], ALU.add)\
                            .then_inc(s_masked, 1)
                        dve.wait_ge(s_masked, FIRST + g * NT + q + 1)
                    step.did(dve.tensor_reduce(cmax[:, c:c + 1], S[:, c], AX.X, ALU.max))

                def row_max(q):
                    step.wait()
                    dve.wait_ge(p_made, FIRST + units(i, j, q))
                    dve.tensor_reduce(nmax[:, 0:1], cmax[:, 0:j + 1], AX.X, ALU.max, negate=True)\
                        .then_inc(max_made, 1)
                    dve.wait_ge(max_made, FIRST + g * NT + q + 1)

                for c in range(j + 1):
                    chunk_max(0, c)
                row_max(0)
                for q in range(NT):
                    u0 = units(i, j, q)
                    for c in range(j + 1):
                        if c % 2:
                            dve.wait_ge(p_turned, FIRST + u0 + c + 1)
                            dve.wait_ge(pv_made, FIRST + u0 + c - 1)
                            dve.tensor_copy(pT[:, 1], bank[3][0:TT, 0:CH].rearrange("p (t k) -> p t k", t=NT))\
                                .then_inc(pT_kept[1], 1)
                        if q + 1 < NT:
                            chunk_max(q + 1, c)
                    if q + 1 < NT:
                        row_max(q + 1)
                    dve.wait_ge(p_made, FIRST + u0 + j + 1)
                    step.did(dve.tensor_reduce(rinv[:, 0:1], rsum[:, q % 2, 0:j + 1], AX.X, ALU.add))
                    step.wait()
                    step.did(dve.reciprocal(rinv[:, 1:2], rinv[:, 0:1]))
                    step.wait()
                    dve.wait_ge(pv_made, FIRST + u0 + j + 1)
                    dve.scalar_tensor_tensor(t1[:, q, :], bank[1][0:TT, 0:C], rinv[:, 1:2], tin[:, h, q, :],
                                             ALU.mult, ALU.add).then_inc(t1_made, 1)
                    if second and q == 0:
                        multiply(*second)
                    if second and q == 1:
                        sum_up(*second)
                step.restart()

            def experts(i, j, h, s):
                g = i * NJ + j
                dve.wait_ge(t1_made, FIRST + g * NT + NT)
                dve.wait_ge(xn_turned, FIRST + g + 1)
                layer_norm(t1, xn, NT, TT, 1e-5).then_inc(xm_made, 1)
                dve.wait_ge(route_made, FIRST + g + 1)
                step.did(dve.tensor_tensor(
                    lg[:, :, :], bank[2][0:TT, 0:NT * NE].rearrange("p (t e) -> p t e", e=NE),
                    b_rt[:, :].unsqueeze(1).broadcast_to([TT, NT, NE]), ALU.add))
                step.wait()
                step.did(dve.tensor_reduce(sred[:, 0], lg[:, :, :], AX.X, ALU.max))
                step.wait()
                dve.tensor_tensor(lg[:, :, :], lg[:, :, :],
                                  sred[:, 0].unsqueeze(2).broadcast_to([TT, NT, NE]), ALU.subtract)\
                    .then_inc(route_shifted, 1)
                dve.wait_ge(route_exp, FIRST + g + 1)
                other = lg[:, :, :].unsqueeze(2).broadcast_to([TT, NT, NE, NE])
                own = lg[:, :, :].unsqueeze(3).broadcast_to([TT, NT, NE, NE])
                step.did(dve.tensor_tensor(cmp1[:, :, :, :], other, own, ALU.is_gt))
                step.did(dve.tensor_tensor(cmp2[:, :, :, :], other, own, ALU.is_equal))
                step.wait()
                step.did(dve.tensor_tensor(
                    cmp2[:, :, :, :].rearrange("p t a b -> p t (a b)"),
                    cmp2[:, :, :, :].rearrange("p t a b -> p t (a b)"),
                    lower[:, :].unsqueeze(1).broadcast_to([TT, NT, NE * NE]), ALU.mult))
                step.wait()
                step.did(dve.tensor_tensor(cmp1[:, :, :, :], cmp1[:, :, :, :], cmp2[:, :, :, :], ALU.add))
                step.wait()
                step.did(dve.tensor_reduce(rank[:, :].rearrange("p (t e) -> p t e", e=NE), cmp1[:, :, :, :],
                                           AX.X, ALU.add))
                step.wait()
                step.did(dve.scalar_tensor_tensor(
                    gate[:, :, :].rearrange("p t e -> p (t e)"), rank[:, :], 2.0,
                    lg[:, :, :].rearrange("p t e -> p (t e)"), ALU.is_lt, ALU.mult))
                step.wait()
                step.did(dve.tensor_reduce(sred[:, 1], gate[:, :, :], AX.X, ALU.add))
                step.wait()
                step.did(dve.reciprocal(sred[:, 2], sred[:, 1]))
                step.wait()
                dve.tensor_tensor(gate[:, :, :], gate[:, :, :],
                                  sred[:, 2].unsqueeze(2).broadcast_to([TT, NT, NE]), ALU.mult)\
                    .then_inc(gate_made, 1)
                dve.wait_ge(o_out, PRIMED + g * 16)
                dve.wait_ge(bias_made, FIRST + g + 1)
                for t in range(NT):
                    step.did(dve.tensor_tensor(picked[:, t % 2, NE], bank[3][0:TT, t * C:(t + 1) * C],
                                               t1[:, t, :], ALU.add))
                    step.wait()
                    dve.wait_ge(picked_made, FIRST + g * NT + t + 1)
                    dve.tensor_reduce(o[:, t, :], picked[:, t % 2].rearrange("p e c -> p c e"), AX.X, ALU.add)\
                        .then_inc(experts_read, 1)
                dve.wait_ge(experts_read, FIRST + g * NT + NT)
                dve.sem_inc(o_made, 1)
                step.restart()

            timeline(dve, tile, attention, experts, front, mlp)

        @block.tensor
        def _(pe):
            primed(pe, (f_turned, f_projected, f_convolved, f_logits, y_turned, z_made, x1_turned, fc1_made,
                        fc2_made, xn_turned, qkv_made, s_made, p_turned, pv_made, xm_turned, route_made,
                        gate_turned, bias_made, experts_made))
            pe.wait_ge(consts_made, 1)

            def banks_left(fronts, n_mlp, n_att):
                p, f = fronts
                if isinstance(p, int) and 2 * NJ * p + f > N * NJ:
                    p, f = PAIRS, 0
                pe.wait_ge(f_proj_kept, FIRST + turned(p, f))
                pe.wait_ge(f_logits_read, FIRST + p * (2 * NJ) + f)
                pe.wait_ge(m_kept, FIRST + n_mlp * 2)
                pe.wait_ge(experts_read, FIRST + n_att * NT)

            def front(p, f, s, n_att, between=None):
                i, j = 2 * p + f // NJ, f % NJ
                banks_left((p, f), s, n_att)

                def turn(c):
                    pe.wait_ge(x_in[c % 2], (i * per_parity(c) + c // 2) * 16 + 16)
                    pe.wait_ge(f_padded, FIRST + i * NJ + c)
                    for t in range(NT):
                        ins = pe.transpose(bank[0][:, t * TT:(t + 1) * TT], xin[:, c % 2, t, :], ident[0:TT, 0:TT])
                    ins.then_inc(f_turned, 1)

                for c in turned_in(j):
                    turn(c)
                for c in turned_in(j):
                    pe.wait_ge(f_flat, FIRST + i * NJ + c + 1)
                    pe.wait_ge(f_proj_kept, FIRST + i * NJ + c)
                    for t in range(NT):
                        ins = pe.matmul(bank[1][0:TT, t * C:(t + 1) * C], xflat[:, c % 2, t * TT:(t + 1) * TT],
                                        w_in[:, :], start=True, stop=True)
                    ins.then_inc(f_projected, 1)
                for k in range(P9):
                    dy, dx = k // 3, k % 3
                    ins = pe.matmul(bank[2 + j % 2][:, 0:CH], diag[:, k, :],
                                    xpad[:, ROWS * j + dy:ROWS * j + dy + ROWS, dx:dx + IMG],
                                    start=(k == 0), stop=(k == P9 - 1))
                ins.then_inc(f_convolved, 1)
                pe.wait_ge(f_hidden, FIRST + i * NJ + j + 1)
                for t in range(NT):
                    ins = pe.matmul(bank[4][0:TT, t * C:t * C + 3 * GP], hT[:, j % 2, t * TT:(t + 1) * TT],
                                    w_om[:, :], start=True, stop=True)
                ins.then_inc(f_logits, 1)
                if between:
                    tile(*between)

            def tile(p, n, k):
                if k % BLK:
                    project(p * PAIR_TILES + n * BLK + k - 1, k - 1)

            def project(t, k):
                pe.wait_ge(y_made, FIRST + t + 1)
                pe.wait_ge(z_kept, FIRST + t)
                pe.transpose(bank[7][:, 0:128], y[:, k % 2], ident[:, :]).then_inc(y_turned, 1)
                pe.wait_ge(yT_kept, FIRST + t + 1)
                pe.matmul(bank[7][:, 128:128 + C], yT[:, :], w_out[:, :], start=True, stop=True).then_inc(z_made, 1)

            def mlp(s, n, last, fronts, n_att, between):
                project(s * BLK + BLK - 1, BLK - 1)
                banks_left(fronts, s, n_att)
                pe.wait_ge(x1_made, FIRST + s + 1)
                halves = ((0, 4), (4, BLK))
                for half, (k0, k1) in enumerate(halves):
                    for k in range(k0, k1):
                        ins = pe.transpose(bank[half][:, (k - k0) * 128:(k - k0 + 1) * 128], x1[:, k, :], ident[:, :])
                    ins.then_inc(x1_turned, 1)
                for half, (k0, k1) in enumerate(halves):
                    pe.wait_ge(x1T_kept, FIRST + s * 2 + half + 1)
                    for c in range(NH):
                        pe.wait_ge(hid_kept, FIRST + s * (2 * NH) + max(half * NH + c - 1, 0))
                        pe.matmul(bank[2 + c % 2][:, 0:(k1 - k0) * 128], w_fc1[:, c * C:(c + 1) * C],
                                  x1T[:, k0 * 128:k1 * 128], start=True, stop=True).then_inc(fc1_made, 1)
                    pe.wait_ge(hid_kept, FIRST + s * (2 * NH) + (half + 1) * NH)
                    for k in range(k0, k1):
                        for c in range(NH):
                            ins = pe.matmul(bank[4 + half][:, (k - k0) * C:(k - k0 + 1) * C],
                                            hid[:, c, (k - k0) * 128:(k - k0 + 1) * 128], w_fc2[:, c, :],
                                            start=(c == 0), stop=(c == NH - 1))
                    ins.then_inc(fc2_made, 1)

            def attention(i, j, h, s, fronts, first, second):
                g = i * NJ + j
                banks_left(fronts, s, g)
                pe.wait_ge(xn_made, FIRST + g + 1)
                for t in range(NT):
                    ins = pe.transpose(bank[0][:, t * TT:(t + 1) * TT], xn[:, t, :], ident[0:TT, 0:TT])
                ins.then_inc(xn_turned, 1)
                pe.wait_ge(xnT_kept, FIRST + g + 1)
                pe.matmul(bank[1][:, 0:CH], wq[:, :], xnT[:, :], start=True, stop=True).then_inc(qkv_made, 1)
                pe.matmul(bank[2][:, 0:CH], wk[:, :], xnT[:, :], start=True, stop=True).then_inc(qkv_made, 1)
                for t in range(NT):
                    ins = pe.matmul(bank[3][0:TT, t * C:(t + 1) * C], xnT[:, t * TT:(t + 1) * TT], wv[:, :],
                                    start=True, stop=True)
                ins.then_inc(qkv_made, 1)

                def scores(q, c):
                    if q == 0 and c in (0, j):
                        pe.wait_ge(qkv_kept, FIRST + g * 3 + (3 if c == j else 1))
                    if c < 2:
                        pe.wait_ge(s_masked, FIRST + g * NT + q)
                    if j:
                        pe.wait_ge(s_copied, FIRST + units_below(i, j, q) + max(c - 1, 0))
                    pe.matmul(bank[4 + c % 2][0:TT, 0:CH], qT[:, q * TT:(q + 1) * TT], kT[:, c],
                              start=True, stop=True).then_inc(s_made, 1)

                def turn(q, c):
                    pe.wait_ge(p_made, FIRST + units(i, j, q) + c + 1)
                    pe.wait_ge(pT_kept[c % 2], FIRST + units_of(c % 2, i, j, q) + c // 2)
                    for t in range(NT):
                        ins = pe.transpose(bank[PT_BANKS[c % 2]][0:TT, t * TT:(t + 1) * TT],
                                           S[:, c, t * TT:(t + 1) * TT], ident[0:TT, 0:TT])
                    ins.then_inc(p_turned, 1)

                for c in range(j + 1):
                    scores(0, c)
                if first:
                    tile(*first)
                for q in range(NT):
                    turn(q, 0)
                    for c in range(j + 1):
                        if c < j:
                            turn(q, c + 1)
                        if q + 1 < NT:
                            scores(q + 1, c)
                        pe.wait_ge(pT_kept[c % 2], FIRST + units_of(c % 2, i, j, q) + c // 2 + 1)
                        if c == 0:
                            pe.wait_ge(t1_made, FIRST + g * NT + q)
                        for t in range(NT):
                            ins = pe.matmul(bank[1][0:TT, 0:C], pT[:, c % 2, t], v[:, NT * c + t],
                                            start=(c == 0 and t == 0), stop=(c == j and t == NT - 1))
                        ins.then_inc(pv_made, 1)
                    if q == 1 and second:
                        tile(*second)

            def experts(i, j, h, s):
                g = i * NJ + j
                pe.wait_ge(xm_made, FIRST + g + 1)
                for t in range(NT):
                    ins = pe.transpose(bank[0][:, t * TT:(t + 1) * TT], xn[:, t, :], ident[0:TT, 0:TT])
                ins.then_inc(xm_turned, 1)
                pe.wait_ge(xmT_kept, FIRST + g + 1)
                for t in range(NT):
                    ins = pe.matmul(bank[2][0:TT, t * NE:(t + 1) * NE], xnT[:, t * TT:(t + 1) * TT], w_rt[:, :],
                                    start=True, stop=True)
                ins.then_inc(route_made, 1)

                def expert(t):
                    for hf in range(2):
                        ins = pe.matmul(bank[EXPERT_BANKS[t % 2][hf]][0:TT, :], xnT[:, t * TT:(t + 1) * TT],
                                        w_ex[:, 4 * hf:4 * hf + 4, :], start=True, stop=True)
                    ins.then_inc(experts_made, 1)

                expert(0)
                expert(1)
                pe.wait_ge(gate_made, FIRST + g + 1)
                for t in range(NT):
                    ins = pe.transpose(bank[0][0:NE, t * TT:(t + 1) * TT], gate[:, t, :], ident[0:TT, 0:TT])
                ins.then_inc(gate_turned, 1)
                pe.wait_ge(gT_kept, FIRST + g + 1)
                for t in range(NT):
                    ins = pe.matmul(bank[3][0:TT, t * C:(t + 1) * C], gT[:, t * TT:(t + 1) * TT], b_ex[:, :],
                                    start=True, stop=True)
                ins.then_inc(bias_made, 1)
                for t in range(2, NT):
                    pe.wait_ge(picked_made, FIRST + g * NT + t - 1)
                    expert(t)

            timeline(pe, tile, attention, experts, front, mlp)


_CONV = ["w_in", "b_in", "dw_w", "dw_b", "bn_g", "bn_b", "bn_m", "bn_v", "w_off", "b_off", "w_msk", "b_msk",
         "w_out", "b_out", "ln1_g", "ln1_b", "w_fc1", "b_fc1", "w_fc2", "b_fc2", "ln2_g", "ln2_b", "gamma1", "gamma2"]
_NAMES = {"L0_conv_" + n: n for n in _CONV}
_NAMES.update({"L1_attn_" + n: n for n in ("Wq", "Wk", "Wv")})
_NAMES.update({"L1_ffn_" + n: n for n in ("router_w", "router_b", "expert_w", "expert_b")})


def shape_constants(n_images):
    import numpy as np
    p = np.arange(TT)
    e = np.arange(GP)
    grid = np.zeros((TT, 2, NT, GP), np.float32)
    grid[:, 0] = (p % IMG)[:, None, None] + (e % P9 // 3)[None, None, :]
    grid[:, 1] = (p // IMG)[:, None, None] + 2 * np.arange(NT)[None, :, None] + (e % P9 % 3)[None, None, :]
    gidx = np.tile((e // P9).astype(np.float32), (TT, NT))
    ioff = np.tile((np.arange(n_images) % TABLES * POS * POS * G).astype(np.float32), (TT, 1))
    causal = np.where(np.arange(3 * TT + CH)[None, :] <= p[:, None] + 3 * TT, 0.0, NEG).astype(np.float32)
    lower = np.tile(np.tril(np.ones((NE, NE), np.float32), -1).reshape(1, -1), (TT, 1))
    return {"ident": np.eye(128, dtype=np.float32), "grid": grid.reshape(TT, -1), "gidx": gidx, "ioff": ioff,
            "causal": causal, "lower": lower}


def kernel(**inputs):
    import numpy as np
    import concourse.bacc as bacc
    from concourse.bass_utils import run_bass_kernel_spmd

    nc = bacc.Bacc("TRN2", target_bir_lowering=False, num_devices=1)
    arrays = {"x": np.ascontiguousarray(inputs["x"])}
    for long, short in _NAMES.items():
        arrays[short] = np.ascontiguousarray(inputs[long])
    consts = shape_constants(arrays["x"].shape[0])
    given = {**arrays, **{"const_" + k: a for k, a in consts.items()}}
    aps = {k: nc.dram_tensor("in_" + k, a.shape, mybir.dt.from_np(a.dtype), kind="ExternalInput").ap()
           for k, a in given.items()}
    out = nc.dram_tensor("out_0", arrays["x"].shape, F32, kind="ExternalOutput").ap()
    build(nc, aps["x"], aps, {k: aps["const_" + k] for k in consts}, out)
    r = run_bass_kernel_spmd(nc, [{"in_" + k: a for k, a in given.items()}], core_ids=[0])
    return r.results[0]["out_0"]
```

```python
from contextlib import ExitStack

import concourse.bass as bass
from concourse import mybir

F32 = mybir.dt.float32
I32 = mybir.dt.int32
U32 = mybir.dt.uint32
ALU = mybir.AluOpType
ACT = mybir.ActivationFunctionType
AX = mybir.AxisListType

C = 128
IMG = 56
PAD = IMG + 2
TOK = IMG * IMG
ROWS = 8
CH = ROWS * IMG
NJ = IMG // ROWS
TT = 112
NT = CH // TT
G = 4
CG = C // G
P9 = 9
GP = G * P9
CORNERS = 4
POS = IMG + 1
BLK = 7
SLOTS2 = 7
TABLES = 3
LEAD = 8
FIRST = 1
PRIMED = 16
RING = 4
HID = 4 * C
NH = HID // C
NE = 8
NEG = -1.0e30
PT_BANKS = (6, 3)
EXPERT_BANKS = (4, 5, 6)
MAGIC = 1597463007.0


class Steps:

    def __init__(self, eng, sem):
        self.eng, self.sem, self.n = eng, sem, 0

    def did(self, ins):
        ins.then_inc(self.sem, 1)
        self.n += 1
        return ins

    def wait(self):
        self.eng.wait_ge(self.sem, self.n)

    def restart(self):
        self.wait()
        self.eng.sem_clear(self.sem)
        self.n = 0


def per_parity(j):
    return (NJ + 1) // 2 if j % 2 == 0 else NJ // 2


def build(nc, x, w, consts, out):
    N = x.shape[0]
    NTOK = N * TOK
    TILES = NTOK // 128
    SLOTS = TILES // BLK
    PAIR_TILES = 2 * TOK // 128
    PAIRS = N // 2
    assert N % 2 == 0 and PAIRS >= 3 and TILES % RING == 0 and TILES == PAIRS * SLOTS2 * BLK

    proj_d = nc.dram_tensor("projected", (2, CH, C), F32).ap()
    table = nc.dram_tensor("corner_table", (TABLES * POS * POS * G, CORNERS * CG), F32).ap()
    idx_d = nc.dram_tensor("corner_index", (NTOK, GP), U32).ap()
    wts_d = nc.dram_tensor("corner_weight", (NTOK, GP * CORNERS), F32).ap()
    tok_d = nc.dram_tensor("tokens", (NTOK, C), F32).ap()

    ctx = ExitStack()

    def sb(name, shape, dt=F32):
        return ctx.enter_context(nc.sbuf_tensor(name, shape, dt))

    def sem(name):
        return ctx.enter_context(nc.semaphore(name))

    with ctx:
        bank = [ctx.enter_context(nc.psum_tensor(f"bank{i}", [128, 512], F32)) for i in range(8)]

        ident = sb("ident", [128, 128])
        diag = sb("diag", [C, P9, C])
        w_in = sb("w_in", [C, C])
        w_om = sb("w_om", [C, 3 * GP])
        w_out = sb("w_out", [C, C])
        w_fc1 = sb("w_fc1", [C, HID])
        w_fc2 = sb("w_fc2", [C, NH, C])
        b_fc1 = sb("b_fc1", [C, NH])
        wq = sb("wq", [C, C])
        wk = sb("wk", [C, C])
        wv = sb("wv", [C, C])
        w_rt = sb("w_rt", [C, NE])
        w_ex = sb("w_ex", [C, NE, C])
        b_ex = sb("b_ex", [NE, C])
        cols = sb("cols", [C, 16])
        dw = sb("dw", [C, P9])
        b_in = sb("b_in", [TT, C])
        b_out = sb("b_out", [128, C])
        b_fc2 = sb("b_fc2", [128, C])
        ln_a = sb("ln_a", [128, 2, C])
        ln_c = sb("ln_c", [128, 2, C])
        b_rt = sb("b_rt", [TT, NE])
        b_om = sb("b_om", [TT, 3 * GP])
        grid = sb("grid", [TT, 2, NT, GP])
        gidx = sb("gidx", [TT, NT * GP])
        ioff = sb("ioff", [TT, N])
        causal = sb("causal", [TT, 3 * TT + CH])
        lower = sb("lower", [TT, NE * NE])

        xin = sb("xin", [TT, 2, NT, C])
        xpad = sb("xpad", [C, PAD, PAD])
        xflat = sb("xflat", [C, 2, CH])
        proj = sb("proj", [TT, 2, NT, C])
        hT = sb("hT", [C, 2, CH])
        idx_s = sb("idx_s", [TT, 2, NT * GP], U32)
        wts_s = sb("wts_s", [TT, 2, NT * GP * CORNERS])

        ring = sb("ring", [128, RING, GP * CORNERS, CG])
        idx_r = sb("idx_r", [128, RING, GP], U32)
        wts_r = sb("wts_r", [128, RING, GP * CORNERS])
        y = sb("y", [128, 2, C])
        yT = sb("yT", [128, 128])
        z = sb("z", [128, BLK, C])
        x1 = sb("x1", [128, BLK, C])

        st = sb("st", [128, BLK, 6])
        mv = sb("mv", [128, BLK, 2])
        nwt = sb("nwt", [128, 6, BLK])
        seed = sb("seed", [128, BLK], I32)

        tin = sb("tin", [TT, 2, NT, C])
        xn = sb("xn", [TT, NT, C])
        xnT = sb("xnT", [C, CH])
        qT = sb("qT", [C, CH])
        kT = sb("kT", [C, NJ, CH])
        v = sb("v", [TT, NJ * NT, C])
        cmax = sb("cmax", [TT, NJ])
        nmax = sb("nmax", [TT, 1])
        rsum = sb("rsum", [TT, 2, NJ])
        rinv = sb("rinv", [TT, 2])
        pT = sb("pT", [TT, 2, NT, TT])
        t1 = sb("t1", [TT, NT, C])
        lg = sb("lg", [TT, NT, NE])
        cmp1 = sb("cmp1", [TT, NT, NE, NE])
        cmp2 = sb("cmp2", [TT, NT, NE, NE])
        rank = sb("rank", [TT, NT * NE])
        gate = sb("gate", [TT, NT, NE])
        sred = sb("sred", [TT, 3, NT])
        gT = sb("gT", [NE, CH])
        o = sb("o", [TT, NT, C])

        arena = sb("arena", [128, 14 * NT * GP + 3 * NT * G + 2 * (NE + 1) * C])
        S = arena[0:TT, 0:NJ * CH].rearrange("p (c n) -> p c n", c=NJ)
        ng = NT * GP
        pos, above, low, frac, my = (
            arena[0:TT, 2 * ng * k:2 * ng * (k + 1)].rearrange("p (a e) -> p a e", a=2) for k in range(5))
        rnd = arena[0:TT, 10 * ng:12 * ng].bitcast(I32).rearrange("p (a e) -> p a e", a=2)
        spot = arena[0:TT, 12 * ng:13 * ng]
        msk = arena[0:TT, 13 * ng:14 * ng]
        mred = arena[0:TT, 14 * ng:14 * ng + 3 * NT * G].rearrange("p (a e) -> p a e", a=3)
        hid = arena[:, 0:NH * 512].rearrange("p (m n) -> p m n", m=NH)
        x1T = arena[:, NH * 512:NH * 512 + BLK * 128]
        gamma = arena[:, 0:2 * C].rearrange("p (k c) -> p k c", k=2)
        x1s = arena[:, NH * 512 + BLK * 128:NH * 512 + 2 * BLK * 128].rearrange("p (k c) -> p k c", k=BLK)
        picked = arena[0:TT, 14 * ng + 3 * NT * G:].rearrange("p (b e c) -> p b e c", b=2, c=C)
        zeros = v[0:POS, 0:G, :].rearrange("p g d -> p (g d)")

        cst_in = sem("cst_in")
        border_out = sem("border_out")
        x_in = [sem(f"x_in{i}") for i in range(2)]
        table_out = [sem(f"table_out{i}") for i in range(2)]
        iw_out = [sem(f"iw_out{i}") for i in range(2)]
        iw_in = sem("iw_in")
        passed = sem("passed")
        table_zeroed = sem("table_zeroed")
        first_in = sem("first_in")
        proj_out = [sem(f"proj_out{i}") for i in range(2)]
        gathered = [sem(f"gathered{i}") for i in range(RING)]
        xb_in = sem("xb_in")
        tok_out = sem("tok_out")
        tok_in = [sem(f"tok_in{i}") for i in range(2)]
        o_out = sem("o_out")
        zeroed = sem("zeroed")
        pad_zeroed = sem("pad_zeroed")
        consts_made = sem("consts_made")
        f_turned = sem("f_turned")
        f_padded = sem("f_padded")
        f_flat = sem("f_flat")
        f_projected = sem("f_projected")
        f_proj_kept = sem("f_proj_kept")
        f_convolved = sem("f_convolved")
        f_hidden = sem("f_hidden")
        f_logits = sem("f_logits")
        f_logits_read = sem("f_logits_read")
        f_mask_shifted = sem("f_mask_shifted")
        f_mask_exp = sem("f_mask_exp")
        f_iw_made = sem("f_iw_made")
        ring_free = sem("ring_free")
        tile_ready = sem("tile_ready")
        tile_begun = sem("tile_begun")
        y_made = sem("y_made")
        y_turned = sem("y_turned")
        yT_kept = sem("yT_kept")
        z_made = sem("z_made")
        z_kept = sem("z_kept")
        x1_made = sem("x1_made")
        x1_turned = sem("x1_turned")
        x1T_kept = sem("x1T_kept")
        fc1_made = sem("fc1_made")
        hid_kept = sem("hid_kept")
        fc2_made = sem("fc2_made")
        m_kept = sem("m_kept")
        x2_made = sem("x2_made")
        xn_made = sem("xn_made")
        xn_turned = sem("xn_turned")
        xnT_kept = sem("xnT_kept")
        qkv_made = sem("qkv_made")
        qkv_kept = sem("qkv_kept")
        s_made = sem("s_made")
        s_copied = sem("s_copied")
        s_masked = sem("s_masked")
        max_made = sem("max_made")
        p_made = sem("p_made")
        p_turned = sem("p_turned")
        pT_kept = [sem(f"pT_kept{i}") for i in range(2)]
        pv_made = sem("pv_made")
        t1_made = sem("t1_made")
        xm_made = sem("xm_made")
        xm_turned = sem("xm_turned")
        xmT_kept = sem("xmT_kept")
        route_made = sem("route_made")
        route_shifted = sem("route_shifted")
        route_exp = sem("route_exp")
        gate_made = sem("gate_made")
        gate_turned = sem("gate_turned")
        bias_made = sem("bias_made")
        picked_made = sem("picked_made")
        gT_kept = sem("gT_kept")
        experts_made = sem("experts_made")
        experts_read = sem("experts_read")
        o_made = sem("o_made")
        dve_steps = sem("dve_steps")

        SC, SH, TMP = 0, 1, 2
        BG, BB, BM, BV, DB = 4, 5, 6, 7, 8

        table_v = table.rearrange("(n y x g) d -> n y x g d", n=TABLES, y=POS, x=POS, g=G)
        x_ch = x.rearrange("n (j t r) w c -> n j (r w) t c", j=NJ, t=NT, r=2)
        x_tok = x.rearrange("n h w c -> (n h w) c")
        idx_ch = idx_d.rearrange("(n j t p) e -> n j p t e", n=N, j=NJ, t=NT)
        wts_ch = wts_d.rearrange("(n j t p) e -> n j p t e", n=N, j=NJ, t=NT)
        idx_t = idx_d.rearrange("(t p) e -> t p e", p=128)
        wts_t = wts_d.rearrange("(t p) e -> t p e", p=128)
        x_slot = x_tok.rearrange("(s k p) c -> s p k c", k=BLK, p=128)
        tok_slot = tok_d.rearrange("(s k p) c -> s p k c", k=BLK, p=128)
        tok_pair = tok_d.rearrange("(s h t p) c -> s h p t c", h=2, t=NT, p=TT)
        out_ch = out.rearrange("n h w c -> (n h w) c").rearrange("(n j t p) c -> n j p t c", n=N, j=NJ, t=NT)

        def column(v_):
            return v_.rearrange("(p a) -> p a", a=1)

        NCONST = [0]
        other_places = table.rearrange("(n y x g) d -> n y x g d", n=TABLES, y=POS, x=POS, g=G)[1:]            .rearrange("n y x g d -> (n y) x (g d)")
        ZERO_STORES = NJ - 1
        STORES = 16 * CORNERS

        def primed(eng, sems):
            for x_ in sems:
                eng.sem_inc(x_, FIRST)

        def units(i, j, q):
            return i * (2 * NJ * (NJ + 1)) + 2 * j * (j + 1) + q * (j + 1)

        def units_below(i, j, q):
            return i * (2 * NJ * (NJ - 1)) + 2 * j * (j - 1) + q * j

        def units_of(par, i, j, q):
            n = [(jj + 2 - par) // 2 for jj in range(NJ)]
            return i * (NT * sum(n)) + NT * sum(n[:j]) + q * n[j]

        def turned_in(i, j):
            if isinstance(i, int) and i == 0:
                return []
            return [0, 1] if j == 0 else [j + 1] if j + 1 < NJ else []

        def turned(p, f):
            i, j = 2 * p + f // NJ, f % NJ
            return i * NJ + (min(j + 1, NJ) if j else 0)

        def timeline(eng, first_image, tile, attention, experts_front, mlp):
            def attended(p, a):
                return 2 * p + a // NJ, a % NJ

            def slots(p):
                fixed = isinstance(p, int)
                for n in range(SLOTS2):
                    s = p * SLOTS2 + n
                    att = not (fixed and p == 0 and n == 0)
                    fronts = [2 * n + LEAD + h for h in range(2)]
                    live = [not (fixed and f + 2 * NJ * p >= N * NJ) for f in fronts]
                    for h in range(2):
                        i, j = attended(p, 2 * (n - 1) + h)
                        first, second, third = ((p, n, 3 * h + k) for k in (1, 2, 3))
                        if att:
                            attention(i, j, h, s, (p, fronts[h]), first, second)
                        else:
                            tile(*first)
                            tile(*second)
                        experts_front((i, j) if att else None, (p, fronts[h]) if live[h] else None, third,
                                      s, i * NJ + j if att else 0)
                    last = fixed and p == PAIRS - 1 and n == SLOTS2 - 1
                    mlp(s, n, last, (p, fronts[1] + 1), i * NJ + j + 1 if att else 0,
                        None if last else (p, n, BLK))

            first_image()
            for f in range(LEAD):
                experts_front(None, (0, f), None, 0, 0)
            tile(0, 0, 0)
            slots(0)
            with eng.Fori(1, PAIRS - 1) as p:
                slots(p)
            slots(PAIRS - 1)
            for h in range(2):
                i, j = attended(PAIRS, h - 2)
                attention(i, j, h, SLOTS, (PAIRS, 0), None, None)
                experts_front((i, j), None, None, SLOTS, i * NJ + j)

        block = ctx.enter_context(nc.Block())

        @block.sync
        def _(sp):
            def const(dst, src, count=None):
                sp.dma_start(dst, src).then_inc(cst_in if count is None else count, 16)
                if count is None:
                    NCONST[0] += 1

            with nc.allow_non_contiguous_dma("constants"):
                for col, name in ((BV, "bn_v"), (BG, "bn_g"), (BB, "bn_b"), (BM, "bn_m"), (DB, "dw_b")):
                    const(cols[:, col:col + 1], column(w[name]), first_in)
                const(dw[:, :], w["dw_w"].rearrange("c a h w -> c (a h w)"), first_in)
                const(ident[:, :], consts["ident"], first_in)
                sp.dma_start(xin[:, 0], x_ch[0, 0]).then_inc(x_in[0], 16)
                sp.dma_start(xin[:, 1], x_ch[0, 1]).then_inc(x_in[1], 16)
                const(w_in[:, :], w["w_in"])
                off_v = w["w_off"].rearrange("c (e a) -> c a e", a=2)
                boff_v = w["b_off"].partition_broadcast(TT).rearrange("p (e a) -> p a e", a=2)
                for a in range(2):
                    const(w_om[:, a * GP:(a + 1) * GP], off_v[:, a, :])
                    const(b_om[:, a * GP:(a + 1) * GP], boff_v[:, a, :])
                const(w_om[:, 2 * GP:], w["w_msk"])
                const(b_om[:, 2 * GP:], w["b_msk"].partition_broadcast(TT))
                const(b_in[:, :], w["b_in"].partition_broadcast(TT))
                const(grid[:, :, :, :], consts["grid"].rearrange("p (a t e) -> p a t e", a=2, t=NT))
                const(ioff[:, :], consts["ioff"])
                const(w_out[:, :], w["w_out"])
                const(w_fc1[:, :], w["w_fc1"])
                const(w_fc2[:, :, :], w["w_fc2"].rearrange("(m p) c -> p m c", p=C))
                const(b_fc1[:, :], w["b_fc1"].rearrange("(m p) -> p m", p=C))
                const(wq[:, :], w["Wq"])
                const(wk[:, :], w["Wk"])
                const(wv[:, :], w["Wv"])
                const(w_rt[:, :], w["router_w"])
                const(w_ex[:, :, :], w["expert_w"].rearrange("e d c -> d e c"))
                const(b_ex[:, :], w["expert_b"])
                for k, (g_, a_, c_) in enumerate((("gamma1", "ln1_g", "ln1_b"), ("gamma2", "ln2_g", "ln2_b"))):
                    const(gamma[:, k, :], w[g_].partition_broadcast(128))
                    const(ln_a[:, k, :], w[a_].partition_broadcast(128))
                    const(ln_c[:, k, :], w[c_].partition_broadcast(128))
                const(causal[:, :], consts["causal"])
                const(lower[:, :], consts["lower"], iw_out[0])
                const(b_rt[:, :], w["router_b"].partition_broadcast(TT), iw_out[1])
                const(b_out[:, :], w["b_out"].partition_broadcast(128), tok_out)
                const(b_fc2[:, :], w["b_fc2"].partition_broadcast(128), o_out)

            sp.wait_ge(zeroed, 1)
            for y0 in (0, POS - 1):
                sp.dma_start(table_v[0, y0].rearrange("x g d -> x (g d)"), zeros).then_inc(border_out, 16)
            for x0 in (0, POS - 1):
                sp.dma_start(table_v[0, 1:POS - 1, x0].rearrange("y g d -> y (g d)"), zeros[0:POS - 2, :])\
                    .then_inc(border_out, 16)
            sp.wait_ge(border_out, 16 * 4)

            def load_x(i, c):
                sp.wait_ge(f_turned, FIRST + i * NJ + max(c - 1, 0))
                sp.sem_inc(passed, 1)
                sp.dma_start(xin[:, c % 2], x_ch[i, c]).then_inc(x_in[c % 2], 16)

            def store_projected(i, c):
                sp.wait_ge(f_proj_kept, FIRST + i * NJ + c + 1)
                sp.sem_inc(passed, 1)
                sp.dma_start(proj_d[c % 2].rearrange("(t p) c -> p t c", p=TT), proj[:, c % 2])\
                    .then_inc(proj_out[c % 2], 16)

            def fill_table(i, c):
                sp.wait_ge(proj_out[c % 2], (i * per_parity(c) + c // 2) * 16 + 16)
                sp.sem_inc(passed, 1)
                for slot in range(CORNERS):
                    y0, x0 = ROWS * c + 1 - slot // 2, 1 - slot % 2
                    sp.dma_start(table_v[i % TABLES, y0:y0 + ROWS, x0:x0 + IMG, :, slot * CG:(slot + 1) * CG]
                                 .rearrange("y x g d -> y (x g) d"),
                                 proj_d[c % 2].rearrange("(y x) (g d) -> y (x g) d", y=ROWS, g=G))\
                        .then_inc(table_out[c % 2], 16)

            def first_image():
                for c in range(NJ):
                    if c >= 2:
                        fill_table(0, c - 2)
                    if c + 2 < NJ:
                        load_x(0, c + 2)
                    store_projected(0, c)
                for c in (NJ - 2, NJ - 1):
                    fill_table(0, c)

            def front(p, f):
                i, j = 2 * p + f // NJ, f % NJ
                i1, fresh = {0: (i, (2, 3)), 1: (i, (4,)), 2: (i, (5,)), 3: (i, (6,)), 5: (i + 1, (0, 1))}\
                    .get(j, (i, ()))
                if not (isinstance(i1, int) and (i1 == 0 or i1 >= N)):
                    for c in fresh:
                        load_x(i1, c)
                if isinstance(i, int) and i == 1 and j == 0:
                    sp.wait_ge(table_zeroed, 16 * ZERO_STORES)
                for c in turned_in(i, j):
                    store_projected(i, c)
                for c in turned_in(i, j):
                    fill_table(i, c)
                if isinstance(i, int) and i == 0 and j < NJ - 1:
                    y0 = j * (TABLES - 1) * POS // (NJ - 1)
                    y1 = (j + 1) * (TABLES - 1) * POS // (NJ - 1)
                    sp.dma_start(other_places[y0:y1].rearrange("y x d -> x y d"),
                                 zeros.unsqueeze(1).broadcast_to([POS, y1 - y0, G * CORNERS * CG]))\
                        .then_inc(table_zeroed, 16)
                sp.wait_ge(f_iw_made, FIRST + i * NJ + j + 1)
                sp.sem_inc(passed, 1)
                sp.dma_start(idx_ch[i, j], idx_s[:, j % 2].rearrange("p (t e) -> p t e", t=NT))\
                    .then_inc(iw_out[j % 2], 16)
                sp.dma_start(wts_ch[i, j], wts_s[:, j % 2].rearrange("p (t e) -> p t e", t=NT))\
                    .then_inc(iw_out[j % 2], 16)
                if isinstance(i, int) and i == 0 and j < 2:
                    if j == 0:
                        for par in range(2):
                            sp.wait_ge(table_out[par], STORES * per_parity(par))
                    sp.wait_ge(iw_out[j], PRIMED + 32)
                    for r in ((0, 1, 2), (3,))[j]:
                        assert (r + 1) * 128 <= (j + 1) * CH
                        ring_load(0, r)
                    if j == 0:
                        sp.dma_start(x1[:, :, :], x_slot[0]).then_inc(xb_in, 16)

            def image_ready(i):
                for par in range(2):
                    sp.wait_ge(table_out[par], (i + 1) * (STORES * per_parity(par)))
                    sp.sem_inc(passed, 1)
                    sp.wait_ge(iw_out[par], PRIMED + (i + 1) * (32 * per_parity(par)))
                    sp.sem_inc(passed, 1)

            def ring_load(p, t):
                r = (p * PAIR_TILES + t) % RING
                sp.wait_ge(ring_free, p * PAIR_TILES + t + 1)
                sp.sem_inc(passed, 1)
                if not (isinstance(p, int) and p * PAIR_TILES + t == 0):
                    sp.wait_ge(iw_in, (p * PAIR_TILES + t) * 32)
                    sp.sem_inc(passed, 1)
                sp.dma_start(idx_r[:, bass.ds(r, 1)].rearrange("p o e -> p (o e)"), idx_t[p * PAIR_TILES + t])\
                    .then_inc(iw_in, 16)
                sp.dma_start(wts_r[:, bass.ds(r, 1)].rearrange("p o e -> p (o e)"), wts_t[p * PAIR_TILES + t])\
                    .then_inc(iw_in, 16)

            def tile(p, n, k):
                t = n * BLK + k + RING
                if isinstance(p, int) and p * PAIR_TILES + t >= TILES:
                    return
                if isinstance(p, int) and p * PAIR_TILES + t == RING:
                    image_ready(0)
                    sp.wait_ge(table_zeroed, 16 * ZERO_STORES)
                if t == PAIR_TILES // 2:
                    image_ready(2 * p + 1)
                if t == PAIR_TILES:
                    image_ready(2 * p + 2)
                ring_load(p, t)

            def attention(i, j, h, s, fronts, first, second):
                if first:
                    tile(*first)
                    tile(*second)

            def mlp(s, n, last, fronts, n_att, between):
                if between:
                    tile(*between)
                sp.wait_ge(x2_made, FIRST + s + 1)
                sp.sem_inc(passed, 1)
                sp.dma_start(tok_slot[s], z[:, :, :]).then_inc(tok_out, 16)
                if not last:
                    sp.dma_start(x1[:, :, :], x_slot[s + 1]).then_inc(xb_in, 16)
                sp.wait_ge(tok_out, PRIMED + s * 16 + 16)
                sp.sem_inc(passed, 1)
                for h in range(2):
                    if not (isinstance(s, int) and s == 0):
                        sp.wait_ge(t1_made, FIRST + s * (2 * NT) + NT * (h - 1))
                        sp.sem_inc(passed, 1)
                    sp.dma_start(tin[:, h], tok_pair[s, h]).then_inc(tok_in[h], 16)

            def experts_front(unit, ahead, third, s, n_att):
                if ahead:
                    front(*ahead)
                if third:
                    tile(*third)
                if unit:
                    i, j = unit
                    sp.wait_ge(o_made, FIRST + i * NJ + j + 1)
                    sp.sem_inc(passed, 1)
                    sp.dma_start(out_ch[i, j], o[:, :, :]).then_inc(o_out, 16)

            timeline(sp, first_image, tile, attention, experts_front, mlp)
            sp.wait_ge(o_out, PRIMED + 16 * N * NJ)

        @block.gpsimd
        def _(pool):
            pool.memset(zeros, 0.0).then_inc(zeroed, 1)
            pool.dma_start(gidx[:, :], consts["gidx"]).then_inc(gathered[RING - 1], 16)

            def fill_ring(q, source):
                for r in range(RING):
                    pool.wait_ge(iw_in, q * (RING * 32) + (r + 1) * 32)
                    pool.sem_inc(tile_begun, 1)
                    for e in range(GP):
                        pool.indirect_dma_start(
                            ring[:, r, e * CORNERS:(e + 1) * CORNERS, :].rearrange("p s c -> p (s c)"), None,
                            source, bass.IndirectOffsetOnAxis(ap=idx_r[:, r, e:e + 1], axis=0),
                        ).then_inc(gathered[r], 16)
                        if e == 5:
                            if r:
                                pool.wait_ge(gathered[r - 1], q * (16 * GP) + 16 * GP)
                            else:
                                pool.wait_ge(gathered[RING - 1], q * (16 * GP) + PRIMED)
                            pool.sem_inc(tile_ready, 1)

            fill_ring(0, table[0:POS * POS * G])
            with pool.Fori(1, TILES // RING) as q:
                fill_ring(q, table)
            pool.wait_ge(gathered[RING - 1], 16 * GP * (TILES // RING) + PRIMED)
            pool.sem_inc(tile_ready, 1)

        @block.scalar
        def _(act):
            primed(act, (f_padded, f_hidden, f_mask_exp, yT_kept, x1T_kept, hid_kept, xnT_kept, qkv_kept, s_copied,
                         p_made, pT_kept[0], xmT_kept, route_exp, gT_kept, picked_made))
            act.wait_ge(pad_zeroed, 1)

            def tile(p, n, k):
                if k % BLK:
                    turned_tile(p * PAIR_TILES + n * BLK + k - 1)

            def turned_tile(t):
                act.wait_ge(y_turned, FIRST + t + 1)
                act.activation(yT[:, :], bank[7][:, 0:128], ACT.Copy).then_inc(yT_kept, 1)

            def mlp(s, n, last, fronts, n_att, between):
                turned_tile(s * BLK + BLK - 1)
                for half, (k0, k1) in enumerate(((0, 4), (4, BLK))):
                    act.wait_ge(x1_turned, FIRST + s * 2 + half + 1)
                    act.activation(x1T[:, k0 * 128:k1 * 128], bank[half][:, 0:(k1 - k0) * 128], ACT.Copy)\
                        .then_inc(x1T_kept, 1)
                for half, (k0, k1) in enumerate(((0, 4), (4, BLK))):
                    cols_ = (k1 - k0) * 128
                    act.wait_ge(fc2_made, FIRST + s * 2 + half)
                    for c in range(NH):
                        act.wait_ge(fc1_made, FIRST + s * (2 * NH) + half * NH + c + 1)
                        act.activation(hid[:, c, 0:cols_], bank[2 + c % 2][:, 0:cols_], ACT.Gelu,
                                       bias=b_fc1[:, c:c + 1]).then_inc(hid_kept, 1)

            def attention(i, j, h, s, fronts, first, second):
                g = i * NJ + j
                act.wait_ge(xn_turned, FIRST + g + 1)
                act.activation(xnT[:, :], bank[0][:, 0:CH], ACT.Copy).then_inc(xnT_kept, 1)
                act.wait_ge(qkv_made, FIRST + g * 3 + 1)
                act.activation(qT[:, :], bank[1][:, 0:CH], ACT.Copy, scale=float(C) ** -0.5).then_inc(qkv_kept, 1)
                act.wait_ge(qkv_made, FIRST + g * 3 + 2)
                if j == 0:
                    act.wait_ge(pv_made, FIRST + units(i, 0, 0))
                act.activation(kT[:, j], bank[2][:, 0:CH], ACT.Copy).then_inc(qkv_kept, 1)
                act.wait_ge(qkv_made, FIRST + g * 3 + 3)
                act.activation(v[:, NT * j:NT * (j + 1), :],
                               bank[3][0:TT, :].rearrange("p (t c) -> p t c", t=NT), ACT.Copy)\
                    .then_inc(qkv_kept, 1)

                def keep_scores(q, c):
                    u0 = units(i, j, q)
                    act.wait_ge(s_made, FIRST + u0 + c + 1)
                    act.wait_ge(p_turned, FIRST + (units(i, j, q - 1) + c + 1 if q else u0))
                    act.activation(S[:, c], bank[4 + c % 2][0:TT, 0:CH], ACT.Copy).then_inc(s_copied, 1)

                for c in range(j):
                    keep_scores(0, c)
                if first:
                    tile(*first)
                for q in range(NT):
                    u0, e0, qg = units(i, j, q), units_of(0, i, j, q), g * NT + q
                    act.wait_ge(max_made, FIRST + qg + 1)
                    act.wait_ge(s_copied, FIRST + units_below(i, j, q) + j)
                    if q >= 2:
                        act.wait_ge(t1_made, FIRST + qg - 1)

                    def exponentials(c):
                        act.activation(S[:, c], S[:, c], ACT.Exp, bias=nmax[:, 0:1],
                                       accum_out=rsum[:, q % 2, c:c + 1]).then_inc(p_made, 1)

                    for c in range(min(2, j + 1)):
                        exponentials(c)
                    for c in range(j + 1):
                        if c % 2 == 0:
                            act.wait_ge(p_turned, FIRST + u0 + c + 1)
                            act.wait_ge(pv_made, FIRST + u0 + max(c - 1, 0))
                            act.activation(pT[:, 0], bank[6][0:TT, 0:CH].rearrange("p (t k) -> p t k", t=NT),
                                           ACT.Copy).then_inc(pT_kept[0], 1)
                        if c + 2 <= j:
                            exponentials(c + 2)
                        if q + 1 < NT and c < j:
                            keep_scores(q + 1, c)
                    if q == 1 and second:
                        tile(*second)

            def keep_turned(i, c):
                act.wait_ge(f_turned, FIRST + i * NJ + c + 1)
                act.activation(xpad[:, 1 + ROWS * c:1 + ROWS * (c + 1), 1:1 + IMG],
                               bank[1][:, 0:CH].rearrange("c (h w) -> c h w", w=IMG), ACT.Copy)\
                    .then_inc(f_padded, 1)

            def first_image():
                for c in range(NJ):
                    keep_turned(0, c)

            def experts_front(unit, ahead, third, s, n_att):
                if ahead:
                    p, f = ahead
                    fi, fj = 2 * p + f // NJ, f % NJ
                    for c in turned_in(fi, fj):
                        if c == 0:
                            act.wait_ge(f_convolved, FIRST + fi * NJ)
                            act.wait_ge(f_flat, FIRST + fi * NJ)
                        keep_turned(fi, c)
                    act.wait_ge(f_convolved, FIRST + fi * NJ + fj + 1)
                    act.wait_ge(f_logits, FIRST + fi * NJ + max(fj - 1, 0))
                    act.activation(hT[:, fj % 2], bank[1][:, 0:CH], ACT.Gelu,
                                   bias=cols[:, SH:SH + 1], scale=cols[:, SC:SC + 1]).then_inc(f_hidden, 1)
                if unit:
                    i, j = unit
                    g = i * NJ + j
                    act.wait_ge(xm_turned, FIRST + g + 1)
                    act.activation(xnT[:, :], bank[0][:, 0:CH], ACT.Copy).then_inc(xmT_kept, 1)
                if third:
                    tile(*third)
                if ahead:
                    act.wait_ge(f_mask_shifted, FIRST + fi * NJ + fj + 1)
                    act.activation(msk, msk, ACT.Exp).then_inc(f_mask_exp, 1)
                if unit:
                    act.wait_ge(route_shifted, FIRST + g + 1)
                    act.activation(lg[:, :, :], lg[:, :, :], ACT.Exp).then_inc(route_exp, 1)
                    act.wait_ge(gate_made, FIRST + g + 1)
                    for m in range(2 * NT):
                        t, half = m // 2, m % 2
                        if m == 2:
                            act.wait_ge(gate_turned, FIRST + g + 1)
                            act.activation(gT[:, :], bank[0][0:NE, 0:CH], ACT.Copy).then_inc(gT_kept, 1)
                        act.wait_ge(experts_made, FIRST + g * (2 * NT) + m + 1)
                        if half == 0:
                            act.wait_ge(experts_read, FIRST + g * NT + max(t - 1, 0))
                        for e in range(4):
                            ins = act.activation(
                                picked[:, t % 2, 4 * half + e], bank[EXPERT_BANKS[m % 3]][0:TT, e * C:(e + 1) * C],
                                ACT.Copy, scale=gate[:, t, 4 * half + e:4 * half + e + 1])
                        ins.then_inc(picked_made, 1)

            timeline(act, first_image, tile, attention, experts_front, mlp)

        @block.vector
        def _(dve):
            step = Steps(dve, dve_steps)
            primed(dve, (f_flat, f_proj_kept, f_logits_read, f_mask_shifted, f_iw_made, y_made, z_kept, x1_made,
                         m_kept, x2_made, xn_made, s_masked, max_made, pT_kept[1], t1_made, xm_made, route_shifted,
                         gate_made, experts_read, o_made))

            def rsqrt(val, n, p, eps, scratch):
                ve, half, y_, a_, b_ = (scratch[0:p, k, 0:n] for k in range(5))
                step.did(dve.tensor_scalar(ve, val, eps, None, ALU.add))
                step.wait()
                step.did(dve.tensor_scalar(half, ve, -0.5, None, ALU.mult))
                step.did(dve.tensor_scalar(seed[0:p, 0:n], ve.bitcast(I32), -0.5, MAGIC, ALU.mult, ALU.add))
                step.wait()
                cur = seed[0:p, 0:n].bitcast(F32)
                for _ in range(3):
                    step.did(dve.tensor_tensor(a_, cur, cur, ALU.mult))
                    step.wait()
                    step.did(dve.tensor_tensor(b_, a_, half, ALU.mult))
                    step.wait()
                    step.did(dve.scalar_tensor_tensor(y_, b_, 1.5, cur, ALU.add, ALU.mult))
                    step.wait()
                    cur = y_
                return y_

            def layer_norm(src, dst, n, p, eps):
                for k in range(n):
                    step.did(dve.bn_stats(st[0:p, k, :], src[:, k, :]))
                step.wait()
                for k in range(n):
                    step.did(dve.bn_aggr(mv[0:p, k, :], st[0:p, k, :]))
                step.wait()
                r = rsqrt(mv[0:p, 0:n, 1], n, p, eps, nwt)
                for k in range(n - 1):
                    step.did(dve.tensor_scalar(dst[:, k, :], src[:, k, :], mv[0:p, k, 0:1], r[:, k:k + 1],
                                               ALU.subtract, ALU.mult))
                return dve.tensor_scalar(dst[:, n - 1, :], src[:, n - 1, :], mv[0:p, n - 1, 0:1], r[:, n - 1:n],
                                         ALU.subtract, ALU.mult)

            dve.memset(xpad[:, :, :], 0.0).then_inc(pad_zeroed, 1)
            dve.wait_ge(first_in, 16 * 7)
            r = rsqrt(cols[:, BV:BV + 1], 1, C, 1e-5, nwt)
            step.did(dve.tensor_tensor(cols[:, SC:SC + 1], cols[:, BG:BG + 1], r, ALU.mult))
            step.did(dve.tensor_tensor(cols[:, TMP:TMP + 1], cols[:, DB:DB + 1], cols[:, BM:BM + 1], ALU.subtract))
            step.wait()
            step.did(dve.scalar_tensor_tensor(cols[:, SH:SH + 1], cols[:, TMP:TMP + 1], cols[:, SC:SC + 1],
                                              cols[:, BB:BB + 1], ALU.mult, ALU.add))
            for k in range(P9):
                step.did(dve.tensor_scalar(diag[:, k, :], ident[:, :], dw[:, k:k + 1], None, ALU.mult))
            step.wait()
            dve.sem_inc(consts_made, 1)
            dve.wait_ge(cst_in, 16 * NCONST[0])
            for x_ in (iw_out[0], iw_out[1], tok_out, o_out, gathered[RING - 1]):
                dve.wait_ge(x_, PRIMED)
            step.did(dve.tensor_tensor(ln_a[:, :, :], ln_a[:, :, :], gamma[:, :, :], ALU.mult))
            step.did(dve.tensor_tensor(ln_c[:, :, :], ln_c[:, :, :], gamma[:, :, :], ALU.mult))
            for a in range(2):
                step.did(dve.tensor_tensor(grid[:, a], grid[:, a],
                                           b_om[:, a * GP:(a + 1) * GP].unsqueeze(1).broadcast_to([TT, NT, GP]),
                                           ALU.add))
            step.restart()
            dve.sem_inc(ring_free, RING)
            dve.sem_inc(consts_made, 1)

            def keep_z(t, k):
                dve.wait_ge(z_made, FIRST + t + 1)
                dve.tensor_tensor(z[:, k, :], bank[7][:, 128:128 + C], b_out[:, :], ALU.add).then_inc(z_kept, 1)

            def multiply(p, n, k):
                t = p * PAIR_TILES + n * BLK + k
                r = t % RING
                dve.wait_ge(tile_ready, t + 2)
                dve.wait_ge(y_turned, FIRST + t - (1 if k % BLK else 0))
                corners = ring[:, bass.ds(r, 1)].rearrange("p o e c -> p (o e) c")
                step.did(dve.tensor_tensor(
                    corners, corners,
                    wts_r[:, bass.ds(r, 1)].rearrange("p o e -> p (o e)").unsqueeze(2)
                    .broadcast_to([128, GP * CORNERS, CG]), ALU.mult))

            def sum_up(p, n, k):
                t = p * PAIR_TILES + n * BLK + k
                step.restart()
                dve.tensor_reduce(
                    y[:, k % BLK % 2].rearrange("p (g c) -> p g c", g=G),
                    ring[:, bass.ds(t % RING, 1)].rearrange("p o (g e) c -> p (o g) c e", g=G), AX.X, ALU.add)\
                    .then_inc(y_made, 1)
                if k % BLK:
                    keep_z(t - 1, k - 1)
                dve.wait_ge(y_made, FIRST + t + 1)
                dve.sem_inc(ring_free, 1)

            def tile(p, n, k):
                multiply(p, n, k)
                sum_up(p, n, k)

            def mlp(s, n, last, fronts, n_att, between):
                def shifted(k_):
                    return dve.tensor_tensor(x1s[:, :, :], x1[:, :, :],
                                             ln_c[:, k_].unsqueeze(1).broadcast_to([128, BLK, C]), ALU.add)

                def normed_and_added(dst, k_):
                    for k in range(BLK):
                        step.did(dve.bn_stats(st[:, k, :], z[:, k, :]))
                    step.wait()
                    for k in range(BLK):
                        step.did(dve.bn_aggr(mv[:, k, :], st[:, k, :]))
                    step.wait()
                    for k in range(BLK):
                        step.did(dve.scalar_tensor_tensor(z[:, k, :], z[:, k, :], mv[:, k, 0:1], ln_a[:, k_],
                                                          ALU.subtract, ALU.mult))
                    r = rsqrt(mv[:, 0:BLK, 1], BLK, 128, 1e-5, nwt)
                    for k in range(BLK):
                        ins = dve.scalar_tensor_tensor(dst[:, k, :], z[:, k, :], r[:, k:k + 1], x1s[:, k, :],
                                                       ALU.mult, ALU.add)
                        if k < BLK - 1:
                            step.did(ins)
                    return ins

                dve.wait_ge(xb_in, s * 16 + 16)
                step.did(shifted(0))
                keep_z(s * BLK + BLK - 1, BLK - 1)
                dve.wait_ge(z_kept, FIRST + s * BLK + BLK)
                normed_and_added(x1, 0).then_inc(x1_made, 1)
                dve.wait_ge(x1_made, FIRST + s + 1)
                step.did(shifted(1))
                if between:
                    tile(*between)
                for half, (k0, k1) in enumerate(((0, 4), (4, BLK))):
                    dve.wait_ge(fc2_made, FIRST + s * 2 + half + 1)
                    dve.tensor_tensor(z[:, k0:k1, :],
                                      bank[4 + half][:, 0:(k1 - k0) * C].rearrange("p (k c) -> p k c", c=C),
                                      b_fc2[:, :].unsqueeze(1).broadcast_to([128, k1 - k0, C]), ALU.add)\
                        .then_inc(m_kept, 1)
                dve.wait_ge(m_kept, FIRST + s * 2 + 2)
                normed_and_added(z, 1).then_inc(x2_made, 1)
                step.restart()
                dve.wait_ge(tok_out, PRIMED + s * 16 + 16)

            def attention(i, j, h, s, fronts, first, second):
                g = i * NJ + j
                if first and h == 0:
                    multiply(*first)
                dve.wait_ge(tok_in[h], s * 16)
                dve.wait_ge(xm_turned, FIRST + g)
                layer_norm(tin[:, h], xn, NT, TT, 1e-5).then_inc(xn_made, 1)
                if first:
                    if h:
                        multiply(*first)
                    sum_up(*first)

                def chunk_max(q, c):
                    u0 = units(i, j, q)
                    if c < j:
                        dve.wait_ge(s_copied, FIRST + units_below(i, j, q) + c + 1)
                    else:
                        dve.wait_ge(s_made, FIRST + u0 + j + 1)
                        dve.wait_ge(p_turned, FIRST + u0)
                        dve.tensor_tensor(S[:, j], bank[4 + j % 2][0:TT, 0:CH],
                                          causal[:, (NT - 1 - q) * TT:(NT - 1 - q) * TT + CH], ALU.add)\
                            .then_inc(s_masked, 1)
                        dve.wait_ge(s_masked, FIRST + g * NT + q + 1)
                    step.did(dve.tensor_reduce(cmax[:, c:c + 1], S[:, c], AX.X, ALU.max))

                def row_max(q):
                    step.wait()
                    dve.wait_ge(p_made, FIRST + units(i, j, q))
                    dve.tensor_reduce(nmax[:, 0:1], cmax[:, 0:j + 1], AX.X, ALU.max, negate=True)\
                        .then_inc(max_made, 1)
                    dve.wait_ge(max_made, FIRST + g * NT + q + 1)

                for c in range(j + 1):
                    chunk_max(0, c)
                row_max(0)
                for q in range(NT):
                    u0 = units(i, j, q)
                    for c in range(j + 1):
                        if c % 2:
                            dve.wait_ge(p_turned, FIRST + u0 + c + 1)
                            dve.wait_ge(pv_made, FIRST + u0 + c - 1)
                            dve.tensor_copy(pT[:, 1], bank[3][0:TT, 0:CH].rearrange("p (t k) -> p t k", t=NT))\
                                .then_inc(pT_kept[1], 1)
                        if q + 1 < NT:
                            chunk_max(q + 1, c)
                    if q + 1 < NT:
                        row_max(q + 1)
                    dve.wait_ge(p_made, FIRST + u0 + j + 1)
                    step.did(dve.tensor_reduce(rinv[:, 0:1], rsum[:, q % 2, 0:j + 1], AX.X, ALU.add))
                    step.wait()
                    step.did(dve.reciprocal(rinv[:, 1:2], rinv[:, 0:1]))
                    step.wait()
                    dve.wait_ge(pv_made, FIRST + u0 + j + 1)
                    dve.scalar_tensor_tensor(t1[:, q, :], bank[1][0:TT, 0:C], rinv[:, 1:2], tin[:, h, q, :],
                                             ALU.mult, ALU.add).then_inc(t1_made, 1)
                    if second and q == 0:
                        multiply(*second)
                    if second and q == 1:
                        sum_up(*second)
                step.restart()

            def flatten(i, c):
                dve.wait_ge(f_padded, FIRST + i * NJ + c + 1)
                dve.wait_ge(f_projected, FIRST + i * NJ + max(c - 1, 0))
                dve.tensor_copy(xflat[:, c % 2].rearrange("c (h w) -> c h w", w=IMG),
                                xpad[:, 1 + ROWS * c:1 + ROWS * (c + 1), 1:1 + IMG]).then_inc(f_flat, 1)

            def keep_projected(i, c):
                dve.wait_ge(f_projected, FIRST + i * NJ + c + 1)
                if not (isinstance(i, int) and i == 0 and c < 2):
                    dve.wait_ge(table_out[c % 2], (i * per_parity(c) + c // 2) * STORES)
                dve.tensor_tensor(proj[:, c % 2], bank[3][0:TT, :].rearrange("p (t c) -> p t c", t=NT),
                                  b_in[:, :].unsqueeze(1).broadcast_to([TT, NT, C]), ALU.add)\
                    .then_inc(f_proj_kept, 1)

            def first_image():
                flatten(0, 0)
                for c in range(NJ):
                    if c + 1 < NJ:
                        flatten(0, c + 1)
                    keep_projected(0, c)

            def front_positions(i, j):
                lt = bank[0][0:TT, :].rearrange("p (t e) -> p t e", t=NT)
                by_group = msk.rearrange("p (g e) -> p g e", e=P9)
                dve.wait_ge(f_logits, FIRST + i * NJ + j + 1)
                for a in range(2):
                    step.did(dve.tensor_tensor(pos[:, a].rearrange("p (t e) -> p t e", t=NT),
                                               lt[:, :, a * GP:(a + 1) * GP], grid[:, a], ALU.add))
                dve.tensor_tensor(msk.rearrange("p (t e) -> p t e", t=NT), lt[:, :, 2 * GP:3 * GP],
                                  b_om[:, 2 * GP:].unsqueeze(1).broadcast_to([TT, NT, GP]), ALU.add)\
                    .then_inc(f_logits_read, 1)
                step.wait()
                dve.wait_ge(f_logits_read, FIRST + i * NJ + j + 1)
                step.did(dve.tensor_reduce(mred[:, 0], by_group, AX.X, ALU.max))
                step.did(dve.tensor_scalar(pos[:, 1], pos[:, 1], float(ROWS * j), None, ALU.add))
                step.wait()
                dve.tensor_tensor(by_group, by_group, mred[:, 0].unsqueeze(2).broadcast_to([TT, NT * G, P9]),
                                  ALU.subtract).then_inc(f_mask_shifted, 1)
                step.did(dve.tensor_scalar(pos, pos, 0.0, float(IMG + 1), ALU.max, ALU.min))
                step.wait()
                step.did(dve.tensor_copy(rnd, pos))
                step.wait()
                step.did(dve.tensor_tensor(above, rnd, pos, ALU.is_gt))
                step.wait()
                step.did(dve.tensor_tensor(low, rnd, above, ALU.subtract))
                step.wait()
                step.did(dve.tensor_scalar(low, low, float(IMG), None, ALU.min))
                step.wait()
                step.did(dve.tensor_tensor(frac, pos, low, ALU.subtract))
                step.did(dve.scalar_tensor_tensor(spot, low[:, 1], float(POS), low[:, 0], ALU.mult, ALU.add))
                step.wait()
                step.did(dve.scalar_tensor_tensor(spot, spot, float(G), gidx[:, :], ALU.mult, ALU.add))
                step.wait()
                dve.wait_ge(iw_out[j % 2], PRIMED + (i * per_parity(j) + j // 2) * 32)
                step.did(dve.tensor_scalar(idx_s[:, j % 2], spot, ioff[:, bass.ds(i, 1)], None, ALU.add))

            def front_weights(i, j):
                by_group = msk.rearrange("p (g e) -> p g e", e=P9)
                dve.wait_ge(f_mask_exp, FIRST + i * NJ + j + 1)
                step.did(dve.tensor_reduce(mred[:, 1], by_group, AX.X, ALU.add))
                step.wait()
                step.did(dve.reciprocal(mred[:, 2], mred[:, 1]))
                step.wait()
                step.did(dve.tensor_tensor(by_group, by_group,
                                           mred[:, 2].unsqueeze(2).broadcast_to([TT, NT * G, P9]), ALU.mult))
                step.wait()
                step.did(dve.tensor_tensor(my[:, 1], msk, frac[:, 1], ALU.mult))
                step.wait()
                step.did(dve.tensor_tensor(my[:, 0], msk, my[:, 1], ALU.subtract))
                step.wait()
                corner = wts_s[:, j % 2].rearrange("p (e y x) -> p y x e", y=2, x=2)
                for dy in range(2):
                    step.did(dve.tensor_tensor(corner[:, dy, 1], my[:, dy], frac[:, 0], ALU.mult))
                step.wait()
                for dy in range(2):
                    step.did(dve.tensor_tensor(corner[:, dy, 0], my[:, dy], corner[:, dy, 1], ALU.subtract))
                step.restart()
                dve.sem_inc(f_iw_made, 1)

            def route(g):
                dve.wait_ge(route_made, FIRST + g + 1)
                step.did(dve.tensor_tensor(
                    lg[:, :, :], bank[2][0:TT, 0:NT * NE].rearrange("p (t e) -> p t e", e=NE),
                    b_rt[:, :].unsqueeze(1).broadcast_to([TT, NT, NE]), ALU.add))
                step.wait()
                step.did(dve.tensor_reduce(sred[:, 0], lg[:, :, :], AX.X, ALU.max))
                step.wait()
                dve.tensor_tensor(lg[:, :, :], lg[:, :, :],
                                  sred[:, 0].unsqueeze(2).broadcast_to([TT, NT, NE]), ALU.subtract)\
                    .then_inc(route_shifted, 1)
                dve.wait_ge(route_exp, FIRST + g + 1)
                other = lg[:, :, :].unsqueeze(2).broadcast_to([TT, NT, NE, NE])
                own = lg[:, :, :].unsqueeze(3).broadcast_to([TT, NT, NE, NE])
                step.did(dve.tensor_tensor(cmp1[:, :, :, :], other, own, ALU.is_gt))
                step.did(dve.tensor_tensor(cmp2[:, :, :, :], other, own, ALU.is_equal))
                step.wait()
                step.did(dve.tensor_tensor(
                    cmp2[:, :, :, :].rearrange("p t a b -> p t (a b)"),
                    cmp2[:, :, :, :].rearrange("p t a b -> p t (a b)"),
                    lower[:, :].unsqueeze(1).broadcast_to([TT, NT, NE * NE]), ALU.mult))
                step.wait()
                step.did(dve.tensor_tensor(cmp1[:, :, :, :], cmp1[:, :, :, :], cmp2[:, :, :, :], ALU.add))
                step.wait()
                step.did(dve.tensor_reduce(rank[:, :].rearrange("p (t e) -> p t e", e=NE), cmp1[:, :, :, :],
                                           AX.X, ALU.add))
                step.wait()
                step.did(dve.scalar_tensor_tensor(
                    gate[:, :, :].rearrange("p t e -> p (t e)"), rank[:, :], 2.0,
                    lg[:, :, :].rearrange("p t e -> p (t e)"), ALU.is_lt, ALU.mult))
                step.wait()
                step.did(dve.tensor_reduce(sred[:, 1], gate[:, :, :], AX.X, ALU.add))
                step.wait()
                step.did(dve.reciprocal(sred[:, 2], sred[:, 1]))
                step.wait()
                dve.tensor_tensor(gate[:, :, :], gate[:, :, :],
                                  sred[:, 2].unsqueeze(2).broadcast_to([TT, NT, NE]), ALU.mult)\
                    .then_inc(gate_made, 1)

            def add_experts(g):
                dve.wait_ge(o_out, PRIMED + g * 16)
                dve.wait_ge(bias_made, FIRST + g + 1)
                for t in range(NT):
                    step.did(dve.tensor_tensor(picked[:, t % 2, NE], bank[2][0:TT, t * C:(t + 1) * C],
                                               t1[:, t, :], ALU.add))
                    step.wait()
                    dve.wait_ge(picked_made, FIRST + g * (2 * NT) + 2 * t + 2)
                    dve.tensor_reduce(o[:, t, :], picked[:, t % 2].rearrange("p e c -> p c e"), AX.X, ALU.add)\
                        .then_inc(experts_read, 1)
                dve.wait_ge(experts_read, FIRST + g * NT + NT)
                dve.sem_inc(o_made, 1)

            def experts_front(unit, ahead, third, s, n_att):
                if unit:
                    i, j = unit
                    g = i * NJ + j
                    dve.wait_ge(t1_made, FIRST + g * NT + NT)
                    dve.wait_ge(xn_turned, FIRST + g + 1)
                    layer_norm(t1, xn, NT, TT, 1e-5).then_inc(xm_made, 1)
                if ahead:
                    p, f = ahead
                    fi, fj = 2 * p + f // NJ, f % NJ
                    for c in turned_in(fi, fj):
                        flatten(fi, c)
                if third:
                    multiply(*third)
                if ahead:
                    for c in turned_in(fi, fj):
                        keep_projected(fi, c)
                    front_positions(fi, fj)
                if unit:
                    route(g)
                if third:
                    sum_up(*third)
                if ahead:
                    front_weights(fi, fj)
                if unit:
                    add_experts(g)
                step.restart()

            timeline(dve, first_image, tile, attention, experts_front, mlp)

        @block.tensor
        def _(pe):
            primed(pe, (f_turned, f_projected, f_convolved, f_logits, y_turned, z_made, x1_turned, fc1_made,
                        fc2_made, xn_turned, qkv_made, s_made, p_turned, pv_made, xm_turned, route_made,
                        gate_turned, bias_made, experts_made))
            pe.wait_ge(consts_made, 1)

            def banks_left(fronts, n_mlp, n_att):
                p, f = fronts
                if isinstance(p, int) and 2 * NJ * p + f > N * NJ:
                    p, f = PAIRS, 0
                pe.wait_ge(f_proj_kept, FIRST + turned(p, f))
                pe.wait_ge(f_logits_read, FIRST + p * (2 * NJ) + f)
                pe.wait_ge(m_kept, FIRST + n_mlp * 2)
                pe.wait_ge(experts_read, FIRST + n_att * NT)

            def tile(p, n, k):
                if k % BLK:
                    project(p * PAIR_TILES + n * BLK + k - 1, k - 1)

            def project(t, k):
                pe.wait_ge(y_made, FIRST + t + 1)
                pe.wait_ge(z_kept, FIRST + t)
                pe.transpose(bank[7][:, 0:128], y[:, k % 2], ident[:, :]).then_inc(y_turned, 1)
                pe.wait_ge(yT_kept, FIRST + t + 1)
                pe.matmul(bank[7][:, 128:128 + C], yT[:, :], w_out[:, :], start=True, stop=True).then_inc(z_made, 1)

            def mlp(s, n, last, fronts, n_att, between):
                project(s * BLK + BLK - 1, BLK - 1)
                banks_left(fronts, s, n_att)
                pe.wait_ge(x1_made, FIRST + s + 1)
                halves = ((0, 4), (4, BLK))
                for half, (k0, k1) in enumerate(halves):
                    for k in range(k0, k1):
                        ins = pe.transpose(bank[half][:, (k - k0) * 128:(k - k0 + 1) * 128], x1[:, k, :], ident[:, :])
                    ins.then_inc(x1_turned, 1)
                for half, (k0, k1) in enumerate(halves):
                    pe.wait_ge(x1T_kept, FIRST + s * 2 + half + 1)
                    for c in range(NH):
                        pe.wait_ge(hid_kept, FIRST + s * (2 * NH) + max(half * NH + c - 1, 0))
                        pe.matmul(bank[2 + c % 2][:, 0:(k1 - k0) * 128], w_fc1[:, c * C:(c + 1) * C],
                                  x1T[:, k0 * 128:k1 * 128], start=True, stop=True).then_inc(fc1_made, 1)
                    pe.wait_ge(hid_kept, FIRST + s * (2 * NH) + (half + 1) * NH)
                    for k in range(k0, k1):
                        for c in range(NH):
                            ins = pe.matmul(bank[4 + half][:, (k - k0) * C:(k - k0 + 1) * C],
                                            hid[:, c, (k - k0) * 128:(k - k0 + 1) * 128], w_fc2[:, c, :],
                                            start=(c == 0), stop=(c == NH - 1))
                    ins.then_inc(fc2_made, 1)

            def attention(i, j, h, s, fronts, first, second):
                g = i * NJ + j
                banks_left(fronts, s, g)
                pe.wait_ge(xn_made, FIRST + g + 1)
                for t in range(NT):
                    ins = pe.transpose(bank[0][:, t * TT:(t + 1) * TT], xn[:, t, :], ident[0:TT, 0:TT])
                ins.then_inc(xn_turned, 1)
                pe.wait_ge(xnT_kept, FIRST + g + 1)
                pe.matmul(bank[1][:, 0:CH], wq[:, :], xnT[:, :], start=True, stop=True).then_inc(qkv_made, 1)
                pe.matmul(bank[2][:, 0:CH], wk[:, :], xnT[:, :], start=True, stop=True).then_inc(qkv_made, 1)
                for t in range(NT):
                    ins = pe.matmul(bank[3][0:TT, t * C:(t + 1) * C], xnT[:, t * TT:(t + 1) * TT], wv[:, :],
                                    start=True, stop=True)
                ins.then_inc(qkv_made, 1)

                def scores(q, c):
                    if q == 0 and c in (0, j):
                        pe.wait_ge(qkv_kept, FIRST + g * 3 + (3 if c == j else 1))
                    if c < 2:
                        pe.wait_ge(s_masked, FIRST + g * NT + q)
                    if j:
                        pe.wait_ge(s_copied, FIRST + units_below(i, j, q) + max(c - 1, 0))
                    pe.matmul(bank[4 + c % 2][0:TT, 0:CH], qT[:, q * TT:(q + 1) * TT], kT[:, c],
                              start=True, stop=True).then_inc(s_made, 1)

                def turn(q, c):
                    pe.wait_ge(p_made, FIRST + units(i, j, q) + c + 1)
                    pe.wait_ge(pT_kept[c % 2], FIRST + units_of(c % 2, i, j, q) + c // 2)
                    for t in range(NT):
                        ins = pe.transpose(bank[PT_BANKS[c % 2]][0:TT, t * TT:(t + 1) * TT],
                                           S[:, c, t * TT:(t + 1) * TT], ident[0:TT, 0:TT])
                    ins.then_inc(p_turned, 1)

                for c in range(j + 1):
                    scores(0, c)
                if first:
                    tile(*first)
                for q in range(NT):
                    turn(q, 0)
                    if q + 1 < NT:
                        scores(q + 1, 0)
                    for c in range(j + 1):
                        if c < j:
                            turn(q, c + 1)
                            if q + 1 < NT:
                                scores(q + 1, c + 1)
                        pe.wait_ge(pT_kept[c % 2], FIRST + units_of(c % 2, i, j, q) + c // 2 + 1)
                        if c == 0:
                            pe.wait_ge(t1_made, FIRST + g * NT + q)
                        for t in range(NT):
                            ins = pe.matmul(bank[1][0:TT, 0:C], pT[:, c % 2, t], v[:, NT * c + t],
                                            start=(c == 0 and t == 0), stop=(c == j and t == NT - 1))
                        ins.then_inc(pv_made, 1)
                    if q == 1 and second:
                        tile(*second)

            def turn_x(i, c):
                pe.wait_ge(x_in[c % 2], (i * per_parity(c) + c // 2) * 16 + 16)
                pe.wait_ge(f_padded, FIRST + i * NJ + c)
                for t in range(NT):
                    ins = pe.transpose(bank[1][:, t * TT:(t + 1) * TT], xin[:, c % 2, t, :], ident[0:TT, 0:TT])
                ins.then_inc(f_turned, 1)

            def project_x(i, c):
                pe.wait_ge(f_flat, FIRST + i * NJ + c + 1)
                pe.wait_ge(f_proj_kept, FIRST + i * NJ + c)
                for t in range(NT):
                    ins = pe.matmul(bank[3][0:TT, t * C:(t + 1) * C], xflat[:, c % 2, t * TT:(t + 1) * TT],
                                    w_in[:, :], start=True, stop=True)
                ins.then_inc(f_projected, 1)

            def first_image():
                turn_x(0, 0)
                pe.wait_ge(consts_made, 2)
                for c in range(NJ):
                    if c + 1 < NJ:
                        turn_x(0, c + 1)
                    project_x(0, c)

            def experts_front(unit, ahead, third, s, n_att):
                if ahead:
                    p, f = ahead
                    fi, fj = 2 * p + f // NJ, f % NJ
                    banks_left(ahead, s, n_att)
                if unit:
                    i, j = unit
                    g = i * NJ + j
                    pe.wait_ge(t1_made, FIRST + g * NT + NT)
                if ahead:
                    for c in turned_in(fi, fj):
                        pe.wait_ge(f_hidden, FIRST + fi * NJ + fj)
                        turn_x(fi, c)
                    if isinstance(fi, int) and fi == 0:
                        pe.wait_ge(f_padded, FIRST + NJ)
                    elif turned_in(fi, fj):
                        pe.wait_ge(f_padded, FIRST + fi * NJ + min(fj + 2, NJ))
                    if not turned_in(fi, fj):
                        pe.wait_ge(f_hidden, FIRST + fi * NJ + fj)
                    for k in range(P9):
                        dy, dx = k // 3, k % 3
                        ins = pe.matmul(bank[1][:, 0:CH], diag[:, k, :],
                                        xpad[:, ROWS * fj + dy:ROWS * fj + dy + ROWS, dx:dx + IMG],
                                        start=(k == 0), stop=(k == P9 - 1))
                    ins.then_inc(f_convolved, 1)
                if unit:
                    pe.wait_ge(xm_made, FIRST + g + 1)
                    if ahead:
                        pe.wait_ge(f_logits_read, FIRST + fi * NJ + fj)
                    for t in range(NT):
                        ins = pe.transpose(bank[0][:, t * TT:(t + 1) * TT], xn[:, t, :], ident[0:TT, 0:TT])
                    ins.then_inc(xm_turned, 1)
                if ahead:
                    for c in turned_in(fi, fj):
                        project_x(fi, c)
                if unit:
                    pe.wait_ge(xmT_kept, FIRST + g + 1)
                if ahead:
                    pe.wait_ge(f_hidden, FIRST + fi * NJ + fj + 1)
                    for t in range(NT):
                        ins = pe.matmul(bank[0][0:TT, t * C:t * C + 3 * GP], hT[:, fj % 2, t * TT:(t + 1) * TT],
                                        w_om[:, :], start=True, stop=True)
                    ins.then_inc(f_logits, 1)
                if third:
                    tile(*third)
                if not unit:
                    return
                for t in range(NT):
                    ins = pe.matmul(bank[2][0:TT, t * NE:(t + 1) * NE], xnT[:, t * TT:(t + 1) * TT], w_rt[:, :],
                                    start=True, stop=True)
                ins.then_inc(route_made, 1)

                def expert_half(m):
                    pe.matmul(bank[EXPERT_BANKS[m % 3]][0:TT, :], xnT[:, m // 2 * TT:(m // 2 + 1) * TT],
                              w_ex[:, 4 * (m % 2):4 * (m % 2) + 4, :], start=True, stop=True)\
                        .then_inc(experts_made, 1)

                for m in range(3):
                    expert_half(m)
                pe.wait_ge(gate_made, FIRST + g + 1)
                if ahead:
                    pe.wait_ge(f_logits_read, FIRST + fi * NJ + fj + 1)
                for t in range(NT):
                    ins = pe.transpose(bank[0][0:NE, t * TT:(t + 1) * TT], gate[:, t, :], ident[0:TT, 0:TT])
                ins.then_inc(gate_turned, 1)
                for m in range(3, 5):
                    pe.wait_ge(picked_made, FIRST + g * (2 * NT) + m - 2)
                    expert_half(m)
                pe.wait_ge(gT_kept, FIRST + g + 1)
                for t in range(NT):
                    ins = pe.matmul(bank[2][0:TT, t * C:(t + 1) * C], gT[:, t * TT:(t + 1) * TT], b_ex[:, :],
                                    start=True, stop=True)
                ins.then_inc(bias_made, 1)
                for m in range(5, 2 * NT):
                    pe.wait_ge(picked_made, FIRST + g * (2 * NT) + m - 2)
                    expert_half(m)

            timeline(pe, first_image, tile, attention, experts_front, mlp)


_CONV = ["w_in", "b_in", "dw_w", "dw_b", "bn_g", "bn_b", "bn_m", "bn_v", "w_off", "b_off", "w_msk", "b_msk",
         "w_out", "b_out", "ln1_g", "ln1_b", "w_fc1", "b_fc1", "w_fc2", "b_fc2", "ln2_g", "ln2_b", "gamma1", "gamma2"]
_NAMES = {"L0_conv_" + n: n for n in _CONV}
_NAMES.update({"L1_attn_" + n: n for n in ("Wq", "Wk", "Wv")})
_NAMES.update({"L1_ffn_" + n: n for n in ("router_w", "router_b", "expert_w", "expert_b")})


def shape_constants(n_images):
    import numpy as np
    p = np.arange(TT)
    e = np.arange(GP)
    grid = np.zeros((TT, 2, NT, GP), np.float32)
    grid[:, 0] = (p % IMG)[:, None, None] + (e % P9 // 3)[None, None, :]
    grid[:, 1] = (p // IMG)[:, None, None] + 2 * np.arange(NT)[None, :, None] + (e % P9 % 3)[None, None, :]
    gidx = np.tile((e // P9).astype(np.float32), (TT, NT))
    ioff = np.tile((np.arange(n_images) % TABLES * POS * POS * G).astype(np.float32), (TT, 1))
    causal = np.where(np.arange(3 * TT + CH)[None, :] <= p[:, None] + 3 * TT, 0.0, NEG).astype(np.float32)
    lower = np.tile(np.tril(np.ones((NE, NE), np.float32), -1).reshape(1, -1), (TT, 1))
    return {"ident": np.eye(128, dtype=np.float32), "grid": grid.reshape(TT, -1), "gidx": gidx, "ioff": ioff,
            "causal": causal, "lower": lower}


def kernel(**inputs):
    import numpy as np
    import concourse.bacc as bacc
    from concourse.bass_utils import run_bass_kernel_spmd

    nc = bacc.Bacc("TRN2", target_bir_lowering=False, num_devices=1)
    arrays = {"x": np.ascontiguousarray(inputs["x"])}
    for long, short in _NAMES.items():
        arrays[short] = np.ascontiguousarray(inputs[long])
    consts = shape_constants(arrays["x"].shape[0])
    given = {**arrays, **{"const_" + k: a for k, a in consts.items()}}
    aps = {k: nc.dram_tensor("in_" + k, a.shape, mybir.dt.from_np(a.dtype), kind="ExternalInput").ap()
           for k, a in given.items()}
    out = nc.dram_tensor("out_0", arrays["x"].shape, F32, kind="ExternalOutput").ap()
    build(nc, aps["x"], aps, {k: aps["const_" + k] for k in consts}, out)
    r = run_bass_kernel_spmd(nc, [{"in_" + k: a for k, a in given.items()}], core_ids=[0])
    return r.results[0]["out_0"]
```
